# Optimizing a Trainium2 kernel written in Bass

```python
import numpy as np
import jax
import jax.numpy as jnp

def _softmax(x, axis=-1):
    return jax.nn.softmax(x, axis=axis)

def _gelu(x):
    return jax.nn.gelu(x, approximate=True)

def _silu(x):
    return jax.nn.silu(x)

def _sigmoid(x):
    return jax.nn.sigmoid(x)

def _layernorm(x, axis=-1, eps=1e-05):
    m = jnp.mean(x, axis=axis, keepdims=True)
    v = jnp.var(x, axis=axis, keepdims=True)
    return (x - m) / jnp.sqrt(v + eps)

def _scatter_add(tgt, idx, src, axis=0):
    return tgt.at[idx].add(src)

def _segment_sum(src, seg, n):
    return jax.ops.segment_sum(src, seg, n)
kernel_name = 'mk_gnn_ffn_d4_gnn_r32_54ac1d'

def setup_inputs(seed: int=0):
    np.random.seed(seed)
    _w = jnp.asarray

    def _rec_inputs():
        import jax
        import jax.numpy as jnp
        _gk = jax.random.key(seed)
        x = -0.0002117 + 1 * jax.random.normal(jax.random.fold_in(_gk, 1), (3125, 256), jnp.float32)
        src = jax.random.randint(jax.random.fold_in(_gk, 2), (50000,), 0, 3125, jnp.int32)
        dst = jnp.minimum((3125 * jax.random.uniform(jax.random.fold_in(_gk, 3), (50000,)) ** 2.0).astype(jnp.int32), 99999)
        _o = jnp.argsort(dst, stable=True)
        src = src[_o]
        dst = dst[_o]
        edge_weight = jax.random.uniform(jax.random.fold_in(_gk, 13), (50000,), jnp.float32, 0.0, 1)
        return (x, src, dst, edge_weight)
    x, src, dst, edge_weight = _rec_inputs()

    def _L0_gnn_setup():
        import jax, jax.numpy as jnp
        import numpy as np
        N_NODES = 3125
        N_EDGES = 100000
        D = 256

        def _spmm(edge_src, edge_dst, edge_val, dense):
            msgs = dense[edge_src] * edge_val[:, None]
            return jax.ops.segment_sum(msgs, edge_dst, num_segments=N_NODES)

        def _gc_layer(x, edge_src, edge_dst, edge_val, W, b):
            support = x @ W
            out = _spmm(edge_src, edge_dst, edge_val, support)
            return jax.nn.elu(out + b)
        key = jax.random.key(seed)
        k = jax.random.split(key, 8)
        stdv = 1.0 / np.sqrt(D)
        return {'x': jax.random.normal(k[0], (N_NODES, D), dtype=jnp.float32), 'edge_src': jax.random.randint(k[1], (N_EDGES,), 0, N_NODES), 'edge_dst': jax.random.randint(k[2], (N_EDGES,), 0, N_NODES), 'edge_val': jax.random.uniform(k[3], (N_EDGES,), dtype=jnp.float32), 'W1': jax.random.uniform(k[4], (D, D), minval=-stdv, maxval=stdv, dtype=jnp.float32), 'b1': jax.random.uniform(k[5], (D,), minval=-stdv, maxval=stdv, dtype=jnp.float32), 'W2': jax.random.uniform(k[6], (D, D), minval=-stdv, maxval=stdv, dtype=jnp.float32), 'b2': jax.random.uniform(k[7], (D,), minval=-stdv, maxval=stdv, dtype=jnp.float32)}
    _L0_gnn_all = _L0_gnn_setup()
    _L0_gnn_in = {k: v for k, v in _L0_gnn_all.items() if k in ('W1', 'b1', 'W2', 'b2')}
    del _L0_gnn_all

    def _L0_ffn_setup():
        import jax, jax.numpy as jnp
        import numpy as np
        NUM_EXPERTS = 8
        TOP_K = 2
        B, S, D = (8, 256, 256)

        def _moe(tokens, router_w, w1, b1, w2, b2):
            N = tokens.shape[0]
            E = router_w.shape[0]
            logits = tokens.astype(jnp.float32) @ router_w.astype(jnp.float32).T
            probs = jax.nn.softmax(logits, axis=-1)
            rw, re = jax.lax.top_k(probs, TOP_K)
            if TOP_K > 1:
                rw = rw / jnp.maximum(rw.sum(-1, keepdims=True), 1e-12)
            rw = rw.astype(tokens.dtype)
            combine = jnp.zeros((N, E), tokens.dtype).at[jnp.arange(N)[:, None], re].set(rw)
            out = tokens
            for e in range(E):
                h = jax.nn.gelu(tokens @ w1[e] + b1[e], approximate=False)
                y = h @ w2[e] + b2[e]
                out = out + combine[:, e:e + 1] * y
            return out
        key = jax.random.key(seed)
        ks = jax.random.split(key, 4)
        scale = 1.0 / np.sqrt(D).astype(np.float32)
        return {'input_embeddings': jax.random.normal(ks[0], (B, S, D), jnp.float32), 'router_w': jax.random.normal(ks[1], (NUM_EXPERTS, D), jnp.float32) * scale, 'w1': jax.random.normal(ks[2], (NUM_EXPERTS, D, D), jnp.float32) * scale, 'b1': jnp.zeros((NUM_EXPERTS, D), jnp.float32), 'w2': jax.random.normal(ks[3], (NUM_EXPERTS, D, D), jnp.float32) * scale, 'b2': jnp.zeros((NUM_EXPERTS, D), jnp.float32)}
    _L0_ffn_all = _L0_ffn_setup()
    _L0_ffn_in = {k: v for k, v in _L0_ffn_all.items() if k in ('router_w', 'w1', 'b1', 'w2', 'b2')}
    del _L0_ffn_all

    def _L1_gnn_setup():
        import jax, jax.numpy as jnp
        import numpy as np
        N = 3125
        E = 50000
        D = 256
        EPS = 1e-05

        def _glorot(key, shape):
            lim = np.sqrt(6.0 / (shape[-2] + shape[-1]))
            return jax.random.uniform(key, shape, jnp.float32, -lim, lim)

        def _gru_params(key):
            s = 1.0 / np.sqrt(D)
            k1, k2, k3, k4 = jax.random.split(key, 4)
            return (jax.random.uniform(k1, (3 * D, D), jnp.float32, -s, s), jax.random.uniform(k2, (3 * D, D), jnp.float32, -s, s), jax.random.uniform(k3, (3 * D,), jnp.float32, -s, s), jax.random.uniform(k4, (3 * D,), jnp.float32, -s, s))

        def gru_step(x, h, wih, whh, bih, bhh):
            gi = x @ wih.T + bih
            gh = h @ whh.T + bhh
            ir, iz, inn = jnp.split(gi, 3, -1)
            hr, hz, hn = jnp.split(gh, 3, -1)
            r = jax.nn.sigmoid(ir + hr)
            z = jax.nn.sigmoid(iz + hz)
            n = jnp.tanh(inn + r * hn)
            return (1.0 - z) * n + z * h

        def build_norm(edge_index):
            loop = jnp.arange(N, dtype=edge_index.dtype)
            src = jnp.concatenate([edge_index[0], loop])
            dst = jnp.concatenate([edge_index[1], loop])
            deg = jax.ops.segment_sum(jnp.ones(src.shape[0], jnp.float32), dst, num_segments=N)
            dinv = jnp.where(deg > 0, jax.lax.rsqrt(deg), 0.0)
            return (src, dst, dinv[src] * dinv[dst])

        def gcn_propagate(W, X, src, dst, norm):
            xw = X @ W
            msg = norm[:, None] * xw[src]
            return jax.ops.segment_sum(msg, dst, num_segments=N)

        def layernorm(x, g, b):
            mu = jnp.mean(x, -1, keepdims=True)
            var = jnp.mean((x - mu) ** 2, -1, keepdims=True)
            return (x - mu) * jax.lax.rsqrt(var + EPS) * g + b
        key = jax.random.key(seed)
        ks = jax.random.split(key, 8)
        inp = {}
        inp['X'] = jax.random.normal(ks[0], (N, D), jnp.float32)
        inp['edge_index'] = jax.random.randint(ks[1], (2, E), 0, N, jnp.int32)
        inp['iw0'] = _glorot(ks[2], (D, D))
        inp['wih0'], inp['whh0'], inp['bih0'], inp['bhh0'] = _gru_params(ks[3])
        inp['ln_g0'] = jnp.ones((D,), jnp.float32)
        inp['ln_b0'] = jnp.zeros((D,), jnp.float32)
        inp['iw1'] = _glorot(ks[4], (D, D))
        inp['wih1'], inp['whh1'], inp['bih1'], inp['bhh1'] = _gru_params(ks[5])
        return inp
    _L1_gnn_all = _L1_gnn_setup()
    _L1_gnn_in = {k: v for k, v in _L1_gnn_all.items() if k in ('iw0', 'wih0', 'whh0', 'bih0', 'bhh0', 'ln_g0', 'ln_b0', 'iw1', 'wih1', 'whh1', 'bih1', 'bhh1')}
    del _L1_gnn_all

    def _L1_ffn_setup():
        import jax, jax.numpy as jnp
        import numpy as np
        B, K, D = (512, 16, 256)
        E = 32
        H = int(D * 0.25)
        key = jax.random.key(seed)
        ks = jax.random.split(key, 7)
        d_rs = D ** (-0.5)
        h_rs = H ** (-0.5)
        x = jax.random.normal(ks[0], (B, K, D), dtype=jnp.float32)
        router_w = jax.random.uniform(ks[1], (E, D), jnp.float32, -d_rs, d_rs)
        router_b = jax.random.uniform(ks[2], (E,), jnp.float32, -d_rs, d_rs)
        W1 = jax.random.uniform(ks[3], (E, D, H), jnp.float32, -h_rs, h_rs)
        b1 = jax.random.uniform(ks[4], (E, H), jnp.float32, -h_rs, h_rs)
        W2 = jax.random.uniform(ks[5], (E, H, D), jnp.float32, -d_rs, d_rs)
        b2 = jax.random.uniform(ks[6], (E, D), jnp.float32, -d_rs, d_rs)
        return {'x': x, 'router_w': router_w, 'router_b': router_b, 'W1': W1, 'b1': b1, 'W2': W2, 'b2': b2}
    _L1_ffn_all = _L1_ffn_setup()
    _L1_ffn_in = {k: v for k, v in _L1_ffn_all.items() if k in ('router_w', 'router_b', 'W1', 'b1', 'W2', 'b2')}
    del _L1_ffn_all

    def _L2_gnn_setup():
        import jax, jax.numpy as jnp
        import numpy as np
        N_NODES = 50000
        key = jax.random.key(seed)
        k1, k2, k3 = jax.random.split(key, 3)
        x = jax.random.normal(k1, (N_NODES, 256), dtype=jnp.float32)
        W = jax.random.normal(k2, (256, 256), dtype=jnp.float32) * (1.0 / np.sqrt(256))
        edge_index = jax.random.randint(k3, (2, 50000), 0, N_NODES, dtype=jnp.int64)
        return {'x': x, 'W': W, 'edge_index': edge_index}
    _L2_gnn_all = _L2_gnn_setup()
    _L2_gnn_in = {k: v for k, v in _L2_gnn_all.items() if k in ('W',)}
    del _L2_gnn_all

    def _L2_ffn_setup():
        import math
        import jax, jax.numpy as jnp
        import numpy as np
        CAPACITY_FACTOR = 1.25
        TOP_K = 2
        LN_EPS = 1e-05

        def _layer_norm(x, gamma, beta):
            mu = jnp.mean(x, axis=-1, keepdims=True)
            var = jnp.var(x, axis=-1, keepdims=True)
            return (x - mu) * jax.lax.rsqrt(var + LN_EPS) * gamma + beta
        key = jax.random.key(seed)
        ks = jax.random.split(key, 4)
        B, S, D, F, E = (8, 128, 256, 512, 8)
        x = jax.random.normal(ks[0], (B, S, D), dtype=jnp.float32)
        Wr = jax.random.normal(ks[1], (D, E), dtype=jnp.float32) / np.sqrt(D)
        br = jnp.zeros((E,), jnp.float32)
        W1 = jax.random.normal(ks[2], (E, D, F), dtype=jnp.float32) / np.sqrt(D)
        b1 = jnp.zeros((E, F), jnp.float32)
        W2 = jax.random.normal(ks[3], (E, F, D), dtype=jnp.float32) / np.sqrt(F)
        b2 = jnp.zeros((E, D), jnp.float32)
        gamma = jnp.ones((D,), jnp.float32)
        beta = jnp.zeros((D,), jnp.float32)
        return {'x': x, 'Wr': Wr, 'br': br, 'W1': W1, 'b1': b1, 'W2': W2, 'b2': b2, 'gamma': gamma, 'beta': beta}
    _L2_ffn_all = _L2_ffn_setup()
    _L2_ffn_in = {k: v for k, v in _L2_ffn_all.items() if k in ('Wr', 'br', 'W1', 'b1', 'W2', 'b2', 'gamma', 'beta')}
    del _L2_ffn_all

    def _L3_gnn_setup():
        import jax, jax.numpy as jnp
        import numpy as np
        N = 3125
        E = 100000
        D_IN = 256
        D_OUT = 256
        key = jax.random.key(seed)
        k = jax.random.split(key, 8)
        stdv = 1.0 / np.sqrt(D_OUT)
        x = jax.random.normal(k[0], (N, D_IN), dtype=jnp.float32)
        edge_row = jax.random.randint(k[1], (E,), 0, N, dtype=jnp.int32)
        edge_col = jax.random.randint(k[2], (E,), 0, N, dtype=jnp.int32)
        edge_val = jax.random.uniform(k[3], (E,), dtype=jnp.float32)
        weight_l = jax.random.uniform(k[4], (D_IN, D_OUT), minval=-stdv, maxval=stdv, dtype=jnp.float32)
        bias_l = jax.random.uniform(k[5], (D_OUT,), minval=-stdv, maxval=stdv, dtype=jnp.float32)
        weight_r = jax.random.uniform(k[6], (D_IN, D_OUT), minval=-stdv, maxval=stdv, dtype=jnp.float32)
        bias_r = jax.random.uniform(k[7], (D_OUT,), minval=-stdv, maxval=stdv, dtype=jnp.float32)
        return {'x': x, 'edge_row': edge_row, 'edge_col': edge_col, 'edge_val': edge_val, 'weight_l': weight_l, 'bias_l': bias_l, 'weight_r': weight_r, 'bias_r': bias_r}
    _L3_gnn_all = _L3_gnn_setup()
    _L3_gnn_in = {k: v for k, v in _L3_gnn_all.items() if k in ('weight_l', 'bias_l', 'weight_r', 'bias_r')}
    del _L3_gnn_all

    def _L3_ffn_setup():
        import jax, jax.numpy as jnp
        import numpy as np
        B, S, H, F, E, K = (8, 128, 256, 512, 16, 2)
        EPS = 1e-05
        key = jax.random.key(seed)
        ks = jax.random.split(key, 9)
        sc = 0.02
        return {'x': jax.random.normal(ks[0], (B, S, H), dtype=jnp.float32), 'gate_w': jax.random.normal(ks[1], (H, E), dtype=jnp.float32) * sc, 'gate_b': jnp.zeros((E,), dtype=jnp.float32), 'w1': jax.random.normal(ks[2], (E, H, F), dtype=jnp.float32) * sc, 'b1': jnp.zeros((E, F), dtype=jnp.float32), 'w2': jax.random.normal(ks[3], (E, F, H), dtype=jnp.float32) * sc, 'b2': jnp.zeros((E, H), dtype=jnp.float32), 'gamma': jnp.ones((H,), dtype=jnp.float32), 'beta': jnp.zeros((H,), dtype=jnp.float32)}
    _L3_ffn_all = _L3_ffn_setup()
    _L3_ffn_in = {k: v for k, v in _L3_ffn_all.items() if k in ('gate_w', 'gate_b', 'w1', 'b1', 'w2', 'b2', 'gamma', 'beta')}
    del _L3_ffn_all
    return {'x': x, 'src': src, 'dst': dst, 'edge_weight': edge_weight, 'L0_gnn_W1': _L0_gnn_in['W1'], 'L0_gnn_b1': _L0_gnn_in['b1'], 'L0_gnn_W2': _L0_gnn_in['W2'], 'L0_gnn_b2': _L0_gnn_in['b2'], 'L0_ffn_router_w': _L0_ffn_in['router_w'], 'L0_ffn_w1': _L0_ffn_in['w1'], 'L0_ffn_b1': _L0_ffn_in['b1'], 'L0_ffn_w2': _L0_ffn_in['w2'], 'L0_ffn_b2': _L0_ffn_in['b2'], 'L1_gnn_iw0': _L1_gnn_in['iw0'], 'L1_gnn_wih0': _L1_gnn_in['wih0'], 'L1_gnn_whh0': _L1_gnn_in['whh0'], 'L1_gnn_bih0': _L1_gnn_in['bih0'], 'L1_gnn_bhh0': _L1_gnn_in['bhh0'], 'L1_gnn_ln_g0': _L1_gnn_in['ln_g0'], 'L1_gnn_ln_b0': _L1_gnn_in['ln_b0'], 'L1_gnn_iw1': _L1_gnn_in['iw1'], 'L1_gnn_wih1': _L1_gnn_in['wih1'], 'L1_gnn_whh1': _L1_gnn_in['whh1'], 'L1_gnn_bih1': _L1_gnn_in['bih1'], 'L1_gnn_bhh1': _L1_gnn_in['bhh1'], 'L1_ffn_router_w': _L1_ffn_in['router_w'], 'L1_ffn_router_b': _L1_ffn_in['router_b'], 'L1_ffn_W1': _L1_ffn_in['W1'], 'L1_ffn_b1': _L1_ffn_in['b1'], 'L1_ffn_W2': _L1_ffn_in['W2'], 'L1_ffn_b2': _L1_ffn_in['b2'], 'L2_gnn_W': _L2_gnn_in['W'], 'L2_ffn_Wr': _L2_ffn_in['Wr'], 'L2_ffn_br': _L2_ffn_in['br'], 'L2_ffn_W1': _L2_ffn_in['W1'], 'L2_ffn_b1': _L2_ffn_in['b1'], 'L2_ffn_W2': _L2_ffn_in['W2'], 'L2_ffn_b2': _L2_ffn_in['b2'], 'L2_ffn_gamma': _L2_ffn_in['gamma'], 'L2_ffn_beta': _L2_ffn_in['beta'], 'L3_gnn_weight_l': _L3_gnn_in['weight_l'], 'L3_gnn_bias_l': _L3_gnn_in['bias_l'], 'L3_gnn_weight_r': _L3_gnn_in['weight_r'], 'L3_gnn_bias_r': _L3_gnn_in['bias_r'], 'L3_ffn_gate_w': _L3_ffn_in['gate_w'], 'L3_ffn_gate_b': _L3_ffn_in['gate_b'], 'L3_ffn_w1': _L3_ffn_in['w1'], 'L3_ffn_b1': _L3_ffn_in['b1'], 'L3_ffn_w2': _L3_ffn_in['w2'], 'L3_ffn_b2': _L3_ffn_in['b2'], 'L3_ffn_gamma': _L3_ffn_in['gamma'], 'L3_ffn_beta': _L3_ffn_in['beta']}

def reference(x, src, dst, edge_weight, L0_gnn_W1, L0_gnn_b1, L0_gnn_W2, L0_gnn_b2, L0_ffn_router_w, L0_ffn_w1, L0_ffn_b1, L0_ffn_w2, L0_ffn_b2, L1_gnn_iw0, L1_gnn_wih0, L1_gnn_whh0, L1_gnn_bih0, L1_gnn_bhh0, L1_gnn_ln_g0, L1_gnn_ln_b0, L1_gnn_iw1, L1_gnn_wih1, L1_gnn_whh1, L1_gnn_bih1, L1_gnn_bhh1, L1_ffn_router_w, L1_ffn_router_b, L1_ffn_W1, L1_ffn_b1, L1_ffn_W2, L1_ffn_b2, L2_gnn_W, L2_ffn_Wr, L2_ffn_br, L2_ffn_W1, L2_ffn_b1, L2_ffn_W2, L2_ffn_b2, L2_ffn_gamma, L2_ffn_beta, L3_gnn_weight_l, L3_gnn_bias_l, L3_gnn_weight_r, L3_gnn_bias_r, L3_ffn_gate_w, L3_ffn_gate_b, L3_ffn_w1, L3_ffn_b1, L3_ffn_w2, L3_ffn_b2, L3_ffn_gamma, L3_ffn_beta):
    import jax
    import jax.numpy as jnp

    def _L0_gnn_ref(x, edge_src, edge_dst, edge_val, W1, b1, W2, b2):
        import jax, jax.numpy as jnp
        import numpy as np
        N_NODES = 3125
        N_EDGES = 100000
        D = 256

        def _spmm(edge_src, edge_dst, edge_val, dense):
            msgs = dense[edge_src] * edge_val[:, None]
            return jax.ops.segment_sum(msgs, edge_dst, num_segments=N_NODES)

        def _gc_layer(x, edge_src, edge_dst, edge_val, W, b):
            support = x @ W
            out = _spmm(edge_src, edge_dst, edge_val, support)
            return jax.nn.elu(out + b)
        norm = jnp.linalg.norm(x, axis=1, keepdims=True)
        x = x / jnp.maximum(norm, 1e-12)
        x1 = jax.nn.relu(_gc_layer(x, edge_src, edge_dst, edge_val, W1, b1))
        x2 = _gc_layer(x1, edge_src, edge_dst, edge_val, W2, b2)
        return x2

    def _L0_ffn_ref(input_embeddings, router_w, w1, b1, w2, b2):
        import jax, jax.numpy as jnp
        import numpy as np
        NUM_EXPERTS = 8
        TOP_K = 2
        B, S, D = (8, 256, 256)

        def _moe(tokens, router_w, w1, b1, w2, b2):
            N = tokens.shape[0]
            E = router_w.shape[0]
            logits = tokens.astype(jnp.float32) @ router_w.astype(jnp.float32).T
            probs = jax.nn.softmax(logits, axis=-1)
            rw, re = jax.lax.top_k(probs, TOP_K)
            if TOP_K > 1:
                rw = rw / jnp.maximum(rw.sum(-1, keepdims=True), 1e-12)
            rw = rw.astype(tokens.dtype)
            combine = jnp.zeros((N, E), tokens.dtype).at[jnp.arange(N)[:, None], re].set(rw)
            out = tokens
            for e in range(E):
                h = jax.nn.gelu(tokens @ w1[e] + b1[e], approximate=False)
                y = h @ w2[e] + b2[e]
                out = out + combine[:, e:e + 1] * y
            return out
        b, s, d = input_embeddings.shape
        tokens = input_embeddings.reshape(b * s, d)
        return _moe(tokens, router_w, w1, b1, w2, b2).reshape(b, s, d)

    def _L1_gnn_ref(X, edge_index, iw0, wih0, whh0, bih0, bhh0, ln_g0, ln_b0, iw1, wih1, whh1, bih1, bhh1):
        import jax, jax.numpy as jnp
        import numpy as np
        N = 3125
        E = 50000
        D = 256
        EPS = 1e-05

        def _glorot(key, shape):
            lim = np.sqrt(6.0 / (shape[-2] + shape[-1]))
            return jax.random.uniform(key, shape, jnp.float32, -lim, lim)

        def _gru_params(key):
            s = 1.0 / np.sqrt(D)
            k1, k2, k3, k4 = jax.random.split(key, 4)
            return (jax.random.uniform(k1, (3 * D, D), jnp.float32, -s, s), jax.random.uniform(k2, (3 * D, D), jnp.float32, -s, s), jax.random.uniform(k3, (3 * D,), jnp.float32, -s, s), jax.random.uniform(k4, (3 * D,), jnp.float32, -s, s))

        def gru_step(x, h, wih, whh, bih, bhh):
            gi = x @ wih.T + bih
            gh = h @ whh.T + bhh
            ir, iz, inn = jnp.split(gi, 3, -1)
            hr, hz, hn = jnp.split(gh, 3, -1)
            r = jax.nn.sigmoid(ir + hr)
            z = jax.nn.sigmoid(iz + hz)
            n = jnp.tanh(inn + r * hn)
            return (1.0 - z) * n + z * h

        def build_norm(edge_index):
            loop = jnp.arange(N, dtype=edge_index.dtype)
            src = jnp.concatenate([edge_index[0], loop])
            dst = jnp.concatenate([edge_index[1], loop])
            deg = jax.ops.segment_sum(jnp.ones(src.shape[0], jnp.float32), dst, num_segments=N)
            dinv = jnp.where(deg > 0, jax.lax.rsqrt(deg), 0.0)
            return (src, dst, dinv[src] * dinv[dst])

        def gcn_propagate(W, X, src, dst, norm):
            xw = X @ W
            msg = norm[:, None] * xw[src]
            return jax.ops.segment_sum(msg, dst, num_segments=N)

        def layernorm(x, g, b):
            mu = jnp.mean(x, -1, keepdims=True)
            var = jnp.mean((x - mu) ** 2, -1, keepdims=True)
            return (x - mu) * jax.lax.rsqrt(var + EPS) * g + b
        src, dst, norm = build_norm(edge_index)
        W0 = gru_step(iw0, iw0, wih0, whh0, bih0, bhh0)
        h = gcn_propagate(W0, X, src, dst, norm)
        h = layernorm(h, ln_g0, ln_b0)
        h = jax.nn.relu(h)
        W1 = gru_step(iw1, iw1, wih1, whh1, bih1, bhh1)
        h = gcn_propagate(W1, h, src, dst, norm)
        return h

    def _L1_ffn_ref(x, router_w, router_b, W1, b1, W2, b2):
        import jax, jax.numpy as jnp
        import numpy as np
        B, K, D = (512, 16, 256)
        E = 32
        H = int(D * 0.25)
        xf = x.reshape(-1, D)
        logits = xf @ router_w.T + router_b
        idx = jnp.argmax(logits, axis=-1)
        w1t = jnp.take(W1, idx, axis=0)
        h = jnp.einsum('nd,ndh->nh', xf, w1t) + jnp.take(b1, idx, axis=0)
        h = jax.nn.relu(h)
        w2t = jnp.take(W2, idx, axis=0)
        out = jnp.einsum('nh,nhd->nd', h, w2t) + jnp.take(b2, idx, axis=0)
        out = jax.nn.relu(out)
        return out.reshape(x.shape)

    def _L2_gnn_ref(x, W, edge_index):
        import jax, jax.numpy as jnp
        import numpy as np
        N_NODES = 50000
        N = x.shape[0]
        src, dst = (edge_index[0], edge_index[1])
        h = x @ W
        deg = jax.ops.segment_sum(jnp.ones_like(dst, dtype=h.dtype), dst, num_segments=N)
        deg_inv_sqrt = jnp.where(deg > 0, jax.lax.rsqrt(jnp.maximum(deg, 1)), 0.0)
        norm = deg_inv_sqrt[src] * deg_inv_sqrt[dst]
        msgs = h[src] * norm[:, None]
        out = jax.ops.segment_sum(msgs, dst, num_segments=N)
        return out

    def _L2_ffn_ref(x, Wr, br, W1, b1, W2, b2, gamma, beta):
        import math
        import jax, jax.numpy as jnp
        import numpy as np
        CAPACITY_FACTOR = 1.25
        TOP_K = 2
        LN_EPS = 1e-05

        def _layer_norm(x, gamma, beta):
            mu = jnp.mean(x, axis=-1, keepdims=True)
            var = jnp.var(x, axis=-1, keepdims=True)
            return (x - mu) * jax.lax.rsqrt(var + LN_EPS) * gamma + beta
        B, S, D = x.shape
        E = Wr.shape[1]
        N = B * S
        K = TOP_K
        logits = jnp.mean(x, axis=1) @ Wr + br
        routing_weights = jax.nn.softmax(logits, axis=-1)
        capacity = float(math.ceil(N * CAPACITY_FACTOR / E))
        expected_loads = routing_weights.sum(axis=0) * (N / B)
        scale = jnp.where(expected_loads > capacity, capacity / expected_loads, 1.0)
        routing_weights = jax.nn.softmax(routing_weights * scale, axis=-1)
        rw_tok = jnp.broadcast_to(routing_weights[:, None, :], (B, S, E)).reshape(N, E)
        top_w, top_i = jax.lax.top_k(rw_tok, K)
        top_w = jax.nn.softmax(top_w, axis=-1)
        xf = x.reshape(N, D)
        h = jax.nn.gelu(jnp.einsum('nd,edf->enf', xf, W1) + b1[:, None, :], approximate=False)
        y = jnp.einsum('enf,efd->end', h, W2) + b2[:, None, :]
        w_dense = jnp.zeros((N, E), x.dtype).at[jnp.arange(N)[:, None], top_i].add(top_w)
        out = jnp.einsum('ne,end->nd', w_dense, y).reshape(B, S, D)
        out = _layer_norm(out + x, gamma, beta)
        return out

    def _L3_gnn_ref(x, edge_row, edge_col, edge_val, weight_l, bias_l, weight_r, bias_r):
        import jax, jax.numpy as jnp
        import numpy as np
        N = 3125
        E = 100000
        D_IN = 256
        D_OUT = 256
        h = x @ weight_l
        msgs = edge_val[:, None] * h[edge_col]
        agg = jax.ops.segment_sum(msgs, edge_row, num_segments=N)
        out = agg + bias_l
        out = out + x @ weight_r + bias_r
        return out

    def _L3_ffn_ref(x, gate_w, gate_b, w1, b1, w2, b2, gamma, beta):
        import jax, jax.numpy as jnp
        import numpy as np
        B, S, H, F, E, K = (8, 128, 256, 512, 16, 2)
        EPS = 1e-05
        gate_logits = x @ gate_w + gate_b
        topk_vals, topk_idx = jax.lax.top_k(gate_logits, K)
        topk_w = jax.nn.softmax(topk_vals, axis=-1)
        h = jax.nn.relu(jnp.einsum('bsh,ehf->bsef', x, w1) + b1)
        expert_out = jnp.einsum('bsef,efh->bseh', h, w2) + b2
        sel = jnp.take_along_axis(expert_out, topk_idx[:, :, :, None], axis=2)
        moe = jnp.sum(topk_w[..., None] * sel, axis=2)
        y = x + moe
        mu = jnp.mean(y, axis=-1, keepdims=True)
        var = jnp.var(y, axis=-1, keepdims=True)
        return (y - mu) / jnp.sqrt(var + EPS) * gamma + beta
    edge_index = jnp.stack([src, dst])
    x = x + _L0_gnn_ref(_layernorm(x, axis=-1), src, dst, edge_weight, L0_gnn_W1, L0_gnn_b1, L0_gnn_W2, L0_gnn_b2)
    x = x + _L0_ffn_ref(_layernorm(x, axis=-1)[None], L0_ffn_router_w, L0_ffn_w1, L0_ffn_b1, L0_ffn_w2, L0_ffn_b2)[0]
    x = x + _L1_gnn_ref(_layernorm(x, axis=-1), edge_index, L1_gnn_iw0, L1_gnn_wih0, L1_gnn_whh0, L1_gnn_bih0, L1_gnn_bhh0, L1_gnn_ln_g0, L1_gnn_ln_b0, L1_gnn_iw1, L1_gnn_wih1, L1_gnn_whh1, L1_gnn_bih1, L1_gnn_bhh1)
    x = x + _L1_ffn_ref(_layernorm(x, axis=-1)[None], L1_ffn_router_w, L1_ffn_router_b, L1_ffn_W1, L1_ffn_b1, L1_ffn_W2, L1_ffn_b2)[0]
    x = x + _L2_gnn_ref(_layernorm(x, axis=-1), L2_gnn_W, edge_index)
    x = x + _L2_ffn_ref(_layernorm(x, axis=-1)[None], L2_ffn_Wr, L2_ffn_br, L2_ffn_W1, L2_ffn_b1, L2_ffn_W2, L2_ffn_b2, L2_ffn_gamma, L2_ffn_beta)[0]
    x = x + _L3_gnn_ref(_layernorm(x, axis=-1), src, dst, edge_weight, L3_gnn_weight_l, L3_gnn_bias_l, L3_gnn_weight_r, L3_gnn_bias_r)
    x = x + _L3_ffn_ref(_layernorm(x, axis=-1)[None], L3_ffn_gate_w, L3_ffn_gate_b, L3_ffn_w1, L3_ffn_b1, L3_ffn_w2, L3_ffn_b2, L3_ffn_gamma, L3_ffn_beta)[0]
    return x

_drawn_inputs = setup_inputs


def setup_inputs(seed=0):
    import zlib

    import numpy as np

    out = dict(_drawn_inputs(seed))
    spreads = {'L0_ffn_b1': (0.0, 0.508),
     'L0_ffn_b2': (0.0, 0.366),
     'L1_gnn_ln_g0': (1.0, 0.6),
     'L1_gnn_ln_b0': (0.0, 0.503),
     'L2_ffn_br': (0.0, 0.1),
     'L2_ffn_b1': (0.0, 0.8),
     'L2_ffn_b2': (0.0, 0.471),
     'L2_ffn_gamma': (1.0, 0.2),
     'L2_ffn_beta': (0.0, 0.299),
     'L3_ffn_gate_b': (0.0, 0.662),
     'L3_ffn_b1': (0.0, 0.8),
     'L3_ffn_b2': (0.0, 0.716),
     'L3_ffn_gamma': (1.0, 0.2),
     'L3_ffn_beta': (0.0, 0.559)}
    factors = {'L1_gnn_whh0': 3.664,
     'L1_gnn_bih0': 8.0,
     'L1_gnn_bhh0': 8.0,
     'L1_ffn_router_b': 5.711,
     'L1_ffn_b1': 8.0,
     'L1_ffn_b2': 8.0,
     'L3_gnn_bias_l': 8.0,
     'L3_gnn_bias_r': 8.0,
     'L3_ffn_gate_w': 3.648,
     'L3_ffn_w1': 6.167,
     'L3_ffn_w2': 5.003}
    for name, (base, spread) in spreads.items():
        noise = np.random.default_rng([zlib.crc32(name.encode()), seed]).standard_normal(out[name].shape)
        drawn = base * np.exp(spread * noise) if base else spread * noise
        out[name] = jnp.asarray(drawn.astype(out[name].dtype))
    for name, factor in factors.items():
        out[name] = (out[name] * factor).astype(out[name].dtype)
    return out
```

```python
from contextlib import ExitStack

import concourse.bass as bass
from concourse import mybir

F32 = mybir.dt.float32
BF16 = mybir.dt.bfloat16
I32 = mybir.dt.int32
U32 = mybir.dt.uint32
ALU = mybir.AluOpType
ACT = mybir.ActivationFunctionType
AX_X = mybir.AxisListType.X

P = 128
N, D, NE = 3125, 256, 50000
KD = D // P
TILES = -(-N // P)
LAST = N - (TILES - 1) * P
WAYS = 8
BANKS = 4
L = -(-NE // (P * WAYS)) * WAYS
LAST_L = NE - (P - 1) * L
NB = TILES + 1
REAL_CHUNKS = (NE + TILES * (P - 1)) // P
CHUNKS = -(-REAL_CHUNKS // WAYS) * WAYS
SLOTS = REAL_CHUNKS + -(-(P * L - NE) // P)
SLOT_TILES = 66
LN_EPS = 1e-5
NO_NODE = 200.0


def over(eng, n, ways, body):
    for u in range(ways):
        body(u, u, 0, True)
    with eng.Fori(1, n // ways) as i:
        for u in range(ways):
            body(i * ways + u, u, i, False)
    for u in range(n % ways):
        body(n // ways * ways + u, u, n // ways, False)


class Shared:
    pass


class Chain:

    def __init__(self, eng, sem):
        self.eng, self.sem, self.n = eng, sem, 0

    def __call__(self, ins):
        self.n += 1
        ins.then_inc(self.sem, 1)
        self.eng.wait_ge(self.sem, self.n)


def one(ap, i, n=1):
    return ap[:, bass.ds(i, n)]



def constants(nc, k, block):
    sem = k.sem
    filled, cut, row = sem("const_filled"), sem("const_cut"), sem("const_row")

    @block.gpsimd
    def _(pool):
        nc.gpsimd.memset(k.ident[:], 1.0).then_inc(filled, 1)
        nc.gpsimd.memset(k.before[:], 1.0).then_inc(filled, 1)
        nc.gpsimd.memset(k.ones[:], 1.0).then_inc(filled, 1)
        pool.wait_ge(filled, 3)
        nc.gpsimd.affine_select(out=k.ident[:], in_=k.ident[:], compare_op=ALU.is_equal, fill=0.0,
                                base=0, pattern=[[-1, P]], channel_multiplier=1).then_inc(cut, 1)
        nc.gpsimd.affine_select(out=k.before[:], in_=k.before[:], compare_op=ALU.is_gt, fill=0.0,
                                base=0, pattern=[[1, P]], channel_multiplier=-1).then_inc(cut, 1)
        nc.gpsimd.iota(k.count_i[:], pattern=[[1, CHUNKS]], base=0, channel_multiplier=0).then_inc(row, 1)
        pool.wait_ge(cut, 2)

    @block.vector
    def _(dve):
        dve.wait_ge(row, 1)
        nc.vector.tensor_copy(k.count[:], k.count_i[:]).then_inc(row, 1)
        dve.wait_ge(row, 2)



def sort_positions(nc, k, block, name, key_ready, key, items, buckets, real, chunks, ids, finish):
    sem = k.sem
    link_sem, counted, offset = sem(name + "_link"), sem(name + "_counted"), sem(name + "_offset")
    member, running, pos, small, psum = k.member, k.running, k.pos, k.small, k.sort_psum
    m = member[:, 0:buckets * items].rearrange("p (b l) -> p b l", b=buckets)
    s = running[:, 0:buckets * items].rearrange("p (b l) -> p b l", b=buckets)
    prev, cnt, chunk_f, end, off = (small[:, j, 0:buckets] for j in range(5))
    chunk_i = k.small_i[:, 0:buckets]

    @block.vector
    def _(dve):
        link = Chain(dve, link_sem)
        key_ready(dve)
        link(nc.vector.tensor_tensor(m, key.unsqueeze(1).to_broadcast([P, buckets, items]),
                                     k.count[:, 0:buckets].unsqueeze(2).to_broadcast([P, buckets, items]),
                                     ALU.is_equal))
        flat = member[:, 0:buckets * items]
        link(nc.vector.tensor_tensor_scan(running[:, 0:buckets * items], flat, flat, 0.0, ALU.add, ALU.max))
        nc.vector.memset(prev[:, 0:1], 0.0).then_inc(link_sem, 1)
        link.n += 1
        link(nc.vector.tensor_copy(prev[:, 1:buckets], s[:, 0:buckets - 1, items - 1]))
        nc.vector.tensor_tensor(cnt, s[:, :, items - 1], prev, ALU.subtract).then_inc(counted, 1)
        dve.wait_ge(offset, 1)
        link(nc.vector.tensor_scalar(chunk_i, psum[:, 1, 0:buckets], float(P - 1), None, ALU.add))
        link(nc.vector.tensor_scalar(chunk_i, chunk_i, 7, None, ALU.arith_shift_right))
        link(nc.vector.tensor_copy(chunk_f, chunk_i))
        link(nc.vector.tensor_tensor_scan(end, chunk_f, chunk_f, 0.0, ALU.add, ALU.max))
        link(nc.vector.tensor_tensor(off, end, chunk_f, ALU.subtract))
        link(nc.vector.scalar_tensor_tensor(off, off, float(P), psum[:, 0, 0:buckets], ALU.mult, ALU.add))
        link(nc.vector.scalar_tensor_tensor(off, off, -1.0, prev, ALU.add, ALU.subtract))
        link(nc.vector.tensor_tensor(s, s, off.unsqueeze(2).to_broadcast([P, buckets, items]), ALU.add))
        link(nc.vector.tensor_tensor(s, s, m, ALU.mult))
        link(nc.vector.tensor_reduce(pos[:, 0:items], s.rearrange("p b l -> p l b"), AX_X, ALU.add))
        ends = running[0:1, 0:chunks * real].rearrange("p (c b) -> p c b", b=real)
        link(nc.vector.tensor_tensor(ends, k.count[0:1, 0:chunks].unsqueeze(2).to_broadcast([1, chunks, real]),
                                     end[0:1, 0:real].unsqueeze(1).to_broadcast([1, chunks, real]), ALU.is_ge))
        link(nc.vector.tensor_reduce(k.id_f[0:1, 0:chunks], ends, AX_X, ALU.add))
        link(nc.vector.tensor_scalar(ids, k.id_f[0:1, 0:chunks], float(buckets - 1), None, ALU.min))
        finish(link, pos[:, 0:items])

    @block.tensor
    def _(pe):
        pe.wait_ge(counted, 1)
        nc.tensor.matmul(psum[:, 0, 0:buckets], k.before[:], cnt, start=True, stop=True)
        nc.tensor.matmul(psum[:, 1, 0:buckets], k.ones[:], cnt, start=True, stop=True).then_inc(offset, 1)


def sort_edges(nc, k, block, by, other, w, records, table_ids, name, loaded):
    sem = k.sem
    key_link = sem(name + "_key")
    rec = k.staging
    done = sem(name + "_positions")

    def key_ready(dve):
        link = Chain(dve, key_link)
        loaded(dve)
        link(nc.vector.memset(rec[:], 0.0))
        link(nc.vector.tensor_scalar(k.key_i[:], by[:], 7, None, ALU.arith_shift_right))
        link(nc.vector.tensor_copy(k.key[:], k.key_i[:]))
        link(nc.vector.tensor_scalar(k.key_i[:], by[:], P - 1, None, ALU.bitwise_and))
        link(nc.vector.tensor_copy(rec[:, :, 1], k.key_i[:]))
        link(nc.vector.tensor_copy(rec[:, :, 2], w[:]))
        link(nc.vector.tensor_scalar(rec[:, :, 0], other[:], float(N - 1), None, ALU.min))

    def finish(link, pos):
        link(nc.vector.tensor_copy(k.pos_i[:], pos))
        link(nc.vector.tensor_scalar(k.key_i[:], k.pos_i[:], P - 1, None, ALU.bitwise_and))
        link(nc.vector.tensor_scalar(k.pos_i[:], k.pos_i[:], 7, None, ALU.arith_shift_right))
        link(nc.vector.tensor_copy(k.key[:], k.key_i[:]))
        link(nc.vector.tensor_copy(pos, k.pos_i[:]))
        nc.vector.scalar_tensor_tensor(k.pos_i[:], k.key[:], float(SLOTS), pos, ALU.mult, ALU.add)\
            .then_inc(done, 1)

    sort_positions(nc, k, block, name, key_ready, k.key[:], L, NB, TILES, CHUNKS, table_ids[:], finish)

    def rows(c, i, u):
        return rec[:, bass.ds(c, 1), :].rearrange("p a b -> p (a b)")

    scatter(nc, k, block, name, L, lambda c: k.pos_i[:, bass.ds(c, 1)], rows, records,
            lambda act: act.wait_ge(done, 1), lambda pool: pool.wait_ge(k.blank_stored, 32))


def scatter(nc, k, block, name, n, index, rows, table, index_ready, table_ready):
    index_at, staged = k.sem(name + "_index"), k.sem(name + "_staged")
    laid = [k.sem(f"{name}_laid{u}") for u in range(WAYS)]

    @block.scalar
    def _(act):
        index_ready(act)

        def step(c, u, i, first):
            if not first:
                act.wait_ge(laid[u], i * 16)
            nc.scalar.activation(k.index[:, u, :], index(c), ACT.Copy).then_inc(index_at, 1)
        over(act, n, WAYS, step)

    @block.vector
    def _(dve):
        def step(c, u, i, first):
            if not first:
                dve.wait_ge(laid[u], i * 16)
            nc.vector.tensor_scalar(k.rows[:, u, 0:table.shape[1]], rows(c, i, u), 1.0, None, ALU.mult).then_inc(staged, 1)
        over(dve, n, WAYS, step)

    @block.gpsimd
    def _(pool):
        table_ready(pool)

        def step(c, u, i, first):
            pool.wait_ge(index_at, c + 1)
            pool.wait_ge(staged, c + 1)
            pool.nop(nofuse=True)
            nc.gpsimd.indirect_dma_start(table, bass.IndirectOffsetOnAxis(ap=k.index[:, u, :], axis=0),
                                         k.rows[:, u, 0:table.shape[1]], None).then_inc(laid[u], 16)
        over(pool, n, WAYS, step)
        for u in range(WAYS):
            pool.wait_ge(laid[u], 16 * (n // WAYS + (u < n % WAYS)))


def load_edges(nc, k, block, a):
    sem = k.sem
    blank, k.edges_in = sem("edge_blank"), sem("edges_in")
    k.blank_stored = sem("blank_stored")

    @block.vector
    def _(dve):
        nc.vector.memset(k.dst[:], TILES * P).then_inc(blank, 1)
        nc.vector.memset(k.src[:], TILES * P).then_inc(blank, 1)
        nc.vector.memset(k.w[:], 0.0).then_inc(blank, 1)
        nc.vector.memset(k.rec_dst[:], 0.0).then_inc(blank, 1)
        dve.wait_ge(blank, 4)
        nc.vector.memset(k.rec_dst[:, :, 1], NO_NODE).then_inc(blank, 1)

    @block.sync
    def _(sp):
        sp.wait_ge(blank, 3)
        for t, d in ((k.dst, a["dst"]), (k.src, a["src"]), (k.w, a["edge_weight"])):
            sp.dma_start(t[0:P - 1, :], d[0:(P - 1) * L].rearrange("(p l) -> p l", l=L)).then_inc(k.edges_in, 16)
            sp.dma_start(t[P - 1:P, 0:LAST_L], d[(P - 1) * L:NE].rearrange("(p l) -> p l", p=1))\
                .then_inc(k.edges_in, 16)
        sp.wait_ge(blank, 5)
        for r in (k.by_dst, k.by_src):
            sp.dma_start(r.rearrange("(p c) f -> p (c f)", p=P), k.rec_dst[:, :, :].rearrange("p c f -> p (c f)"))\
                .then_inc(k.blank_stored, 16)
        sp.wait_ge(k.blank_stored, 32)


def load_records(nc, k, block, records, rec, name):
    got = k.sem(name + "_records_in")

    @block.sync
    def _(sp):
        sp.dma_start(rec[:, :, :].rearrange("p c f -> p (c f)"), records.rearrange("(p c) f -> p (c f)", p=P))\
            .then_inc(got, 16)
        sp.wait_ge(got, 16)



def spmm(nc, k, block, name, table, rec, ids, weighted, degree):
    sem = k.sem
    gathered = [sem(f"{name}_gathered{u}") for u in range(WAYS)]
    hot_ready, summed, added = sem(name + "_hot"), sem(name + "_summed"), sem(name + "_added")
    width = D + 1 if degree else D

    index_at = sem(name + "_index")

    @block.scalar
    def _(act):
        def step(c, u, i, first):
            if not first:
                act.wait_ge(gathered[u], i * 16)
            nc.scalar.activation(k.index[:, u, :], rec[:, bass.ds(c, 1), 0], ACT.Copy)\
                .then_inc(index_at, 1)
        over(act, CHUNKS, WAYS, step)

    @block.gpsimd
    def _(pool):
        def step(c, u, i, first):
            if not first:
                pool.wait_ge(summed, c - WAYS + 1)
            pool.wait_ge(index_at, c + 1)
            pool.nop(nofuse=True)
            nc.gpsimd.indirect_dma_start(k.rows[:, u, :], None, table,
                                         bass.IndirectOffsetOnAxis(ap=k.index[:, u, :], axis=0))\
                .then_inc(gathered[u], 16)
        over(pool, CHUNKS, WAYS, step)

    @block.vector
    def _(dve):
        def one_hot(c, u, first):
            if not first:
                dve.wait_ge(summed, c - WAYS + 1)
            local = rec[:, bass.ds(c, 1), 1]
            if degree:
                nc.vector.tensor_scalar(k.hot1[:, u, :], k.count[:, 0:P], local, None, ALU.is_equal)
            if weighted:
                hot = nc.vector.tensor_scalar(k.hot[:, u, :], k.count[:, 0:P], local, rec[:, bass.ds(c, 1), 2],
                                              ALU.is_equal, ALU.mult)
            else:
                hot = nc.vector.tensor_scalar(k.hot[:, u, :], k.count[:, 0:P], local, None, ALU.is_equal)
            hot.then_inc(hot_ready, 1)

        def add(c, u, first):
            tile = dve.value_load(ids[0:1, bass.ds(c, 1)], min_val=0, max_val=TILES)
            dve.wait_ge(summed, c + 1)
            if not first:
                dve.wait_ge(added, c)
            into = k.acc[:, bass.ds(tile, 1), 0:width].rearrange("p a f -> p (a f)")
            nc.vector.tensor_tensor(into, into, k.sum_psum[:, u % BANKS, 0:width], ALU.add).then_inc(added, 1)

        def group(c0, first):
            one_hot(c0, 0, first)
            for u in range(WAYS):
                if u + 1 < WAYS:
                    one_hot(c0 + u + 1, u + 1, first)
                add(c0 + u, u, first and u == 0)
        group(0, True)
        with dve.Fori(1, CHUNKS // WAYS) as i:
            group(i * WAYS, False)

    @block.tensor
    def _(pe):
        def step(c, u, i, first):
            pe.wait_ge(gathered[u], (i + 1) * 16)
            pe.wait_ge(hot_ready, c + 1)
            if not first or u >= BANKS:
                pe.wait_ge(added, c - BANKS + 1)
            mm = nc.tensor.matmul(k.sum_psum[:, u % BANKS, 0:D], k.hot[:, u, :], k.rows[:, u, :],
                                  start=True, stop=True)
            if degree:
                mm = nc.tensor.matmul(k.sum_psum[:, u % BANKS, D:D + 1], k.hot1[:, u, :], k.ones[:, 0:1],
                                      start=True, stop=True)
            mm.then_inc(summed, 1)
        over(pe, CHUNKS, WAYS, step)



def ln_stats(nc, k, dve, link, src, done=None, unit=False):
    st, w = k.stats, k.ln_work
    mean, var, t, r, a = (w[:, j, :] for j in range(5))
    with dve.Fori(0, TILES // 5) as i:
        for u in range(5):
            tile = src[:, bass.ds(i * 5 + u, 1), 0:D].rearrange("p a f -> p (a f)")
            nc.vector.bn_stats(st[:, bass.ds(i * 5 + u, 1), :].rearrange("p a f -> p (a f)"), tile)
    nc.vector.memset(a, 0.0).then_inc(link.sem, 1)
    link.n += 1
    dve.wait_ge(link.sem, link.n)
    link(nc.vector.tensor_tensor(mean, st[:, :, 1], st[:, :, 4], ALU.add))
    link(nc.vector.tensor_tensor(a, st[:, :, 1], st[:, :, 4], ALU.subtract))
    link(nc.vector.tensor_tensor(var, st[:, :, 2], st[:, :, 5], ALU.add))
    link(nc.vector.tensor_scalar(mean, mean, 0.5, None, ALU.mult))
    link(nc.vector.tensor_tensor(a, a, a, ALU.mult))
    link(nc.vector.tensor_scalar(a, a, 0.25, None, ALU.mult))
    link(nc.vector.scalar_tensor_tensor(var, var, 1.0 / D, a, ALU.mult, ALU.add))
    link(nc.vector.tensor_scalar(t, var, LN_EPS, None, ALU.add))
    inverse_root(nc, k, dve, link, t, k.ln_scale[:, :])
    if unit:
        link(nc.vector.tensor_scalar(t, var, float(D), None, ALU.mult))
        link(nc.vector.tensor_tensor(t, t, k.ln_scale[:, :], ALU.mult))
        link(nc.vector.tensor_tensor(t, t, k.ln_scale[:, :], ALU.mult))
        link(nc.vector.tensor_scalar(t, t, 1e-24, None, ALU.max))
        inverse_root(nc, k, dve, link, t, r)
        link(nc.vector.tensor_tensor(k.ln_scale[:, :], k.ln_scale[:, :], r, ALU.mult))
    ins = nc.vector.scalar_tensor_tensor(k.ln_shift[:, :], mean, -1.0, k.ln_scale[:, :], ALU.mult, ALU.mult)
    if done is not None:
        ins.then_inc(done, 1)
    else:
        link(ins)


def inverse_root(nc, k, dve, link, t, out):
    a = k.ln_work[:, 5, :]
    link(nc.vector.tensor_copy(k.root_in[:, :], t))
    k.roots += 1
    nc.vector.tensor_copy(a, k.root_in[:, :]).then_inc(k.root_asked, 1)
    dve.wait_ge(k.root_done, k.roots)
    link(nc.vector.reciprocal(out, k.root_out[:, :]))
    link(nc.vector.tensor_tensor(a, out, out, ALU.mult))
    link(nc.vector.tensor_tensor(a, a, k.root_in[:, :], ALU.mult))
    link(nc.vector.tensor_scalar(a, a, -0.5, 1.5, ALU.mult, ALU.add))
    link(nc.vector.tensor_tensor(out, out, a, ALU.mult))


def serve_root(nc, k, act, count=1):
    for _ in range(count):
        k.served += 1
        act.wait_ge(k.root_asked, k.served)
        nc.scalar.activation(k.root_out[:, :], k.root_in[:, :], ACT.Sqrt).then_inc(k.root_done, 1)



def project(nc, k, block, name, weight, table, *, norm_src=None, unit=False, plain_src=None,
            affine=None, row_scale=None, second=None, ready=None, loads=()):
    sem = k.sem
    stat_done, link_sem = sem(name + "_stats"), sem(name + "_link")
    prepared, turned, turned_sb = sem(name + "_prepared"), sem(name + "_turned"), sem(name + "_turned_sb")
    fine = sem(name + "_affine") if affine else prepared
    projected, evacuated = sem(name + "_projected"), sem(name + "_evacuated")
    w_in, stored = sem(name + "_w_in"), sem(name + "_stored")
    src = norm_src if norm_src is not None else plain_src
    n_loads = len(loads)
    x_part = sem(name + "_x_part")

    @block.sync
    def _(sp):
        for held, given in loads:
            sp.dma_start(held, given).then_inc(w_in, 16)

        def step(c, u, i, first):
            sp.wait_ge(evacuated, c + 1)
            sp.dma_start(table[bass.ds(c * P, P), :], k.y[:, bass.ds(c, 1), :].rearrange("p a f -> p (a f)"))\
                .then_inc(stored, 16)
        over(sp, TILES, 2, step)
        sp.wait_ge(stored, 16 * TILES)

    @block.scalar
    def _(act):
        if norm_src is not None:
            serve_root(nc, k, act, 2 if unit else 1)
            act.wait_ge(stat_done, 1)

        def step(c, u, i, first):
            if not first:
                act.wait_ge(turned, c - 1)
            tile = src[:, bass.ds(c, 1), 0:D].rearrange("p a f -> p (a f)")
            if norm_src is not None:
                ins = nc.scalar.activation(k.ybuf[:, u, :], tile, ACT.Identity, bias=one(k.ln_shift, c),
                                           scale=one(k.ln_scale, c))
            else:
                ins = nc.scalar.activation(k.ybuf[:, u, :], tile, ACT.Copy)
            ins.then_inc(prepared, 1)
        over(act, TILES, 2, step)

    @block.tensor
    def _(pe):
        if n_loads:
            pe.wait_ge(w_in, 16 * n_loads)

        def turn(c, u, first):
            pe.wait_ge(fine, 3 * c + 3 if affine else c + 1)
            if not first:
                pe.wait_ge(turned_sb, c - 1)
            for b in range(KD):
                mm = nc.tensor.transpose(k.turn_psum[:, u, b * P:(b + 1) * P], k.ybuf[:, u, b * P:(b + 1) * P],
                                         k.ident[:])
            mm.then_inc(turned, 1)

        def step(c, u, i, first):
            turn(c, u, first)
            pe.wait_ge(turned_sb, c + 1)
            if not first:
                pe.wait_ge(evacuated, c - 1)
            for b in range(KD):
                mm = nc.tensor.matmul(k.out_psum[:, u, 0:D], k.yt[:, u, b * P:(b + 1) * P], weight[:, b, :],
                                      start=(b == 0), stop=(b == KD - 1))
            if second:
                for b in range(KD):
                    mm = nc.tensor.matmul(k.out2_psum[:, u, 0:D], k.yt[:, u, b * P:(b + 1) * P], second[0][:, b, :],
                                          start=(b == 0), stop=(b == KD - 1))
            mm.then_inc(projected, 1)
        over(pe, TILES, 2, step)

    @block.vector
    def _(dve):
        link = Chain(dve, link_sem)
        if ready is not None:
            ready(dve, link)
        if norm_src is not None:
            ln_stats(nc, k, dve, link, norm_src, done=stat_done, unit=unit)
        if affine or second:
            dve.wait_ge(w_in, 16 * n_loads)
        if second:
            link(nc.vector.tensor_tensor(second[1], second[1], second[2], ALU.add))

        def step(c, u, i, first):
            if affine:
                dve.wait_ge(prepared, c + 1)
                y = k.ybuf[:, u, :]
                nc.vector.tensor_tensor(y, y, affine[0], ALU.mult).then_inc(fine, 1)
                dve.wait_ge(fine, 3 * c + 1)
                nc.vector.tensor_tensor(y, y, affine[1], ALU.add).then_inc(fine, 1)
                dve.wait_ge(fine, 3 * c + 2)
                nc.vector.tensor_scalar(y, y, 0.0, None, ALU.max).then_inc(fine, 1)
            dve.wait_ge(turned, c + 1)
            nc.vector.tensor_copy(k.yt[:, u, :], k.turn_psum[:, u, 0:D]).then_inc(turned_sb, 1)
            dve.wait_ge(projected, c + 1)
            if second:
                xt = k.x[:, bass.ds(c, 1), :].rearrange("p a f -> p (a f)")
                nc.vector.tensor_tensor(xt, xt, k.out2_psum[:, u, 0:D], ALU.add).then_inc(x_part, 1)
                dve.wait_ge(x_part, c + 1)
                nc.vector.tensor_tensor(xt, xt, second[1], ALU.add)
            out = k.y[:, bass.ds(c, 1), :].rearrange("p a f -> p (a f)")
            if row_scale is not None:
                nc.vector.tensor_scalar(out, k.out_psum[:, u, 0:D], one(row_scale, c), None, ALU.mult)\
                    .then_inc(evacuated, 1)
            else:
                nc.vector.tensor_scalar(out, k.out_psum[:, u, 0:D], 1.0, None, ALU.mult).then_inc(evacuated, 1)
        over(dve, TILES, 2, step)



def wide(row):
    return row.unsqueeze(1).to_broadcast([P, TILES, D])


def narrow(col):
    return col.unsqueeze(2).to_broadcast([P, TILES, D])


def set_acc(nc, k, from_y):
    done = k.sem("acc_set")
    with nc.Block() as block:
        @block.vector
        def _(dve):
            nc.vector.memset(k.acc[:, TILES, :], 0.0).then_inc(done, 1)
            if from_y:
                nc.vector.tensor_copy(k.acc[:, 0:TILES, 0:D], k.y[:]).then_inc(done, 1)
            else:
                nc.vector.memset(k.acc[:, 0:TILES, :], 0.0).then_inc(done, 1)
            dve.wait_ge(done, 2)


def degrees(nc, k):
    done = k.sem("degree_link")
    with nc.Block() as block:
        @block.vector
        def _(dve):
            link = Chain(dve, done)
            t, has = k.ln_work[:, 0, :], k.ln_work[:, 1, :]
            link(nc.vector.tensor_copy(k.degree[:], k.acc[:, 0:TILES, D]))
            link(nc.vector.tensor_scalar(t, k.degree[:], 1.0, None, ALU.add))
            inverse_root(nc, k, dve, link, t, k.dinv_loop[:])
            link(nc.vector.tensor_scalar(t, k.degree[:], 1.0, None, ALU.max))
            inverse_root(nc, k, dve, link, t, k.dinv[:])
            link(nc.vector.tensor_scalar(has, k.degree[:], 0.0, None, ALU.is_gt))
            link(nc.vector.tensor_tensor(k.dinv[:], k.dinv[:], has, ALU.mult))

        @block.scalar
        def _(act):
            serve_root(nc, k, act, 2)


def relu_bias(nc, k, name, vec):
    got, linked = k.sem(name + "_in"), k.sem(name + "_link")
    with nc.sbuf_tensor(name + "_row", [P, D], F32) as row, nc.Block() as block:
        @block.sync
        def _(sp):
            sp.dma_start(row[:], spread(vec)).then_inc(got, 16)

        @block.vector
        def _(dve):
            link = Chain(dve, linked)
            dve.wait_ge(got, 16)
            link(nc.vector.tensor_tensor(k.y[:], k.acc[:, 0:TILES, 0:D], wide(row[:]), ALU.add))
            link(nc.vector.tensor_scalar(k.y[:], k.y[:], 0.0, None, ALU.max))


def add_elu(nc, k, name, vec):
    got, linked, low, raised = (k.sem(name + s) for s in ("_in", "_link", "_low", "_exp"))
    acc = k.acc[:, 0:TILES, 0:D]
    with nc.sbuf_tensor(name + "_row", [P, D], F32) as row, nc.Block() as block:
        @block.sync
        def _(sp):
            sp.dma_start(row[:], spread(vec)).then_inc(got, 16)

        @block.vector
        def _(dve):
            link = Chain(dve, linked)
            dve.wait_ge(got, 16)
            link(nc.vector.tensor_tensor(acc, acc, wide(row[:]), ALU.add))
            nc.vector.tensor_scalar(k.y[:], acc, 0.0, None, ALU.min).then_inc(low, 1)
            link(nc.vector.scalar_tensor_tensor(k.x[:], acc, 0.0, k.x[:], ALU.max, ALU.add))
            dve.wait_ge(raised, 1)
            link(nc.vector.scalar_tensor_tensor(k.x[:], k.y[:], -1.0, k.x[:], ALU.add, ALU.add))

        @block.scalar
        def _(act):
            act.wait_ge(low, 1)
            nc.scalar.activation(k.y[:], k.y[:], ACT.Exp).then_inc(raised, 1)


def add_acc(nc, k, name, scale, to_x):
    linked = k.sem(name + "_link")
    acc = k.acc[:, 0:TILES, 0:D]
    with nc.Block() as block:
        @block.vector
        def _(dve):
            link = Chain(dve, linked)
            if scale is not None:
                link(nc.vector.tensor_tensor(acc if to_x else k.y[:], acc, narrow(scale[:]), ALU.mult))
            if to_x:
                link(nc.vector.tensor_tensor(k.x[:], k.x[:], acc, ALU.add))


def add_norm(nc, k, name, gamma, beta):
    got, linked = k.sem(name + "_in"), k.sem(name + "_link")
    with nc.sbuf_tensor(name + "_rows", [P, 2, D], F32) as row, nc.Block() as block:
        @block.sync
        def _(sp):
            sp.dma_start(row[:, 0, :], spread(gamma)).then_inc(got, 16)
            sp.dma_start(row[:, 1, :], spread(beta)).then_inc(got, 16)

        @block.scalar
        def _(act):
            serve_root(nc, k, act)

        @block.vector
        def _(dve):
            link = Chain(dve, linked)
            ln_stats(nc, k, dve, link, k.y)
            link(nc.vector.tensor_tensor(k.y[:], k.y[:], narrow(k.ln_scale[:]), ALU.mult))
            link(nc.vector.tensor_tensor(k.y[:], k.y[:], narrow(k.ln_shift[:]), ALU.add))
            dve.wait_ge(got, 32)
            link(nc.vector.tensor_tensor(k.y[:], k.y[:], wide(row[:, 0, :]), ALU.mult))
            link(nc.vector.tensor_tensor(k.x[:], k.x[:], wide(row[:, 1, :]), ALU.add))
            link(nc.vector.tensor_tensor(k.x[:], k.x[:], k.y[:], ALU.add))



def gru(nc, k, name, iw, wih, whh, bih, bhh, weight):
    G = 3 * D
    GB = G // P
    sem = k.sem
    got, turned, copied, linked = (sem(name + s) for s in ("_in", "_turned", "_copied", "_link"))
    mul, act_done = sem(name + "_mul"), sem(name + "_act")
    with ExitStack() as scope:
        def sb(n, shape):
            return scope.enter_context(nc.sbuf_tensor(name + n, shape, F32))
        h = sb("_h", [P, KD, D])
        ws = [sb("_wi", [P, GB, D]), sb("_wh", [P, GB, D])]
        b = sb("_b", [P, 2, G])
        ht = sb("_ht", [P, KD, D])
        wt = [sb("_wit", [P, KD, G]), sb("_wht", [P, KD, G])]
        r, z, n, t = (sb(f"_{x}", [P, KD, D]) for x in "rznt")
        tp = scope.enter_context(nc.psum_tensor(name + "_tp", [P, 2, 512], F32))
        gates = scope.enter_context(nc.psum_tensor(name + "_gates", [P, KD, 2, 512], F32))
        turns = [(h[:, rb, cb * P:(cb + 1) * P], ht[:, cb, rb * P:(rb + 1) * P]) for cb in range(KD) for rb in range(KD)]
        for w, o in zip(ws, wt):
            turns += [(w[:, rb, cb * P:(cb + 1) * P], o[:, cb, rb * P:(rb + 1) * P]) for cb in range(KD) for rb in range(GB)]
        with nc.Block() as block:
            @block.sync
            def _(sp):
                sp.dma_start(h[:], rows_of(iw, KD)).then_inc(got, 16)
                sp.dma_start(ws[0][:], rows_of(wih, GB)).then_inc(got, 16)
                sp.dma_start(ws[1][:], rows_of(whh, GB)).then_inc(got, 16)
                sp.dma_start(b[:, 0, :], spread(bih)).then_inc(got, 16)
                sp.dma_start(b[:, 1, :], spread(bhh)).then_inc(got, 16)

            @block.tensor
            def _(pe):
                pe.wait_ge(got, 80)
                for j, (s, _) in enumerate(turns):
                    if j >= 2:
                        pe.wait_ge(copied, j - 1)
                    nc.tensor.transpose(tp[:, j % 2, 0:P], s, k.ident[:]).then_inc(turned, 1)
                pe.wait_ge(copied, len(turns))
                for rb in range(KD):
                    own = [ht[:, cb, rb * P:(rb + 1) * P] for cb in range(KD)]
                    for j in range(2 * KD):
                        nc.tensor.matmul(gates[:, rb, 0, :], own[j % KD], wt[j // KD][:, j % KD, 0:2 * D],
                                         start=(j == 0), stop=(j == 2 * KD - 1))
                    for part in range(2):
                        for cb in range(KD):
                            mm = nc.tensor.matmul(gates[:, rb, 1, part * D:(part + 1) * D], own[cb],
                                                  wt[part][:, cb, 2 * D:G], start=(cb == 0), stop=(cb == KD - 1))
                mm.then_inc(mul, 1)

            @block.vector
            def _(dve):
                link = Chain(dve, linked)
                for j, (_, o) in enumerate(turns):
                    dve.wait_ge(turned, j + 1)
                    nc.vector.tensor_copy(o, tp[:, j % 2, 0:P]).then_inc(copied, 1)
                link(nc.vector.tensor_tensor(b[:, 0, 0:2 * D], b[:, 0, 0:2 * D], b[:, 1, 0:2 * D], ALU.add))
                dve.wait_ge(mul, 1)
                for rb in range(KD):
                    link(nc.vector.tensor_tensor(r[:, rb, :], gates[:, rb, 0, 0:D], b[:, 0, 0:D], ALU.add))
                    link(nc.vector.tensor_tensor(z[:, rb, :], gates[:, rb, 0, D:2 * D], b[:, 0, D:2 * D], ALU.add))
                    link(nc.vector.tensor_tensor(n[:, rb, :], gates[:, rb, 1, 0:D], b[:, 0, 2 * D:G], ALU.add))
                    link(nc.vector.tensor_tensor(t[:, rb, :], gates[:, rb, 1, D:2 * D], b[:, 1, 2 * D:G], ALU.add))
                nc.vector.tensor_copy(weight, t[:]).then_inc(act_done, 1)
                dve.wait_ge(act_done, 3)
                link(nc.vector.tensor_tensor(t[:], r[:], t[:], ALU.mult))
                link(nc.vector.tensor_tensor(n[:], n[:], t[:], ALU.add))
                nc.vector.tensor_copy(weight, n[:]).then_inc(act_done, 1)
                dve.wait_ge(act_done, 5)
                link(nc.vector.tensor_scalar(t[:], z[:], -1.0, 1.0, ALU.mult, ALU.add))
                link(nc.vector.tensor_tensor(n[:], n[:], t[:], ALU.mult))
                link(nc.vector.tensor_tensor(z[:], z[:], h[:], ALU.mult))
                link(nc.vector.tensor_tensor(weight, n[:], z[:], ALU.add))

            @block.scalar
            def _(act):
                act.wait_ge(act_done, 1)
                nc.scalar.activation(r[:], r[:], ACT.Sigmoid).then_inc(act_done, 1)
                nc.scalar.activation(z[:], z[:], ACT.Sigmoid).then_inc(act_done, 1)
                act.wait_ge(act_done, 4)
                nc.scalar.activation(n[:], n[:], ACT.Tanh).then_inc(act_done, 1)



class Experts:

    def __init__(self, name, experts, top, hidden):
        self.name, self.E, self.K, self.F = name, experts, top, hidden
        self.items = TILES * top
        self.FP = min(P, hidden)
        self.FB = hidden // self.FP
        self.tiles = (TILES * P * top + experts * (P - 1)) // P
        self.tiles += self.tiles % 2


def route(nc, k, m, router, router_by_expert, bias, mode, slots):
    sem, E, K = k.sem, m.E, m.K
    s = {n: sem(f"{m.name}_{n}") for n in ("in", "stats", "link", "prepared", "kept", "turned", "turned_sb",
                                           "scored", "biased", "rt_turned", "rt", "exp_asked", "exp_done",
                                           "keyed", "slots", "index_of")}
    with ExitStack() as scope:
        def sb(n, shape, dt=F32):
            return scope.enter_context(nc.sbuf_tensor(f"{m.name}_{n}", shape, dt))

        def bank(n, shape):
            return scope.enter_context(nc.psum_tensor(f"{m.name}_{n}", shape, F32))
        ybuf, yt = sb("ybuf", [P, 2, D]), sb("yt", [P, 2, D])
        rt = sb("rt", [P, KD, E])
        given = sb("router", [E, D]) if router_by_expert else None
        bias_row = sb("bias", [P, E]) if bias is not None else None
        logits, best, which = sb("logits", [P, TILES, E]), sb("best", [P, TILES, 8]), sb("which", [P, TILES, 8], U32)
        probs, t1, t2 = sb("probs", [P, TILES, E + 8]), sb("t1", [P, TILES]), sb("t2", [P, TILES])
        k.member, k.running = sb("member", [P, E * m.items], BF16), sb("running", [P, max(E * m.items, m.tiles * E)])
        k.pos, k.key = sb("pos", [P, m.items]), sb("key", [P, m.items])
        k.small, k.small_i, k.id_f = sb("small", [P, 5, 32]), sb("small_i", [P, 32], I32), sb("id_f", [1, m.tiles])
        turn_psum, out_psum = bank("turn_psum", [P, 2, 512]), bank("out_psum", [P, 2, 512])
        k.sort_psum, rt_psum = bank("sort_psum", [P, 2, 64]), bank("rt_psum", [P, KD, 64])
        n_in = 1 + (bias is not None)
        choice = k.choice[:, 0:m.items].rearrange("p (t c) -> p t c", c=K)

        def finish(link, pos):
            nc.vector.tensor_copy(k.slot_i[:, 0:m.items], pos).then_inc(s["slots"], 1)

        def key_ready(dve):
            dve.wait_ge(s["keyed"], 1)

        with nc.Block() as block:
            @block.sync
            def _(sp):
                if router_by_expert:
                    sp.dma_start(given[:], router).then_inc(s["in"], 16)
                else:
                    sp.dma_start(rt[:], rows_of(router, KD)).then_inc(s["in"], 16)
                if bias is not None:
                    sp.dma_start(bias_row[:], spread(bias)).then_inc(s["in"], 16)

            @block.scalar
            def _(act):
                serve_root(nc, k, act)
                act.wait_ge(s["stats"], 1)

                def step(c, u, i, first):
                    if not first:
                        act.wait_ge(s["turned"], c - 1)
                        act.wait_ge(s["kept"], c - 1)
                    nc.scalar.activation(ybuf[:, u, :], k.x[:, bass.ds(c, 1), :].rearrange("p a f -> p (a f)"),
                                         ACT.Identity, bias=one(k.ln_shift, c), scale=one(k.ln_scale, c))\
                        .then_inc(s["prepared"], 1)
                over(act, TILES, 2, step)
                if mode != "none":
                    act.wait_ge(s["exp_asked"], 1)
                    used = probs[:, :, 0:E + K if mode == "softmax_all" else K]
                    nc.scalar.activation(used, used, ACT.Exp).then_inc(s["exp_done"], 1)

            @block.gpsimd
            def _(pool):
                def step(c, u, i, first):
                    pool.wait_ge(s["prepared"], c + 1)
                    nc.gpsimd.tensor_copy(k.y[:, bass.ds(c, 1), :].rearrange("p a f -> p (a f)"), ybuf[:, u, :])\
                        .then_inc(s["kept"], 1)
                over(pool, TILES, 2, step)

            @block.tensor
            def _(pe):
                pe.wait_ge(s["in"], 16 * n_in)
                if router_by_expert:
                    for b in range(KD):
                        mm = nc.tensor.transpose(rt_psum[:, b, 0:E], given[:, b * P:(b + 1) * P], k.ident[0:E, 0:E])
                    mm.then_inc(s["rt_turned"], 1)
                    pe.wait_ge(s["rt"], 1)

                def step(c, u, i, first):
                    pe.wait_ge(s["prepared"], c + 1)
                    if not first:
                        pe.wait_ge(s["turned_sb"], c - 1)
                    for b in range(KD):
                        mm = nc.tensor.transpose(turn_psum[:, u, b * P:(b + 1) * P], ybuf[:, u, b * P:(b + 1) * P],
                                                 k.ident[:])
                    mm.then_inc(s["turned"], 1)
                    pe.wait_ge(s["turned_sb"], c + 1)
                    if not first:
                        pe.wait_ge(s["biased"], c - 1)
                    for b in range(KD):
                        mm = nc.tensor.matmul(out_psum[:, u, 0:E], yt[:, u, b * P:(b + 1) * P], rt[:, b, :],
                                              start=(b == 0), stop=(b == KD - 1))
                    mm.then_inc(s["scored"], 1)
                over(pe, TILES, 2, step)

            @block.vector
            def _(dve):
                link = Chain(dve, s["link"])
                if router_by_expert:
                    dve.wait_ge(s["rt_turned"], 1)
                    nc.vector.tensor_copy(rt[:], rt_psum[:, :, 0:E]).then_inc(s["rt"], 1)
                ln_stats(nc, k, dve, link, k.x, done=s["stats"])
                if bias is not None:
                    dve.wait_ge(s["in"], 16 * n_in)

                def step(c, u, i, first):
                    dve.wait_ge(s["turned"], c + 1)
                    nc.vector.tensor_copy(yt[:, u, :], turn_psum[:, u, 0:D]).then_inc(s["turned_sb"], 1)
                    dve.wait_ge(s["scored"], c + 1)
                    lg = logits[:, bass.ds(c, 1), :].rearrange("p a e -> p (a e)")
                    if bias is None:
                        nc.vector.tensor_scalar(lg, out_psum[:, u, 0:E], 0.0, None, ALU.add).then_inc(s["biased"], 1)
                    else:
                        nc.vector.tensor_tensor(lg, out_psum[:, u, 0:E], bias_row[:], ALU.add).then_inc(s["biased"], 1)
                over(dve, TILES, 2, step)
                dve.wait_ge(s["biased"], TILES)
                for c in range(TILES):
                    ins = nc.vector.max(best[:, c, :], logits[:, c, :])
                link(ins)
                for c in range(TILES):
                    ins = nc.vector.max_index(which[:, c, :], best[:, c, :], logits[:, c, :])
                link(ins)
                link(nc.vector.tensor_copy(k.key[:, :].rearrange("p (t c) -> p t c", c=K), which[:, :, 0:K]))
                if mode == "softmax_all":
                    link(nc.vector.tensor_tensor(probs[:, :, 0:E], logits[:], best[:, :, 0:1].to_broadcast([P, TILES, E]),
                                                 ALU.subtract))
                    nc.vector.tensor_tensor(probs[:, :, E:E + K], best[:, :, 0:K],
                                            best[:, :, 0:1].to_broadcast([P, TILES, K]), ALU.subtract)\
                        .then_inc(s["exp_asked"], 1)
                    dve.wait_ge(s["exp_done"], 1)
                    link(nc.vector.tensor_reduce(t1[:], probs[:, :, 0:E], AX_X, ALU.add))
                    link(nc.vector.reciprocal(t1[:], t1[:]))
                    link(nc.vector.tensor_tensor(probs[:, :, E:E + K], probs[:, :, E:E + K],
                                                 t1[:].unsqueeze(2).to_broadcast([P, TILES, K]), ALU.mult))
                    link(nc.vector.tensor_tensor(t1[:], probs[:, :, E], probs[:, :, E + 1], ALU.add))
                    link(nc.vector.tensor_scalar(t1[:], t1[:], 1e-12, None, ALU.max))
                    link(nc.vector.reciprocal(t1[:], t1[:]))
                    link(nc.vector.tensor_tensor(choice, probs[:, :, E:E + K],
                                                 t1[:].unsqueeze(2).to_broadcast([P, TILES, K]), ALU.mult))
                elif mode == "softmax_top":
                    link(nc.vector.tensor_tensor(probs[:, :, 0:K], best[:, :, 0:K],
                                                 best[:, :, 0:1].to_broadcast([P, TILES, K]), ALU.subtract))
                    nc.vector.memset(t2[:], 0.0).then_inc(s["exp_asked"], 1)
                    dve.wait_ge(s["exp_done"], 1)
                    link(nc.vector.tensor_reduce(t1[:], probs[:, :, 0:K], AX_X, ALU.add))
                    link(nc.vector.reciprocal(t1[:], t1[:]))
                    link(nc.vector.tensor_tensor(choice, probs[:, :, 0:K],
                                                 t1[:].unsqueeze(2).to_broadcast([P, TILES, K]), ALU.mult))
                nc.vector.memset(t2[:], 0.0).then_inc(s["keyed"], 1)
            sort_positions(nc, k, block, m.name + "_sort", key_ready, k.key[:], m.items, E, E, m.tiles,
                           k.slot_expert[0:1, 0:m.tiles], finish)
        with nc.Block() as block:
            scatter(nc, k, block, m.name + "_scatter", m.items, lambda c: k.slot_i[:, bass.ds(c, 1)],
                    lambda c, i, u: k.y[:, bass.ds(i * (WAYS // K) + u // K, 1), :].rearrange("p a f -> p (a f)"),
                    slots, lambda act: None, lambda pool: None)


def run_experts(nc, k, m, func, w1, b1, w2, b2, relu_out, slots, results):
    sem, F, FP, FB, E = k.sem, m.F, m.FP, m.FB, m.E
    s = {n: sem(f"{m.name}_x_{n}") for n in ("turned", "turned_sb", "up", "hidden", "down", "out", "b1_in",
                                             "b1_turned", "b1", "sum")}
    loaded = [sem(f"{m.name}_x_loaded{u}") for u in range(2)]
    stored = [sem(f"{m.name}_x_stored{u}") for u in range(2)]
    rows_b1 = E * FB
    with ExitStack() as scope:
        def sb(n, shape, dt=F32):
            return scope.enter_context(nc.sbuf_tensor(f"{m.name}_x_{n}", shape, dt))

        def bank(n, shape):
            return scope.enter_context(nc.psum_tensor(f"{m.name}_x_{n}", shape, F32))
        wa, wb, b2b = sb("wa", [P, 2, KD, F]), sb("wb", [FP, 2, FB, D]), sb("b2b", [P, 2, D])
        xin, xt, h, yo = sb("xin", [P, 2, D]), sb("xt", [P, 2, D]), sb("h", [FP, 2, FB, P]), sb("yo", [P, 2, D])
        b1_given, b1t = sb("b1_given", [rows_b1, FP]), sb("b1t", [FP, rows_b1])
        turn_psum, h_psum, y_psum = bank("tp", [P, 2, 512]), bank("hp", [FP, 2, 512]), bank("yp", [P, 2, 512])
        b1_psum = bank("b1p", [FP, rows_b1])
        with nc.Block() as block:
            @block.sync
            def _(sp):
                sp.dma_start(b1_given[:], b1.rearrange("e (b f) -> (e b) f", f=FP)).then_inc(s["b1_in"], 16)

                def store(c, u):
                    sp.wait_ge(s["out"], c + 1)
                    sp.dma_start(results[bass.ds(c * P, P), :], yo[:, u, :]).then_inc(stored[u], 16)

                def step(c, u, i, first):
                    e = sp.value_load(k.slot_expert[0:1, bass.ds(c, 1)], min_val=0, max_val=E - 1)
                    if not first:
                        sp.wait_ge(s["down"], c - 1)
                        sp.wait_ge(s["out"], c - 1)
                    sp.dma_start(xin[:, u, :], slots[bass.ds(c * P, P), :]).then_inc(loaded[u], 16)
                    sp.dma_start(wa[:, u, :, :], w1[bass.ds(e, 1), :, :].rearrange("e (b p) f -> p (e b) f", p=P))\
                        .then_inc(loaded[u], 16)
                    sp.dma_start(wb[:, u, :, :], w2[bass.ds(e, 1), :, :].rearrange("e (b p) f -> p (e b) f", p=FP))\
                        .then_inc(loaded[u], 16)
                    sp.dma_start(b2b[:, u, :], b2[bass.ds(e, 1), :].rearrange("e f -> (e f)").partition_broadcast(P))\
                        .then_inc(loaded[u], 16)
                    if not first or u:
                        store(c - 1, 1 - u)
                over(sp, m.tiles, 2, step)
                store(m.tiles - 1, 1)
                for u in range(2):
                    sp.wait_ge(stored[u], 16 * (m.tiles // 2))

            @block.tensor
            def _(pe):
                pe.wait_ge(s["b1_in"], 16)
                nc.tensor.transpose(b1_psum[:], b1_given[:], k.ident[0:rows_b1, 0:rows_b1]).then_inc(s["b1_turned"], 1)

                def step(c, u, i, first):
                    pe.wait_ge(loaded[u], (i + 1) * 64)
                    if not first:
                        pe.wait_ge(s["turned_sb"], c - 1)
                    for b in range(KD):
                        mm = nc.tensor.transpose(turn_psum[:, u, b * P:(b + 1) * P], xin[:, u, b * P:(b + 1) * P],
                                                 k.ident[:])
                    mm.then_inc(s["turned"], 1)
                    pe.wait_ge(s["turned_sb"], c + 1)
                    if not first:
                        pe.wait_ge(s["hidden"], c - 1)
                    for f in range(FB):
                        for b in range(KD):
                            mm = nc.tensor.matmul(h_psum[:, u, f * P:(f + 1) * P], wa[:, u, b, f * FP:(f + 1) * FP],
                                                  xt[:, u, b * P:(b + 1) * P], start=(b == 0), stop=(b == KD - 1))
                    mm.then_inc(s["up"], 1)
                    pe.wait_ge(s["hidden"], c + 1)
                    if not first:
                        pe.wait_ge(s["out"], c - 1)
                    for f in range(FB):
                        mm = nc.tensor.matmul(y_psum[:, u, 0:D], h[:, u, f, :], wb[:, u, f, :],
                                              start=(f == 0), stop=(f == FB - 1))
                    mm.then_inc(s["down"], 1)
                over(pe, m.tiles, 2, step)

            @block.scalar
            def _(act):
                act.wait_ge(s["b1"], 1)

                def step(c, u, i, first):
                    e = act.value_load(k.slot_expert[0:1, bass.ds(c, 1)], min_val=0, max_val=E - 1)
                    act.wait_ge(s["up"], c + 1)
                    if not first:
                        act.wait_ge(s["down"], c - 1)
                    for f in range(FB):
                        ins = nc.scalar.activation(h[:, u, f, :], h_psum[:, u, f * P:(f + 1) * P], func,
                                                   bias=b1t[:, bass.ds(e * FB + f, 1)])
                    ins.then_inc(s["hidden"], 1)
                over(act, m.tiles, 2, step)

            @block.vector
            def _(dve):
                dve.wait_ge(s["b1_turned"], 1)
                nc.vector.tensor_copy(b1t[:], b1_psum[:]).then_inc(s["b1"], 1)

                def step(c, u, i, first):
                    dve.wait_ge(s["turned"], c + 1)
                    if not first:
                        dve.wait_ge(s["up"], c - 1)
                    nc.vector.tensor_copy(xt[:, u, :], turn_psum[:, u, 0:D]).then_inc(s["turned_sb"], 1)
                    dve.wait_ge(s["down"], c + 1)
                    if not first:
                        dve.wait_ge(stored[u], i * 16)
                    if relu_out:
                        nc.vector.tensor_tensor(yo[:, u, :], y_psum[:, u, 0:D], b2b[:, u, :], ALU.add)\
                            .then_inc(s["sum"], 1)
                        dve.wait_ge(s["sum"], c + 1)
                        nc.vector.tensor_scalar(yo[:, u, :], yo[:, u, :], 0.0, None, ALU.max).then_inc(s["out"], 1)
                    else:
                        nc.vector.tensor_tensor(yo[:, u, :], y_psum[:, u, 0:D], b2b[:, u, :], ALU.add)\
                            .then_inc(s["out"], 1)
                over(dve, m.tiles, 2, step)


def combine(nc, k, m, results, into, weighted):
    index_at, added = k.sem(m.name + "_c_index"), k.sem(m.name + "_c_added")
    gathered = [k.sem(f"{m.name}_c_gathered{u}") for u in range(WAYS)]
    with nc.Block() as block:
        @block.scalar
        def _(act):
            def step(c, u, i, first):
                if not first:
                    act.wait_ge(gathered[u], i * 16)
                nc.scalar.activation(k.index[:, u, :], k.slot_i[:, bass.ds(c, 1)], ACT.Copy).then_inc(index_at, 1)
            over(act, m.items, WAYS, step)

        @block.gpsimd
        def _(pool):
            def step(c, u, i, first):
                if not first:
                    pool.wait_ge(added, c - WAYS + 1)
                pool.wait_ge(index_at, c + 1)
                pool.nop(nofuse=True)
                nc.gpsimd.indirect_dma_start(k.rows[:, u, :], None, results[0:m.tiles * P, :],
                                             bass.IndirectOffsetOnAxis(ap=k.index[:, u, :], axis=0))\
                    .then_inc(gathered[u], 16)
            over(pool, m.items, WAYS, step)

        @block.vector
        def _(dve):
            def step(c, u, i, first):
                dve.wait_ge(gathered[u], (i + 1) * 16)
                if not first or u:
                    dve.wait_ge(added, c)
                to = into[:, bass.ds(i * (WAYS // m.K) + u // m.K, 1), :].rearrange("p a f -> p (a f)")
                if weighted:
                    nc.vector.scalar_tensor_tensor(to, k.rows[:, u, :], k.choice[:, bass.ds(c, 1)], to,
                                                   ALU.mult, ALU.add).then_inc(added, 1)
                else:
                    nc.vector.tensor_tensor(to, to, k.rows[:, u, :], ALU.add).then_inc(added, 1)
            over(dve, m.items, WAYS, step)


def add_y(nc, k, name):
    done = k.sem(name)
    with nc.Block() as block:
        @block.vector
        def _(dve):
            nc.vector.tensor_tensor(k.x[:], k.x[:], k.y[:], ALU.add).then_inc(done, 1)
            dve.wait_ge(done, 1)



def pooled_ffn(nc, k, router, router_bias, w1, b1, w2, b2):
    E, _, F = w1.shape
    FB, K = F // P, 2
    capacity = float(-(-N * 5 // (4 * E)))
    sem = k.sem
    s = {n: sem("pool_" + n) for n in ("in", "stats", "link", "prepared", "kept", "turned", "turned_sb", "mean",
                                       "scored", "chosen", "exp_asked", "exp_done", "wide", "experts_in", "scaled",
                                       "b1_turned", "up", "hidden", "down", "out", "sum")}
    with ExitStack() as scope:
        def sb(n, shape, dt=F32):
            return scope.enter_context(nc.sbuf_tensor("pool_" + n, shape, dt))

        def bank(n, shape):
            return scope.enter_context(nc.psum_tensor("pool_" + n, shape, F32))
        ybuf, rt, rb = sb("ybuf", [P, 2, D]), sb("rt", [P, KD, E]), sb("rb", [1, E])
        yt = k.acc[:, :, :].rearrange("p t f -> p (t f)")[:, 0:KD * TILES * P].rearrange("p (b n) -> p b n", b=KD)
        mean, lg, t = sb("mean", [P, KD]), sb("lg", [1, 8]), sb("t", [1, 8])
        best, which, cw = sb("best", [1, 8]), sb("which", [1, 8], U32), sb("cw", [1, K])
        cwb = sb("cwb", [P, K])
        wa, wb, b2b = sb("wa", [P, K, KD, F]), sb("wb", [P, K, FB, D]), sb("b2b", [P, K, D])
        b1_given, b1t, b1s = sb("b1_given", [E * FB, P]), sb("b1t", [P, E * FB]), sb("b1s", [P, K, FB])
        h = sb("h", [P, 2, K * FB, P])
        turn_psum = bank("tp", [P, 2, 512])
        small_psum = bank("sp", [P, 512])
        h_psum, y_psum = bank("hp", [P, K, 512]), bank("yp", [P, 2, 512])
        with nc.Block() as block:
            @block.sync
            def _(sp):
                sp.dma_start(rt[:], rows_of(router, KD)).then_inc(s["in"], 16)
                sp.dma_start(rb[:], router_bias.rearrange("(a e) -> a e", a=1)).then_inc(s["in"], 16)
                sp.dma_start(b1_given[:], b1.rearrange("e (b f) -> (e b) f", f=P)).then_inc(s["in"], 16)
                sp.wait_ge(s["chosen"], 1)
                for j in range(K):
                    e = sp.value_load(which[0:1, j:j + 1], min_val=0, max_val=E - 1)
                    sp.dma_start(wa[:, j, :, :], w1[bass.ds(e, 1), :, :].rearrange("e (b p) f -> p (e b) f", p=P))\
                        .then_inc(s["experts_in"], 16)
                    sp.dma_start(wb[:, j, :, :], w2[bass.ds(e, 1), :, :].rearrange("e (b p) f -> p (e b) f", p=P))\
                        .then_inc(s["experts_in"], 16)
                    sp.dma_start(b2b[:, j, :], b2[bass.ds(e, 1), :].rearrange("e f -> (e f)").partition_broadcast(P))\
                        .then_inc(s["experts_in"], 16)

            @block.scalar
            def _(act):
                serve_root(nc, k, act)
                act.wait_ge(s["stats"], 1)

                def step(c, u, i, first):
                    if not first:
                        act.wait_ge(s["turned"], c - 1)
                        act.wait_ge(s["kept"], c - 1)
                    nc.scalar.activation(ybuf[:, u, :], k.x[:, bass.ds(c, 1), :].rearrange("p a f -> p (a f)"),
                                         ACT.Identity, bias=one(k.ln_shift, c), scale=one(k.ln_scale, c))\
                        .then_inc(s["prepared"], 1)
                over(act, TILES, 2, step)
                for n in range(3):
                    act.wait_ge(s["exp_asked"], n + 1)
                    nc.scalar.activation(t[:], t[:], ACT.Exp).then_inc(s["exp_done"], 1)

                def gelu(c, u, i, first):
                    if not first:
                        act.wait_ge(s["down"], c - 1)
                    for j in range(K):
                        act.wait_ge(s["up"], c * K + j + 1)
                        for f in range(FB):
                            ins = nc.scalar.activation(h[:, u, j * FB + f, :], h_psum[:, j, f * P:(f + 1) * P],
                                                       ACT.Gelu, bias=b1s[:, j, f:f + 1])
                        ins.then_inc(s["hidden"], 1)
                act.wait_ge(s["scaled"], 1)
                over(act, TILES, 2, gelu)

            @block.gpsimd
            def _(pool):
                def step(c, u, i, first):
                    pool.wait_ge(s["prepared"], c + 1)
                    nc.gpsimd.tensor_copy(k.y[:, bass.ds(c, 1), :].rearrange("p a f -> p (a f)"), ybuf[:, u, :])\
                        .then_inc(s["kept"], 1)
                over(pool, TILES, 2, step)

            @block.tensor
            def _(pe):
                pe.wait_ge(s["in"], 48)
                nc.tensor.transpose(small_psum[:, 0:E * FB], b1_given[:], k.ident[0:E * FB, 0:E * FB])\
                    .then_inc(s["b1_turned"], 1)

                def step(c, u, i, first):
                    pe.wait_ge(s["prepared"], c + 1)
                    if not first:
                        pe.wait_ge(s["turned_sb"], c - 1)
                    for b in range(KD):
                        mm = nc.tensor.transpose(turn_psum[:, u, b * P:(b + 1) * P], ybuf[:, u, b * P:(b + 1) * P],
                                                 k.ident[:])
                    mm.then_inc(s["turned"], 1)
                over(pe, TILES, 2, step)
                pe.wait_ge(s["mean"], 1)
                for b in range(KD):
                    mm = nc.tensor.matmul(y_psum[0:1, 0, 0:E], mean[:, b:b + 1], rt[:, b, :],
                                          start=(b == 0), stop=(b == KD - 1))
                mm.then_inc(s["scored"], 1)
                pe.wait_ge(s["chosen"], 2)
                nc.tensor.matmul(y_psum[:, 1, 0:K], k.ones[0:1, :], cw[:], start=True, stop=True)\
                    .then_inc(s["wide"], 1)
                pe.wait_ge(s["scaled"], 1)

                def work(c, u, i, first):
                    for j in range(K):
                        if not (first and u == 0):
                            pe.wait_ge(s["hidden"], c * K + j - 1)
                        for f in range(FB):
                            for b in range(KD):
                                mm = nc.tensor.matmul(h_psum[:, j, f * P:(f + 1) * P], wa[:, j, b, f * P:(f + 1) * P],
                                                      yt[:, b, bass.ds(c * P, P)], start=(b == 0), stop=(b == KD - 1))
                        mm.then_inc(s["up"], 1)
                    pe.wait_ge(s["hidden"], c * K + K)
                    if not first:
                        pe.wait_ge(s["out"], c - 1)
                    for j in range(K * FB):
                        mm = nc.tensor.matmul(y_psum[:, u, 0:D], h[:, u, j, :], wb[:, j // FB, j % FB, :],
                                              start=(j == 0), stop=(j == K * FB - 1))
                    mm.then_inc(s["down"], 1)
                over(pe, TILES, 2, work)

            @block.vector
            def _(dve):
                link = Chain(dve, s["link"])
                dve.wait_ge(s["b1_turned"], 1)
                link(nc.vector.tensor_copy(b1t[:], small_psum[:, 0:E * FB]))
                ln_stats(nc, k, dve, link, k.x, done=s["stats"])

                def step(c, u, i, first):
                    dve.wait_ge(s["turned"], c + 1)
                    nc.vector.tensor_scalar(yt[:, :, bass.ds(c * P, P)],
                                            turn_psum[:, u, 0:D].rearrange("p (b n) -> p b n", b=KD), 1.0, None, ALU.mult)\
                        .then_inc(s["turned_sb"], 1)
                over(dve, TILES, 2, step)
                dve.wait_ge(s["turned_sb"], TILES)
                link(nc.vector.tensor_reduce(mean[:], yt[:, :, 0:N], AX_X, ALU.add))
                nc.vector.tensor_scalar(mean[:], mean[:], 1.0 / N, None, ALU.mult).then_inc(s["mean"], 1)
                dve.wait_ge(s["scored"], 1)
                link(nc.vector.tensor_tensor(lg[:], y_psum[0:1, 0, 0:E], rb[:], ALU.add))

                def softmax(n):
                    link(nc.vector.tensor_reduce(best[:, 0:1], lg[:], AX_X, ALU.max))
                    nc.vector.tensor_scalar(t[:], lg[:], best[:, 0:1], None, ALU.subtract).then_inc(s["exp_asked"], 1)
                    dve.wait_ge(s["exp_done"], n)
                    link(nc.vector.tensor_reduce(best[:, 0:1], t[:], AX_X, ALU.add))
                    link(nc.vector.reciprocal(best[:, 0:1], best[:, 0:1]))
                    link(nc.vector.tensor_scalar(lg[:], t[:], best[:, 0:1], None, ALU.mult))
                softmax(1)
                link(nc.vector.tensor_scalar(t[:], lg[:], float(N), None, ALU.mult))
                link(nc.vector.reciprocal(t[:], t[:]))
                link(nc.vector.tensor_scalar(t[:], t[:], capacity, 1.0, ALU.mult, ALU.min))
                link(nc.vector.tensor_tensor(lg[:], lg[:], t[:], ALU.mult))
                softmax(2)
                link(nc.vector.max(best[:], lg[:]))
                nc.vector.max_index(which[:], best[:], lg[:]).then_inc(s["chosen"], 1)
                nc.vector.tensor_scalar(t[:], best[:], best[:, 0:1], None, ALU.subtract).then_inc(s["exp_asked"], 1)
                dve.wait_ge(s["exp_done"], 3)
                link(nc.vector.tensor_reduce(lg[:, 0:1], t[:, 0:K], AX_X, ALU.add))
                link(nc.vector.reciprocal(lg[:, 0:1], lg[:, 0:1]))
                nc.vector.tensor_scalar(cw[:], t[:, 0:K], lg[:, 0:1], None, ALU.mult).then_inc(s["chosen"], 1)
                dve.wait_ge(s["wide"], 1)
                link(nc.vector.tensor_copy(cwb[:], y_psum[:, 1, 0:K]))
                dve.wait_ge(s["experts_in"], 48 * K)
                for j in range(K):
                    link(nc.vector.tensor_scalar(wb[:, j, :, :], wb[:, j, :, :], cwb[:, j:j + 1], None, ALU.mult))
                    link(nc.vector.tensor_scalar(b2b[:, j, :], b2b[:, j, :], cwb[:, j:j + 1], None, ALU.mult))
                    e = dve.value_load(which[0:1, j:j + 1], min_val=0, max_val=E - 1)
                    link(nc.vector.tensor_copy(b1s[:, j, :], b1t[:, bass.ds(e * FB, FB)]))
                nc.vector.tensor_tensor(b2b[:, 0, :], b2b[:, 0, :], b2b[:, 1, :], ALU.add).then_inc(s["scaled"], 1)

                def out(c, u, i, first):
                    dve.wait_ge(s["down"], c + 1)
                    to = k.y[:, bass.ds(c, 1), :].rearrange("p a f -> p (a f)")
                    nc.vector.tensor_tensor(to, to, y_psum[:, u, 0:D], ALU.add).then_inc(s["out"], 1)
                    dve.wait_ge(s["out"], c + 1)
                    nc.vector.tensor_tensor(to, to, b2b[:, 0, :], ALU.add)
                dve.wait_ge(s["kept"], TILES)
                over(dve, TILES, 2, out)



def rows_of(w, blocks):
    return w.rearrange("(b p) n -> p b n", p=P)


def spread(v):
    return v.partition_broadcast(P)


def build(nc, a, out):
    k = Shared()
    k.made = 0

    def numbered(name):
        k.made += 1
        k.used.append(nc.alloc_semaphore(f"{name}_{k.made}"))
        return k.used[-1]
    k.sem, k.used = numbered, []

    def reuse_semaphores():
        nc.clear_and_free_semaphores(k.used)
        nc.all_engine_barrier()
        k.used = []
    ctx = ExitStack()

    def held(scope, name, shape, dt=F32):
        k.made += 1
        t = scope.enter_context(nc.sbuf_tensor(f"{name}_{k.made}", shape, dt))
        return t

    def bank(scope, name, shape):
        k.made += 1
        t = scope.enter_context(nc.psum_tensor(f"{name}_{k.made}", shape, F32))
        return t

    def dram(name, shape, dt=F32):
        return nc.dram_tensor(name, shape, dt).ap()

    k.by_dst = dram("by_dst", (P * SLOTS, 4))
    k.by_src = dram("by_src", (P * SLOTS, 4))
    table = dram("table", (TILES * P, D))

    with ctx:
        k.ident = held(ctx, "ident", [P, P])
        k.before = held(ctx, "before", [P, P])
        k.ones = held(ctx, "ones", [P, P])
        k.count_i = held(ctx, "count_i", [P, CHUNKS], I32)
        k.count = held(ctx, "count", [P, CHUNKS])
        k.x = held(ctx, "x", [P, TILES, D])
        k.y = held(ctx, "y", [P, TILES, D])
        k.rec_dst = held(ctx, "rec_dst", [P, SLOTS, 4])
        k.ids_dst = held(ctx, "ids_dst", [1, CHUNKS], I32)
        k.ids_src = held(ctx, "ids_src", [1, CHUNKS], I32)
        k.index = held(ctx, "index", [P, WAYS, 1], I32)
        k.rows = held(ctx, "rows", [P, WAYS, D])
        k.stats = held(ctx, "stats", [P, TILES, 6])
        k.ln_work = held(ctx, "ln_work", [P, 6, TILES])
        k.ln_scale = held(ctx, "ln_scale", [P, TILES])
        k.ln_shift = held(ctx, "ln_shift", [P, TILES])
        k.root_in = held(ctx, "root_in", [P, TILES])
        k.root_out = held(ctx, "root_out", [P, TILES])
        k.choice = held(ctx, "choice", [P, 2 * TILES])
        k.slot_i = held(ctx, "slot_i", [P, 2 * TILES], I32)
        k.slot_expert = held(ctx, "slot_expert", [1, SLOT_TILES], I32)
        k.gru0 = held(ctx, "gru0", [P, KD, D])
        k.gru1 = held(ctx, "gru1", [P, KD, D])
        k.dinv_loop = held(ctx, "dinv_loop", [P, TILES])
        k.dinv = held(ctx, "dinv", [P, TILES])
        k.degree = held(ctx, "degree", [P, TILES])
        k.root_asked, k.root_done = nc.alloc_semaphore("root_asked"), nc.alloc_semaphore("root_done")
        k.roots = k.served = 0

        def gnn_buffers(scope):
            k.ybuf = held(scope, "ybuf", [P, 2, D])
            k.yt = held(scope, "yt", [P, 2, D])
            k.w_a = held(scope, "w_a", [P, KD, D])
            k.turn_psum = bank(scope, "turn_psum", [P, 2, 512])
            k.out_psum = bank(scope, "out_psum", [P, 2, 512])

        def sum_buffers(scope):
            k.hot = held(scope, "hot", [P, WAYS, P])
            k.hot1 = held(scope, "hot1", [P, WAYS, P])
            k.sum_psum = bank(scope, "sum_psum", [P, BANKS, 512])

        with ExitStack() as scope:
            k.dst = held(scope, "dst", [P, L], I32)
            k.src = held(scope, "src", [P, L], I32)
            k.w = held(scope, "w", [P, L])
            k.key_i = held(scope, "key_i", [P, L], I32)
            k.key = held(scope, "key", [P, L])
            k.pos = held(scope, "pos", [P, L])
            k.pos_i = held(scope, "pos_i", [P, L], I32)
            k.staging = held(scope, "staging", [P, L, 4])
            k.member = held(scope, "member", [P, NB * L], BF16)
            k.running = held(scope, "running", [P, NB * CHUNKS])
            k.small = held(scope, "small", [P, 5, 32])
            k.small_i = held(scope, "small_i", [P, 32], I32)
            k.id_f = held(scope, "id_f", [1, CHUNKS])
            k.sort_psum = bank(scope, "sort_psum", [P, 2, 64])
            x_in = k.sem("x_in")
            with nc.Block() as block:
                constants(nc, k, block)
                load_edges(nc, k, block, a)
            with nc.Block() as block:
                sort_edges(nc, k, block, k.dst, k.src, k.w, k.by_dst, k.ids_dst, "dst",
                           lambda dve: dve.wait_ge(k.edges_in, 96))
            with nc.Block() as block:
                sort_edges(nc, k, block, k.src, k.dst, k.w, k.by_src, k.ids_src, "src",
                           lambda dve: dve.wait_ge(k.edges_in, 96))

        k.acc = held(ctx, "acc", [P, NB, D + 1])

        x_blank = k.sem("x_blank")
        with nc.Block() as block:
            @block.vector
            def _(dve):
                nc.vector.memset(k.x[:, TILES - 1, :], 0.0).then_inc(x_blank, 1)

            @block.sync
            def _(sp):
                sp.dma_start(k.x[:, 0:TILES - 1, :], a["x"][0:(TILES - 1) * P, :].rearrange("(t p) f -> p t f", p=P))\
                    .then_inc(x_in, 16)
                sp.wait_ge(x_blank, 1)
                sp.dma_start(k.x[0:LAST, TILES - 1, :], a["x"][(TILES - 1) * P:N, :]).then_inc(x_in, 16)
                sp.wait_ge(x_in, 32)
        with nc.Block() as block:
            load_records(nc, k, block, k.by_dst, k.rec_dst, "dst")

        slots = dram("slots", (SLOT_TILES * P, D))
        results = dram("results", (SLOT_TILES * P, D))

        def projected(name, weight=None, weight_in=None, **more):
            with ExitStack() as scope:
                gnn_buffers(scope)
                loads = list(more.pop("loads", ()))
                if weight_in is not None:
                    loads.append((k.w_a[:], rows_of(weight_in, KD)))
                    weight = k.w_a
                with nc.Block() as block:
                    project(nc, k, block, name, weight, table, loads=loads, **more)

        def summed(name, ids, weighted, degree):
            with ExitStack() as scope:
                sum_buffers(scope)
                with nc.Block() as block:
                    spmm(nc, k, block, name, table, k.rec_dst, ids, weighted, degree)

        def routed(m, func, router, by_expert, bias, mode, w1, b1, w2, b2, relu_out):
            route(nc, k, m, router, by_expert, bias, mode, slots)
            run_experts(nc, k, m, func, w1, b1, w2, b2, relu_out, slots, results)

        def blank_slots():
            blank = k.sem("slots_blank")
            with nc.Block() as block:
                @block.vector
                def _(dve):
                    nc.vector.memset(k.acc[:], 0.0).then_inc(blank, 1)

                @block.sync
                def _(sp):
                    sp.wait_ge(blank, 1)
                    for t in range(0, SLOT_TILES, TILES):
                        n = min(TILES, SLOT_TILES - t)
                        sp.dma_start(slots[t * P:(t + n) * P, :].rearrange("(t p) f -> p t f", p=P),
                                     k.acc[:, 0:n, 0:D]).then_inc(blank, 16)
                    sp.wait_ge(blank, 1 + 16 * -(-SLOT_TILES // TILES))
        blank_slots()

        projected("l0a", weight_in=a["L0_gnn_W1"], norm_src=k.x, unit=True)
        set_acc(nc, k, False)
        summed("l0a", k.ids_dst, True, True)
        degrees(nc, k)
        relu_bias(nc, k, "l0r", a["L0_gnn_b1"])
        projected("l0b", weight_in=a["L0_gnn_W2"], plain_src=k.y)
        set_acc(nc, k, False)
        summed("l0b", k.ids_dst, True, False)
        add_elu(nc, k, "l0e", a["L0_gnn_b2"])
        reuse_semaphores()
        m = Experts("m0", 8, 2, 256)
        routed(m, ACT.Gelu, a["L0_ffn_router_w"], True, None, "softmax_all",
               a["L0_ffn_w1"], a["L0_ffn_b1"], a["L0_ffn_w2"], a["L0_ffn_b2"], False)
        add_y(nc, k, "m0_add_y")
        combine(nc, k, m, results, k.x, True)
        reuse_semaphores()
        gru(nc, k, "gru0", a["L1_gnn_iw0"], a["L1_gnn_wih0"], a["L1_gnn_whh0"], a["L1_gnn_bih0"], a["L1_gnn_bhh0"], k.gru0[:])
        gru(nc, k, "gru1", a["L1_gnn_iw1"], a["L1_gnn_wih1"], a["L1_gnn_whh1"], a["L1_gnn_bih1"], a["L1_gnn_bhh1"], k.gru1[:])
        projected("l1a", weight=k.gru0, norm_src=k.x, row_scale=k.dinv_loop)
        set_acc(nc, k, True)
        summed("l1a", k.ids_dst, False, False)
        add_acc(nc, k, "l1a", k.dinv_loop, False)
        with nc.sbuf_tensor("l1_affine", [P, 2, D], F32) as affine:
            projected("l1b", weight=k.gru1, norm_src=k.y, affine=(affine[:, 0, :], affine[:, 1, :]),
                      row_scale=k.dinv_loop,
                      loads=[(affine[:, 0, :], spread(a["L1_gnn_ln_g0"])), (affine[:, 1, :], spread(a["L1_gnn_ln_b0"]))])
        set_acc(nc, k, True)
        summed("l1b", k.ids_dst, False, False)
        add_acc(nc, k, "l1b", k.dinv_loop, True)
        reuse_semaphores()
        m = Experts("m1", 32, 1, 64)
        routed(m, ACT.Relu, a["L1_ffn_router_w"], True, a["L1_ffn_router_b"], "none",
               a["L1_ffn_W1"], a["L1_ffn_b1"], a["L1_ffn_W2"], a["L1_ffn_b2"], True)
        combine(nc, k, m, results, k.x, False)
        reuse_semaphores()
        projected("l2", weight_in=a["L2_gnn_W"], norm_src=k.x, row_scale=k.dinv)
        set_acc(nc, k, False)
        summed("l2", k.ids_dst, False, False)
        add_acc(nc, k, "l2", k.dinv, True)
        reuse_semaphores()
        pooled_ffn(nc, k, a["L2_ffn_Wr"], a["L2_ffn_br"], a["L2_ffn_W1"], a["L2_ffn_b1"], a["L2_ffn_W2"], a["L2_ffn_b2"])
        add_norm(nc, k, "l2n", a["L2_ffn_gamma"], a["L2_ffn_beta"])
        reuse_semaphores()
        with nc.Block() as block:
            load_records(nc, k, block, k.by_src, k.rec_dst, "src")
        with nc.sbuf_tensor("l3_wr", [P, KD, D], F32) as wr, nc.sbuf_tensor("l3_b", [P, 2, D], F32) as b, \
                nc.psum_tensor("l3_psum", [P, 2, 512], F32) as k.out2_psum:
            projected("l3", weight_in=a["L3_gnn_weight_l"], norm_src=k.x, second=(wr, b[:, 0, :], b[:, 1, :]),
                      loads=[(wr[:], rows_of(a["L3_gnn_weight_r"], KD)), (b[:, 0, :], spread(a["L3_gnn_bias_l"])),
                             (b[:, 1, :], spread(a["L3_gnn_bias_r"]))])
        set_acc(nc, k, False)
        summed("l3", k.ids_src, True, False)
        add_acc(nc, k, "l3", None, True)
        reuse_semaphores()
        m = Experts("m3", 16, 2, 512)
        routed(m, ACT.Relu, a["L3_ffn_gate_w"], False, a["L3_ffn_gate_b"], "softmax_top",
               a["L3_ffn_w1"], a["L3_ffn_b1"], a["L3_ffn_w2"], a["L3_ffn_b2"], False)
        combine(nc, k, m, results, k.y, True)
        add_norm(nc, k, "l3n", a["L3_ffn_gamma"], a["L3_ffn_beta"])
        last = k.sem("out_stored")
        with nc.Block() as block:
            @block.sync
            def _(sp):
                sp.dma_start(out[0:(TILES - 1) * P, :].rearrange("(t p) f -> p t f", p=P), k.x[:, 0:TILES - 1, :])\
                    .then_inc(last, 16)
                sp.dma_start(out[(TILES - 1) * P:N, :], k.x[0:LAST, TILES - 1, :]).then_inc(last, 16)
                sp.wait_ge(last, 32)


def kernel(**inputs):
    import numpy as _np
    import concourse.bacc as _bacc
    from concourse import mybir as _mybir
    from concourse.bass_utils import run_bass_kernel_spmd as _run

    nc = _bacc.Bacc("TRN2", target_bir_lowering=False, num_devices=1)
    arrays, given = {}, {}
    for name, value in inputs.items():
        v = _np.ascontiguousarray(value)
        arrays[f"in_{name}_dram"] = v
        given[name] = nc.dram_tensor(f"in_{name}_dram", v.shape, _mybir.dt.from_np(v.dtype), kind="ExternalInput").ap()
    out = nc.dram_tensor("out_0_dram", (N, D), F32, kind="ExternalOutput").ap()
    build(nc, given, out)
    r = _run(nc, [arrays], core_ids=[0])
    return r.results[0]["out_0_dram"]
```

```python
from contextlib import ExitStack

import concourse.bass as bass
from concourse import mybir

F32 = mybir.dt.float32
BF16 = mybir.dt.bfloat16
I32 = mybir.dt.int32
U32 = mybir.dt.uint32
ALU = mybir.AluOpType
ACT = mybir.ActivationFunctionType
AX_X = mybir.AxisListType.X

P = 128
N, D, NE = 3125, 256, 50000
KD = D // P
TILES = -(-N // P)
LAST = N - (TILES - 1) * P
GROUP = 8
PARTS = 4
RING = PARTS * GROUP
BANKS = 4
DEEP = 4
L = -(-NE // (P * GROUP)) * GROUP
LAST_L = NE - (P - 1) * L
NB = TILES + 1
REAL_CHUNKS = (NE + TILES * (P - 1)) // P
CHUNKS = -(-REAL_CHUNKS // RING) * RING
SLOTS = REAL_CHUNKS + -(-(P * L - NE) // P)
SLOT_TILES = 66
FIRST_GROUPS = 11
LN_EPS = 1e-5
NO_NODE = 200.0


def over(eng, n, ways, body, last_apart=False, peeled=1):
    rounds = (n - last_apart) // ways
    for c in range(peeled * ways):
        body(c, c % ways, c // ways, c < ways)
    with eng.Fori(peeled, rounds) as i:
        for u in range(ways):
            body(i * ways + u, u, i, False)
    for u in range(n - rounds * ways):
        body(rounds * ways + u, u, rounds, False)


class Shared:
    pass


class Chain:

    def __init__(self, eng, sem):
        self.eng, self.sem, self.n = eng, sem, 0

    def __call__(self, ins):
        self.n += 1
        ins.then_inc(self.sem, 1)
        self.eng.wait_ge(self.sem, self.n)


def one(ap, i, n=1):
    return ap[:, bass.ds(i, n)]



def constants(nc, k, block):
    sem = k.sem
    filled, cut, row = sem("const_filled"), sem("const_cut"), sem("const_row")

    @block.gpsimd
    def _(pool):
        nc.gpsimd.memset(k.ident[:], 1.0).then_inc(filled, 1)
        nc.gpsimd.memset(k.before[:], 1.0).then_inc(filled, 1)
        nc.gpsimd.memset(k.ones[:], 1.0).then_inc(filled, 1)
        nc.gpsimd.memset(k.one_col[:], 1.0).then_inc(filled, 1)
        pool.wait_ge(filled, 4)
        nc.gpsimd.affine_select(out=k.ident[:], in_=k.ident[:], compare_op=ALU.is_equal, fill=0.0,
                                base=0, pattern=[[-1, P]], channel_multiplier=1).then_inc(cut, 1)
        nc.gpsimd.affine_select(out=k.before[:], in_=k.before[:], compare_op=ALU.is_gt, fill=0.0,
                                base=0, pattern=[[1, P]], channel_multiplier=-1).then_inc(cut, 1)
        nc.gpsimd.iota(k.count_i[:], pattern=[[1, CHUNKS]], base=0, channel_multiplier=0).then_inc(row, 1)
        pool.wait_ge(cut, 2)

    @block.vector
    def _(dve):
        dve.wait_ge(row, 1)
        nc.vector.tensor_copy(k.count[:], k.count_i[:]).then_inc(row, 1)
        dve.wait_ge(row, 2)



def sort_positions(nc, k, block, name, key_ready, key, items, buckets, real, chunks, ids, finish):
    sem = k.sem
    link_sem, counted, offset = sem(name + "_link"), sem(name + "_counted"), sem(name + "_offset")
    member, running, pos, small, psum = k.member, k.running, k.pos, k.small, k.sort_psum
    m = member[:, 0:buckets * items].rearrange("p (b l) -> p b l", b=buckets)
    s = running[:, 0:buckets * items].rearrange("p (b l) -> p b l", b=buckets)
    prev, cnt, chunk_f, end, off = (small[:, j, 0:buckets] for j in range(5))
    chunk_i = k.small_i[:, 0:buckets]

    @block.vector
    def _(dve):
        link = Chain(dve, link_sem)
        key_ready(dve)
        link(nc.vector.tensor_tensor(m, key.unsqueeze(1).to_broadcast([P, buckets, items]),
                                     k.count[:, 0:buckets].unsqueeze(2).to_broadcast([P, buckets, items]),
                                     ALU.is_equal))
        flat = member[:, 0:buckets * items]
        link(nc.vector.tensor_tensor_scan(running[:, 0:buckets * items], flat, flat, 0.0, ALU.add, ALU.max))
        nc.vector.memset(prev[:, 0:1], 0.0).then_inc(link_sem, 1)
        link.n += 1
        link(nc.vector.tensor_copy(prev[:, 1:buckets], s[:, 0:buckets - 1, items - 1]))
        nc.vector.tensor_tensor(cnt, s[:, :, items - 1], prev, ALU.subtract).then_inc(counted, 1)
        dve.wait_ge(offset, 1)
        link(nc.vector.tensor_scalar(chunk_i, psum[:, 1, 0:buckets], float(P - 1), None, ALU.add))
        link(nc.vector.tensor_scalar(chunk_i, chunk_i, 7, None, ALU.arith_shift_right))
        link(nc.vector.tensor_copy(chunk_f, chunk_i))
        link(nc.vector.tensor_tensor_scan(end, chunk_f, chunk_f, 0.0, ALU.add, ALU.max))
        link(nc.vector.tensor_tensor(off, end, chunk_f, ALU.subtract))
        link(nc.vector.scalar_tensor_tensor(off, off, float(P), psum[:, 0, 0:buckets], ALU.mult, ALU.add))
        link(nc.vector.scalar_tensor_tensor(off, off, -1.0, prev, ALU.add, ALU.subtract))
        for b in range(buckets):
            ins = nc.vector.scalar_tensor_tensor(s[:, b, :], s[:, b, :], off[:, b:b + 1], m[:, b, :],
                                                 ALU.add, ALU.mult)
        link(ins)
        link(nc.vector.tensor_reduce(pos[:, 0:items], s.rearrange("p b l -> p l b"), AX_X, ALU.add))
        finish(link, pos[:, 0:items])
        ends = running[0:1, 0:chunks * real].rearrange("p (c b) -> p c b", b=real)
        link(nc.vector.tensor_tensor(ends, k.count[0:1, 0:chunks].unsqueeze(2).to_broadcast([1, chunks, real]),
                                     end[0:1, 0:real].unsqueeze(1).to_broadcast([1, chunks, real]), ALU.is_ge))
        link(nc.vector.tensor_reduce(k.id_f[0:1, 0:chunks], ends, AX_X, ALU.add))
        link(nc.vector.tensor_scalar(ids, k.id_f[0:1, 0:chunks], float(buckets - 1), None, ALU.min))

    @block.tensor
    def _(pe):
        pe.wait_ge(counted, 1)
        nc.tensor.matmul(psum[:, 0, 0:buckets], k.before[:], cnt, start=True, stop=True)
        nc.tensor.matmul(psum[:, 1, 0:buckets], k.ones[:], cnt, start=True, stop=True).then_inc(offset, 1)


def sort_edges(nc, k, block, by, other, w, rec, pos_i, table_ids, name, loaded):
    key_link = k.sem(name + "_key")

    def key_ready(dve):
        link = Chain(dve, key_link)
        loaded(dve)
        link(nc.vector.tensor_scalar(k.key_i[:], by[:], 7, None, ALU.arith_shift_right))
        link(nc.vector.tensor_copy(k.key[:], k.key_i[:]))
        link(nc.vector.tensor_scalar(k.key_i[:], by[:], P - 1, None, ALU.bitwise_and))
        link(nc.vector.tensor_copy(rec[:, :, 1], k.key_i[:]))
        link(nc.vector.tensor_copy(rec[:, :, 2], w[:]))
        link(nc.vector.tensor_copy(rec[:, :, 3], w[:]))
        link(nc.vector.tensor_scalar(rec[:, :, 0], other[:], float(N - 1), None, ALU.min))

    def finish(link, pos):
        link(nc.vector.tensor_copy(pos_i[:], pos))
        link(nc.vector.tensor_scalar(k.key_i[:], pos_i[:], P - 1, None, ALU.bitwise_and))
        link(nc.vector.tensor_scalar(pos_i[:], pos_i[:], 7, None, ALU.arith_shift_right))
        link(nc.vector.tensor_copy(k.key[:], k.key_i[:]))
        link(nc.vector.tensor_copy(pos, pos_i[:]))
        link(nc.vector.scalar_tensor_tensor(pos_i[:], k.key[:], float(SLOTS), pos, ALU.mult, ALU.add))

    sort_positions(nc, k, block, name, key_ready, k.key[:], L, NB, TILES, CHUNKS, table_ids[:], finish)


def scatter_edges(nc, k, block, name, pos_i, rec, table, start, groups):
    staged = k.sem(name + "_staged")
    laid = [k.sem(f"{name}_laid{half}") for half in range(2)]

    @block.gpsimd
    def _(pool):
        def turns(i, first, halves=2):
            for half in range(halves):
                at = (start + i * 2 + half) * GROUP
                if not first:
                    pool.wait_ge(laid[half], i * (16 * GROUP))
                    pool.nop(nofuse=True)
                nc.gpsimd.tensor_copy(k.index[:, half, :], pos_i[:, bass.ds(at, GROUP)]).then_inc(staged, 1)
                nc.gpsimd.tensor_copy(k.records[:, half, :, :], rec[:, bass.ds(at, GROUP), :]).then_inc(staged, 1)
                pool.wait_ge(staged, (i * 2 + half + 1) * 2)
                pool.nop(nofuse=True)
                for j in range(GROUP):
                    nc.gpsimd.indirect_dma_start(
                        table, bass.IndirectOffsetOnAxis(ap=k.index[:, half, j:j + 1], axis=0),
                        k.records[:, half, j, :], None).then_inc(laid[half], 16)
        turns(0, True)
        if groups >= 4:
            with pool.Fori(1, groups // 2) as i:
                turns(i, False)
        if groups % 2:
            turns(groups // 2, False, 1)
        for half in range(2):
            pool.wait_ge(laid[half], (groups + 1 - half) // 2 * 16 * GROUP)


def load_edges(nc, k, block, a):
    sem = k.sem
    blank, k.edges_in = sem("edge_blank"), sem("edges_in")
    k.blank_stored = sem("blank_stored")

    @block.vector
    def _(dve):
        nc.vector.memset(k.dst[:], TILES * P).then_inc(blank, 1)
        nc.vector.memset(k.src[:], TILES * P).then_inc(blank, 1)
        nc.vector.memset(k.w[:], 0.0).then_inc(blank, 1)
        nc.vector.memset(k.rec_dst[:], 0.0).then_inc(blank, 1)
        dve.wait_ge(blank, 4)
        nc.vector.memset(k.rec_dst[:, :, 1], NO_NODE).then_inc(blank, 1)

    @block.sync
    def _(sp):
        sp.wait_ge(blank, 3)
        for t, d in ((k.dst, a["dst"]), (k.src, a["src"]), (k.w, a["edge_weight"])):
            sp.dma_start(t[0:P - 1, :], d[0:(P - 1) * L].rearrange("(p l) -> p l", l=L)).then_inc(k.edges_in, 16)
            sp.dma_start(t[P - 1:P, 0:LAST_L], d[(P - 1) * L:NE].rearrange("(p l) -> p l", p=1))\
                .then_inc(k.edges_in, 16)
        sp.wait_ge(blank, 5)
        for r in (k.by_dst, k.by_src):
            sp.dma_start(r.rearrange("(p c) f -> p (c f)", p=P), k.rec_dst[:, :, :].rearrange("p c f -> p (c f)"))\
                .then_inc(k.blank_stored, 16)
        sp.wait_ge(k.blank_stored, 32)


def load_x(nc, k, block, x, slots):
    blank, x_in, slots_blank = k.sem("x_blank"), k.sem("x_in"), k.sem("slots_blank")

    @block.gpsimd
    def _(pool):
        nc.gpsimd.memset(k.x[:, TILES - 1, :], 0.0).then_inc(blank, 1)
        nc.gpsimd.memset(k.acc[:], 0.0).then_inc(blank, 1)

    @block.sync
    def _(sp):
        sp.wait_ge(blank, 1)
        sp.dma_start(k.x[:, 0:TILES - 1, :], x[0:(TILES - 1) * P, :].rearrange("(t p) f -> p t f", p=P))\
            .then_inc(x_in, 16)
        sp.dma_start(k.x[0:LAST, TILES - 1, :], x[(TILES - 1) * P:N, :]).then_inc(x_in, 16)
        sp.wait_ge(blank, 2)
        parts = range(0, SLOT_TILES, TILES)
        for t in parts:
            n = min(TILES, SLOT_TILES - t)
            sp.dma_start(slots[t * P:(t + n) * P, :].rearrange("(t p) f -> p t f", p=P), k.acc[:, 0:n, 0:D])\
                .then_inc(slots_blank, 16)
        sp.wait_ge(x_in, 32)
        sp.wait_ge(slots_blank, 16 * len(parts))


def load_records(nc, k, block, records, rec, name):
    got = k.sem(name + "_records_in")

    @block.sync
    def _(sp):
        sp.dma_start(rec[:, :, :].rearrange("p c f -> p (c f)"), records.rearrange("(p c) f -> p (c f)", p=P))\
            .then_inc(got, 16)
        sp.wait_ge(got, 16)



def spmm(nc, k, block, name, table, rec, ids, weighted, degree):
    sem = k.sem
    gathered = [sem(f"{name}_gathered{u}") for u in range(RING)]
    hot_ready, summed, added = sem(name + "_hot"), sem(name + "_summed"), sem(name + "_added")
    away, hot1_ready = sem(name + "_away"), sem(name + "_hot1")
    index_at = sem(name + "_index")
    width = D + 1 if degree else D

    @block.scalar
    def _(act):
        def indices(i, part, first):
            at = i * RING + part * GROUP
            if not first:
                act.wait_ge(summed, at + GROUP - RING)
            nc.scalar.activation(k.index[:, part, :], rec[:, bass.ds(at, GROUP), 0], ACT.Copy).then_inc(index_at, 1)

        def one_hots(i, part):
            for j in range(GROUP):
                c = i * RING + part * GROUP + j
                if j >= 2:
                    act.wait_ge(hot1_ready, c - 1)
                nc.scalar.activation(k.away[:, j % 2, :], k.count[:, 0:P], ACT.Abs,
                                     bias=rec[:, bass.ds(c, 1), 1], scale=-1.0).then_inc(away, 1)
                act.wait_ge(away, c + 1)
                nc.scalar.activation(k.hot1[:, part * GROUP + j, :], k.away[:, j % 2, :], ACT.Relu,
                                     bias=1.0, scale=-1.0).then_inc(hot1_ready, 1)

        def round_of(i, first):
            for part in range(PARTS):
                indices(i, part, first)
                if degree:
                    one_hots(i, part)
        round_of(0, True)
        with act.Fori(1, CHUNKS // RING) as i:
            round_of(i, False)

    @block.gpsimd
    def _(pool):
        def round_of(i):
            for part in range(PARTS):
                pool.wait_ge(index_at, i * PARTS + part + 1)
                pool.nop(nofuse=True)
                for j in range(GROUP):
                    u = part * GROUP + j
                    nc.gpsimd.indirect_dma_start(
                        k.rows[:, u, :], None, table,
                        bass.IndirectOffsetOnAxis(ap=k.index[:, part, j:j + 1], axis=0)).then_inc(gathered[u], 16)
        round_of(0)
        with pool.Fori(1, CHUNKS // RING) as i:
            round_of(i)

    @block.vector
    def _(dve):
        def one_hot(c, u):
            local = rec[:, bass.ds(c, 1), 1]
            if weighted:
                hot = nc.vector.tensor_scalar(k.hot[:, u, :], k.count[:, 0:P], local, rec[:, bass.ds(c, 1), 2],
                                              ALU.is_equal, ALU.mult)
            else:
                hot = nc.vector.tensor_scalar(k.hot[:, u, :], k.count[:, 0:P], local, None, ALU.is_equal)
            hot.then_inc(hot_ready, 1)

        def add(c, u, tile, first):
            dve.wait_ge(summed, c + 1)
            if not first:
                dve.wait_ge(added, c)
            into = k.acc[:, bass.ds(tile, 1), 0:width].rearrange("p a f -> p (a f)")
            nc.vector.tensor_tensor(into, into, k.sum_psum[:, u % BANKS, 0:width], ALU.add).then_inc(added, 1)

        def part_of(at, part, first=False, last=False):
            tiles = nc.values_load_multi_w_load_instructions(
                ids[0:1, bass.ds(at, GROUP)], engines=[mybir.EngineType.DVE], min_val=0, max_val=TILES)[1]
            for j in range(GROUP):
                u = part * GROUP + j
                if not last:
                    one_hot(at + GROUP + j, (u + GROUP) % RING)
                add(at + j, u, tiles[j], first and j == 0)

        for j in range(GROUP):
            one_hot(j, j)
        part_of(0, 0, first=True)
        with dve.Fori(0, CHUNKS // RING - 1) as i:
            for part in range(1, PARTS + 1):
                part_of(i * RING + part * GROUP, part % PARTS)
        for part in range(1, PARTS):
            part_of(CHUNKS + (part - PARTS) * GROUP, part, last=part == PARTS - 1)

    @block.tensor
    def _(pe):
        def step(c, u, i, first):
            pe.wait_ge(gathered[u], (i + 1) * 16)
            pe.wait_ge(hot_ready, c + 1)
            if not first or u >= BANKS:
                pe.wait_ge(added, c - BANKS + 1)
            mm = nc.tensor.matmul(k.sum_psum[:, u % BANKS, 0:D], k.hot[:, u, :], k.rows[:, u, :],
                                  start=True, stop=True)
            if degree:
                pe.wait_ge(hot1_ready, c + 1)
                mm = nc.tensor.matmul(k.sum_psum[:, u % BANKS, D:D + 1], k.hot1[:, u, :], k.one_col[:],
                                      start=True, stop=True)
            mm.then_inc(summed, 1)
        over(pe, CHUNKS, RING, step)



def ln_stats(nc, k, dve, link, src, done=None, unit=False):
    st, w = k.stats, k.ln_work
    mean, var, t, r, a = (w[:, j, :] for j in range(5))
    with dve.Fori(0, TILES // 5) as i:
        for u in range(5):
            tile = src[:, bass.ds(i * 5 + u, 1), 0:D].rearrange("p a f -> p (a f)")
            nc.vector.bn_stats(st[:, bass.ds(i * 5 + u, 1), :].rearrange("p a f -> p (a f)"), tile)
    nc.vector.memset(a, 0.0).then_inc(link.sem, 1)
    link.n += 1
    dve.wait_ge(link.sem, link.n)
    link(nc.vector.tensor_tensor(mean, st[:, :, 1], st[:, :, 4], ALU.add))
    link(nc.vector.tensor_tensor(a, st[:, :, 1], st[:, :, 4], ALU.subtract))
    link(nc.vector.tensor_tensor(var, st[:, :, 2], st[:, :, 5], ALU.add))
    link(nc.vector.tensor_scalar(mean, mean, 0.5, None, ALU.mult))
    link(nc.vector.tensor_tensor(a, a, a, ALU.mult))
    link(nc.vector.tensor_scalar(a, a, 0.25, None, ALU.mult))
    link(nc.vector.scalar_tensor_tensor(var, var, 1.0 / D, a, ALU.mult, ALU.add))
    link(nc.vector.tensor_scalar(t, var, LN_EPS, None, ALU.add))
    inverse_root(nc, k, dve, link, t, k.ln_scale[:, :])
    if unit:
        link(nc.vector.tensor_scalar(t, var, float(D), None, ALU.mult))
        link(nc.vector.tensor_tensor(t, t, k.ln_scale[:, :], ALU.mult))
        link(nc.vector.tensor_tensor(t, t, k.ln_scale[:, :], ALU.mult))
        link(nc.vector.tensor_scalar(t, t, 1e-24, None, ALU.max))
        inverse_root(nc, k, dve, link, t, r)
        link(nc.vector.tensor_tensor(k.ln_scale[:, :], k.ln_scale[:, :], r, ALU.mult))
    ins = nc.vector.scalar_tensor_tensor(k.ln_shift[:, :], mean, -1.0, k.ln_scale[:, :], ALU.mult, ALU.mult)
    if done is not None:
        ins.then_inc(done, 1)
    else:
        link(ins)


def inverse_root(nc, k, dve, link, t, out):
    a = k.ln_work[:, 5, :]
    link(nc.vector.tensor_copy(k.root_in[:, :], t))
    k.roots += 1
    nc.vector.tensor_copy(a, k.root_in[:, :]).then_inc(k.root_asked, 1)
    dve.wait_ge(k.root_done, k.roots)
    link(nc.vector.reciprocal(out, k.root_out[:, :]))
    link(nc.vector.tensor_tensor(a, out, out, ALU.mult))
    link(nc.vector.tensor_tensor(a, a, k.root_in[:, :], ALU.mult))
    link(nc.vector.tensor_scalar(a, a, -0.5, 1.5, ALU.mult, ALU.add))
    link(nc.vector.tensor_tensor(out, out, a, ALU.mult))


def serve_root(nc, k, act, count=1):
    for _ in range(count):
        k.served += 1
        act.wait_ge(k.root_asked, k.served)
        nc.scalar.activation(k.root_out[:, :], k.root_in[:, :], ACT.Sqrt).then_inc(k.root_done, 1)



def project(nc, k, block, name, weight, table, *, norm_src=None, unit=False, plain_src=None,
            affine=None, row_scale=None, second=None, self_loop=False, loads=()):
    sem = k.sem
    stat_done, link_sem = sem(name + "_stats"), sem(name + "_link")
    prepared, turned, turned_sb = sem(name + "_prepared"), sem(name + "_turned"), sem(name + "_turned_sb")
    fine = sem(name + "_affine") if affine else prepared
    projected, evacuated = sem(name + "_projected"), sem(name + "_evacuated")
    w_in, stored = sem(name + "_w_in"), sem(name + "_stored")
    src = norm_src if norm_src is not None else plain_src
    n_loads = len(loads)
    x_part = sem(name + "_x_part")

    @block.sync
    def _(sp):
        for held, given in loads:
            sp.dma_start(held, given).then_inc(w_in, 16)

    @block.scalar
    def _(act):
        if norm_src is not None:
            serve_root(nc, k, act, 2 if unit else 1)
            act.wait_ge(stat_done, 1)

        def step(c, u, i, first):
            if not first:
                act.wait_ge(turned, c - 1)
            tile = src[:, bass.ds(c, 1), 0:D].rearrange("p a f -> p (a f)")
            if norm_src is not None:
                ins = nc.scalar.activation(k.ybuf[:, u, :], tile, ACT.Identity, bias=one(k.ln_shift, c),
                                           scale=one(k.ln_scale, c))
            else:
                ins = nc.scalar.activation(k.ybuf[:, u, :], tile, ACT.Copy)
            ins.then_inc(prepared, 1)
        over(act, TILES, 2, step)

        def store(c, u, i, first):
            act.wait_ge(evacuated, c + 1)
            act.dma_start(table[bass.ds(c * P, P), :], k.y[:, bass.ds(c, 1), :].rearrange("p a f -> p (a f)"))\
                .then_inc(stored, 16)
        over(act, TILES, 2, store)
        act.wait_ge(stored, 16 * TILES)

    @block.tensor
    def _(pe):
        if n_loads:
            pe.wait_ge(w_in, 16 * n_loads)

        def turn(c, u, first):
            pe.wait_ge(fine, 3 * c + 3 if affine else c + 1)
            if not first:
                pe.wait_ge(turned_sb, c - 1)
            for b in range(KD):
                mm = nc.tensor.transpose(k.turn_psum[:, u, b * P:(b + 1) * P], k.ybuf[:, u, b * P:(b + 1) * P],
                                         k.ident[:])
            mm.then_inc(turned, 1)

        def step(c, u, i, first):
            if not (isinstance(c, int) and c == TILES - 1):
                turn(c + 1, 1 - u, first and u == 0)
            pe.wait_ge(turned_sb, c + 1)
            if not first:
                pe.wait_ge(evacuated, c - 1)
            for b in range(KD):
                mm = nc.tensor.matmul(k.out_psum[:, u, 0:D], k.yt[:, u, b * P:(b + 1) * P], weight[:, b, :],
                                      start=(b == 0), stop=(b == KD - 1))
            if second:
                for b in range(KD):
                    mm = nc.tensor.matmul(k.out2_psum[:, u, 0:D], k.yt[:, u, b * P:(b + 1) * P], second[0][:, b, :],
                                          start=(b == 0), stop=(b == KD - 1))
            mm.then_inc(projected, 1)
        turn(0, 0, True)
        over(pe, TILES, 2, step, last_apart=True)

    @block.vector
    def _(dve):
        link = Chain(dve, link_sem)
        if norm_src is not None:
            ln_stats(nc, k, dve, link, norm_src, done=stat_done, unit=unit)
        if affine or second:
            dve.wait_ge(w_in, 16 * n_loads)
        if second:
            link(nc.vector.tensor_tensor(second[1], second[1], second[2], ALU.add))

        def ahead(c, u):
            if affine:
                dve.wait_ge(prepared, c + 1)
                y = k.ybuf[:, u, :]
                nc.vector.tensor_tensor(y, y, affine[0], ALU.mult).then_inc(fine, 1)
                dve.wait_ge(fine, 3 * c + 1)
                nc.vector.tensor_tensor(y, y, affine[1], ALU.add).then_inc(fine, 1)
                dve.wait_ge(fine, 3 * c + 2)
                nc.vector.tensor_scalar(y, y, 0.0, None, ALU.max).then_inc(fine, 1)
            dve.wait_ge(turned, c + 1)
            if not isinstance(c, int) or c >= 2:
                dve.wait_ge(projected, c - 1)
            nc.vector.tensor_copy(k.yt[:, u, :], k.turn_psum[:, u, 0:D]).then_inc(turned_sb, 1)

        def step(c, u, i, first):
            if not (isinstance(c, int) and c == TILES - 1):
                ahead(c + 1, 1 - u)
            dve.wait_ge(projected, c + 1)
            if second:
                xt = k.x[:, bass.ds(c, 1), :].rearrange("p a f -> p (a f)")
                nc.vector.tensor_tensor(xt, xt, k.out2_psum[:, u, 0:D], ALU.add).then_inc(x_part, 1)
                dve.wait_ge(x_part, c + 1)
                nc.vector.tensor_tensor(xt, xt, second[1], ALU.add)
            out = k.y[:, bass.ds(c, 1), :].rearrange("p a f -> p (a f)")
            nc.vector.tensor_scalar(out, k.out_psum[:, u, 0:D],
                                    one(row_scale, c) if row_scale is not None else 1.0, None, ALU.mult)\
                .then_inc(evacuated, 1)
        ahead(0, 0)
        over(dve, TILES, 2, step, last_apart=True)

    @block.gpsimd
    def _(pool):
        if self_loop:
            own_rows = sem(name + "_own")
            nc.gpsimd.memset(k.acc[:, TILES, :], 0.0).then_inc(own_rows, 1)

            def copy(c, u, i, first):
                pool.wait_ge(evacuated, c + 1)
                pool.nop(nofuse=True)
                nc.gpsimd.tensor_copy(k.acc[:, bass.ds(c, 1), 0:D].rearrange("p a f -> p (a f)"),
                                      k.y[:, bass.ds(c, 1), :].rearrange("p a f -> p (a f)")).then_inc(own_rows, 1)
            over(pool, TILES, 2, copy)
            pool.wait_ge(own_rows, TILES + 1)
        else:
            cleared = sem(name + "_cleared")
            nc.gpsimd.memset(k.acc[:], 0.0).then_inc(cleared, 1)
            pool.wait_ge(cleared, 1)



def wide(row):
    return row.unsqueeze(1).to_broadcast([P, TILES, D])


def narrow(col):
    return col.unsqueeze(2).to_broadcast([P, TILES, D])


def degrees(nc, k):
    done = k.sem("degree_link")
    with nc.Block() as block:
        @block.vector
        def _(dve):
            link = Chain(dve, done)
            t, has = k.ln_work[:, 0, :], k.ln_work[:, 1, :]
            link(nc.vector.tensor_copy(k.degree[:], k.acc[:, 0:TILES, D]))
            link(nc.vector.tensor_scalar(t, k.degree[:], 1.0, None, ALU.add))
            inverse_root(nc, k, dve, link, t, k.dinv_loop[:])
            link(nc.vector.tensor_scalar(t, k.degree[:], 1.0, None, ALU.max))
            inverse_root(nc, k, dve, link, t, k.dinv[:])
            link(nc.vector.tensor_scalar(has, k.degree[:], 0.0, None, ALU.is_gt))
            link(nc.vector.tensor_tensor(k.dinv[:], k.dinv[:], has, ALU.mult))

        @block.scalar
        def _(act):
            serve_root(nc, k, act, 2)


def relu_bias(nc, k, name, vec):
    got, linked = k.sem(name + "_in"), k.sem(name + "_link")
    with nc.sbuf_tensor(name + "_row", [P, D], F32) as row, nc.Block() as block:
        @block.sync
        def _(sp):
            sp.dma_start(row[:], spread(vec)).then_inc(got, 16)

        @block.vector
        def _(dve):
            link = Chain(dve, linked)
            dve.wait_ge(got, 16)
            link(nc.vector.tensor_tensor(k.y[:], k.acc[:, 0:TILES, 0:D], wide(row[:]), ALU.add))
            link(nc.vector.tensor_scalar(k.y[:], k.y[:], 0.0, None, ALU.max))


def add_elu(nc, k, name, vec):
    got, linked, low, raised = (k.sem(name + s) for s in ("_in", "_link", "_low", "_exp"))
    acc = k.acc[:, 0:TILES, 0:D]
    with nc.sbuf_tensor(name + "_row", [P, D], F32) as row, nc.Block() as block:
        @block.sync
        def _(sp):
            sp.dma_start(row[:], spread(vec)).then_inc(got, 16)

        @block.vector
        def _(dve):
            link = Chain(dve, linked)
            dve.wait_ge(got, 16)
            link(nc.vector.tensor_tensor(acc, acc, wide(row[:]), ALU.add))
            nc.vector.tensor_scalar(k.y[:], acc, 0.0, None, ALU.min).then_inc(low, 1)
            link(nc.vector.scalar_tensor_tensor(k.x[:], acc, 0.0, k.x[:], ALU.max, ALU.add))
            dve.wait_ge(raised, 1)
            link(nc.vector.scalar_tensor_tensor(k.x[:], k.y[:], -1.0, k.x[:], ALU.add, ALU.add))

        @block.scalar
        def _(act):
            act.wait_ge(low, 1)
            nc.scalar.activation(k.y[:], k.y[:], ACT.Exp).then_inc(raised, 1)


def add_acc(nc, k, name, scale, to_x):
    linked = k.sem(name + "_link")
    acc = k.acc[:, 0:TILES, 0:D]
    with nc.Block() as block:
        @block.vector
        def _(dve):
            link = Chain(dve, linked)
            if scale is not None:
                link(nc.vector.tensor_tensor(acc if to_x else k.y[:], acc, narrow(scale[:]), ALU.mult))
            if to_x:
                link(nc.vector.tensor_tensor(k.x[:], k.x[:], acc, ALU.add))


def add_norm(nc, k, name, gamma, beta):
    got, linked = k.sem(name + "_in"), k.sem(name + "_link")
    with nc.sbuf_tensor(name + "_rows", [P, 2, D], F32) as row, nc.Block() as block:
        @block.sync
        def _(sp):
            sp.dma_start(row[:, 0, :], spread(gamma)).then_inc(got, 16)
            sp.dma_start(row[:, 1, :], spread(beta)).then_inc(got, 16)

        @block.scalar
        def _(act):
            serve_root(nc, k, act)

        @block.vector
        def _(dve):
            link = Chain(dve, linked)
            ln_stats(nc, k, dve, link, k.y)
            link(nc.vector.tensor_tensor(k.y[:], k.y[:], narrow(k.ln_scale[:]), ALU.mult))
            link(nc.vector.tensor_tensor(k.y[:], k.y[:], narrow(k.ln_shift[:]), ALU.add))
            dve.wait_ge(got, 32)
            link(nc.vector.tensor_tensor(k.y[:], k.y[:], wide(row[:, 0, :]), ALU.mult))
            link(nc.vector.tensor_tensor(k.x[:], k.x[:], wide(row[:, 1, :]), ALU.add))
            link(nc.vector.tensor_tensor(k.x[:], k.x[:], k.y[:], ALU.add))



def gru(nc, k, block, scope, layers):
    def sb(n, shape):
        return scope.enter_context(nc.sbuf_tensor("gru" + n, shape, F32))
    GB = 3 * D // P
    k.gru_h = sb("_h", [P, KD, D])
    k.gru_w = [sb("_wi", [P, GB, D]), sb("_wh", [P, GB, D])]
    k.gru_b = sb("_b", [P, 2, 3 * D])
    k.gru_ht = sb("_ht", [P, KD, D])
    k.gru_wt = [sb("_wit", [P, KD, 3 * D]), sb("_wht", [P, KD, 3 * D])]
    k.gru_rznt = [sb(f"_{x}", [P, KD, D]) for x in "rznt"]
    k.gru_turned = scope.enter_context(nc.psum_tensor("gru_tp", [P, 2, 512], F32))
    k.gru_gates = scope.enter_context(nc.psum_tensor("gru_gates", [P, 2, 512], F32))
    before = None
    for layer in layers:
        before = gru_layer(nc, k, block, before, *layer)


def gru_layer(nc, k, block, before, name, iw, wih, whh, bih, bhh, weight):
    G = 3 * D
    GB = G // P
    sem = k.sem
    got, turned, copied, linked = (sem(name + s) for s in ("_in", "_turned", "_copied", "_link"))
    mul, read, act_done, finished = sem(name + "_mul"), sem(name + "_read"), sem(name + "_act"), sem(name + "_done")
    h, ws, b, ht, wt, tp, gates = k.gru_h, k.gru_w, k.gru_b, k.gru_ht, k.gru_wt, k.gru_turned, k.gru_gates
    r, z, n, t = k.gru_rznt
    turns = [(h[:, rb, cb * P:(cb + 1) * P], ht[:, cb, rb * P:(rb + 1) * P]) for cb in range(KD) for rb in range(KD)]
    for w, o in zip(ws, wt):
        turns += [(w[:, rb, cb * P:(cb + 1) * P], o[:, cb, rb * P:(rb + 1) * P]) for cb in range(KD) for rb in range(GB)]
    @block.sync
    def _(sp):
        if before is not None:
            sp.wait_ge(before, 1)
        sp.dma_start(h[:], rows_of(iw, KD)).then_inc(got, 16)
        sp.dma_start(ws[0][:], rows_of(wih, GB)).then_inc(got, 16)
        sp.dma_start(ws[1][:], rows_of(whh, GB)).then_inc(got, 16)
        sp.dma_start(b[:, 0, :], spread(bih)).then_inc(got, 16)
        sp.dma_start(b[:, 1, :], spread(bhh)).then_inc(got, 16)

    @block.tensor
    def _(pe):
        pe.wait_ge(got, 80)
        for j, (s, _) in enumerate(turns):
            if j >= 2:
                pe.wait_ge(copied, j - 1)
            nc.tensor.transpose(tp[:, j % 2, 0:P], s, k.ident[:]).then_inc(turned, 1)
        pe.wait_ge(copied, len(turns))
        for rb in range(KD):
            if rb:
                pe.wait_ge(read, rb)
            own = [ht[:, cb, rb * P:(rb + 1) * P] for cb in range(KD)]
            for j in range(2 * KD):
                nc.tensor.matmul(gates[:, 0, :], own[j % KD], wt[j // KD][:, j % KD, 0:2 * D],
                                 start=(j == 0), stop=(j == 2 * KD - 1))
            for part in range(2):
                for cb in range(KD):
                    mm = nc.tensor.matmul(gates[:, 1, part * D:(part + 1) * D], own[cb],
                                          wt[part][:, cb, 2 * D:G], start=(cb == 0), stop=(cb == KD - 1))
            mm.then_inc(mul, 1)

    @block.vector
    def _(dve):
        link = Chain(dve, linked)
        for j, (_, o) in enumerate(turns):
            dve.wait_ge(turned, j + 1)
            nc.vector.tensor_copy(o, tp[:, j % 2, 0:P]).then_inc(copied, 1)
        link(nc.vector.tensor_tensor(b[:, 0, 0:2 * D], b[:, 0, 0:2 * D], b[:, 1, 0:2 * D], ALU.add))
        for rb in range(KD):
            dve.wait_ge(mul, rb + 1)
            link(nc.vector.tensor_tensor(r[:, rb, :], gates[:, 0, 0:D], b[:, 0, 0:D], ALU.add))
            link(nc.vector.tensor_tensor(z[:, rb, :], gates[:, 0, D:2 * D], b[:, 0, D:2 * D], ALU.add))
            link(nc.vector.tensor_tensor(n[:, rb, :], gates[:, 1, 0:D], b[:, 0, 2 * D:G], ALU.add))
            nc.vector.tensor_tensor(t[:, rb, :], gates[:, 1, D:2 * D], b[:, 1, 2 * D:G], ALU.add)\
                .then_inc(read, 1)
            dve.wait_ge(read, rb + 1)
        nc.vector.tensor_copy(weight, t[:]).then_inc(act_done, 1)
        dve.wait_ge(act_done, 3)
        link(nc.vector.tensor_tensor(t[:], r[:], t[:], ALU.mult))
        link(nc.vector.tensor_tensor(n[:], n[:], t[:], ALU.add))
        nc.vector.tensor_copy(weight, n[:]).then_inc(act_done, 1)
        dve.wait_ge(act_done, 5)
        link(nc.vector.tensor_scalar(t[:], z[:], -1.0, 1.0, ALU.mult, ALU.add))
        link(nc.vector.tensor_tensor(n[:], n[:], t[:], ALU.mult))
        link(nc.vector.tensor_tensor(z[:], z[:], h[:], ALU.mult))
        nc.vector.tensor_tensor(weight, n[:], z[:], ALU.add).then_inc(finished, 1)
        dve.wait_ge(finished, 1)

    @block.scalar
    def _(act):
        act.wait_ge(act_done, 1)
        nc.scalar.activation(r[:], r[:], ACT.Sigmoid).then_inc(act_done, 1)
        nc.scalar.activation(z[:], z[:], ACT.Sigmoid).then_inc(act_done, 1)
        act.wait_ge(act_done, 4)
        nc.scalar.activation(n[:], n[:], ACT.Tanh).then_inc(act_done, 1)
    return finished



class Experts:

    def __init__(self, name, experts, top, hidden):
        self.name, self.E, self.K, self.F = name, experts, top, hidden
        self.items = TILES * top
        self.FP = min(P, hidden)
        self.FB = hidden // self.FP
        self.tiles = (TILES * P * top + experts * (P - 1)) // P


def route(nc, k, m, router, router_by_expert, bias, mode, slots):
    sem, E, K = k.sem, m.E, m.K
    s = {n: sem(f"{m.name}_{n}") for n in ("in", "stats", "link", "prepared", "kept", "turned", "turned_sb",
                                           "scored", "biased", "rt_turned", "rt", "exp_asked", "exp_done",
                                           "keyed", "slots", "laid")}
    with ExitStack() as scope:
        def sb(n, shape, dt=F32):
            return scope.enter_context(nc.sbuf_tensor(f"{m.name}_{n}", shape, dt))

        def bank(n, shape):
            return scope.enter_context(nc.psum_tensor(f"{m.name}_{n}", shape, F32))
        ybuf, yt = sb("ybuf", [P, 2, D]), sb("yt", [P, 2, D])
        rt = sb("rt", [P, KD, E])
        given = sb("router", [E, D]) if router_by_expert else None
        bias_row = sb("bias", [P, E]) if bias is not None else None
        logits, best, which = sb("logits", [P, TILES, E]), sb("best", [P, TILES, 8]), sb("which", [P, TILES, 8], U32)
        probs, t1, t2 = sb("probs", [P, TILES, E + 8]), sb("t1", [P, TILES]), sb("t2", [P, TILES])
        k.member, k.running = sb("member", [P, E * m.items], BF16), sb("running", [P, max(E * m.items, m.tiles * E)])
        k.pos, k.key = sb("pos", [P, m.items]), sb("key", [P, m.items])
        k.small, k.small_i, k.id_f = sb("small", [P, 5, 32]), sb("small_i", [P, 32], I32), sb("id_f", [1, m.tiles])
        turn_psum, out_psum = bank("turn_psum", [P, 2, 512]), bank("out_psum", [P, 2, 512])
        k.sort_psum, rt_psum = bank("sort_psum", [P, 2, 64]), bank("rt_psum", [P, KD, 64])
        n_in = 1 + (bias is not None)
        choice = k.choice[:, 0:m.items].rearrange("p (t c) -> p t c", c=K)

        def finish(link, pos):
            nc.vector.tensor_copy(k.slot_i[:, 0:m.items], pos).then_inc(s["slots"], 1)

        def key_ready(dve):
            dve.wait_ge(s["keyed"], 1)

        with nc.Block() as block:
            @block.sync
            def _(sp):
                if router_by_expert:
                    sp.dma_start(given[:], router).then_inc(s["in"], 16)
                else:
                    sp.dma_start(rt[:], rows_of(router, KD)).then_inc(s["in"], 16)
                if bias is not None:
                    sp.dma_start(bias_row[:], spread(bias)).then_inc(s["in"], 16)

            @block.scalar
            def _(act):
                serve_root(nc, k, act)
                act.wait_ge(s["stats"], 1)

                def step(c, u, i, first):
                    if not first:
                        act.wait_ge(s["turned"], c - 1)
                        act.wait_ge(s["kept"], c - 1)
                    nc.scalar.activation(ybuf[:, u, :], k.x[:, bass.ds(c, 1), :].rearrange("p a f -> p (a f)"),
                                         ACT.Identity, bias=one(k.ln_shift, c), scale=one(k.ln_scale, c))\
                        .then_inc(s["prepared"], 1)
                over(act, TILES, 2, step)
                if mode != "none":
                    act.wait_ge(s["exp_asked"], 1)
                    used = probs[:, :, 0:E + K if mode == "softmax_all" else K]
                    nc.scalar.activation(used, used, ACT.Exp).then_inc(s["exp_done"], 1)

            @block.gpsimd
            def _(pool):
                def step(c, u, i, first):
                    pool.wait_ge(s["prepared"], c + 1)
                    nc.gpsimd.tensor_copy(k.y[:, bass.ds(c, 1), :].rearrange("p a f -> p (a f)"), ybuf[:, u, :])\
                        .then_inc(s["kept"], 1)
                over(pool, TILES, 2, step)

            @block.tensor
            def _(pe):
                pe.wait_ge(s["in"], 16 * n_in)
                if router_by_expert:
                    for b in range(KD):
                        mm = nc.tensor.transpose(rt_psum[:, b, 0:E], given[:, b * P:(b + 1) * P], k.ident[0:E, 0:E])
                    mm.then_inc(s["rt_turned"], 1)
                    pe.wait_ge(s["rt"], 1)

                def turn(c, u, first):
                    pe.wait_ge(s["prepared"], c + 1)
                    if not first:
                        pe.wait_ge(s["turned_sb"], c - 1)
                    for b in range(KD):
                        mm = nc.tensor.transpose(turn_psum[:, u, b * P:(b + 1) * P], ybuf[:, u, b * P:(b + 1) * P],
                                                 k.ident[:])
                    mm.then_inc(s["turned"], 1)

                def step(c, u, i, first):
                    if not (isinstance(c, int) and c == TILES - 1):
                        turn(c + 1, 1 - u, first and u == 0)
                    pe.wait_ge(s["turned_sb"], c + 1)
                    if not first:
                        pe.wait_ge(s["biased"], c - 1)
                    for b in range(KD):
                        mm = nc.tensor.matmul(out_psum[:, u, 0:E], yt[:, u, b * P:(b + 1) * P], rt[:, b, :],
                                              start=(b == 0), stop=(b == KD - 1))
                    mm.then_inc(s["scored"], 1)
                turn(0, 0, True)
                over(pe, TILES, 2, step, last_apart=True)

            @block.vector
            def _(dve):
                link = Chain(dve, s["link"])
                if router_by_expert:
                    dve.wait_ge(s["rt_turned"], 1)
                    nc.vector.tensor_copy(rt[:], rt_psum[:, :, 0:E]).then_inc(s["rt"], 1)
                ln_stats(nc, k, dve, link, k.x, done=s["stats"])
                if bias is not None:
                    dve.wait_ge(s["in"], 16 * n_in)

                def ahead(c, u):
                    dve.wait_ge(s["turned"], c + 1)
                    if not isinstance(c, int) or c >= 2:
                        dve.wait_ge(s["scored"], c - 1)
                    nc.vector.tensor_copy(yt[:, u, :], turn_psum[:, u, 0:D]).then_inc(s["turned_sb"], 1)

                def step(c, u, i, first):
                    if not (isinstance(c, int) and c == TILES - 1):
                        ahead(c + 1, 1 - u)
                    dve.wait_ge(s["scored"], c + 1)
                    lg = logits[:, bass.ds(c, 1), :].rearrange("p a e -> p (a e)")
                    if bias is None:
                        nc.vector.tensor_scalar(lg, out_psum[:, u, 0:E], 0.0, None, ALU.add).then_inc(s["biased"], 1)
                    else:
                        nc.vector.tensor_tensor(lg, out_psum[:, u, 0:E], bias_row[:], ALU.add).then_inc(s["biased"], 1)
                ahead(0, 0)
                over(dve, TILES, 2, step, last_apart=True)
                dve.wait_ge(s["biased"], TILES)
                for c in range(TILES):
                    ins = nc.vector.max(best[:, c, :], logits[:, c, :])
                link(ins)
                for c in range(TILES):
                    ins = nc.vector.max_index(which[:, c, :], best[:, c, :], logits[:, c, :])
                link(ins)
                link(nc.vector.tensor_copy(k.key[:, :].rearrange("p (t c) -> p t c", c=K), which[:, :, 0:K]))
                if mode == "softmax_all":
                    link(nc.vector.tensor_tensor(probs[:, :, 0:E], logits[:], best[:, :, 0:1].to_broadcast([P, TILES, E]),
                                                 ALU.subtract))
                    nc.vector.tensor_tensor(probs[:, :, E:E + K], best[:, :, 0:K],
                                            best[:, :, 0:1].to_broadcast([P, TILES, K]), ALU.subtract)\
                        .then_inc(s["exp_asked"], 1)
                    dve.wait_ge(s["exp_done"], 1)
                    link(nc.vector.tensor_reduce(t1[:], probs[:, :, 0:E], AX_X, ALU.add))
                    link(nc.vector.reciprocal(t1[:], t1[:]))
                    link(nc.vector.tensor_tensor(probs[:, :, E:E + K], probs[:, :, E:E + K],
                                                 t1[:].unsqueeze(2).to_broadcast([P, TILES, K]), ALU.mult))
                    link(nc.vector.tensor_tensor(t1[:], probs[:, :, E], probs[:, :, E + 1], ALU.add))
                    link(nc.vector.tensor_scalar(t1[:], t1[:], 1e-12, None, ALU.max))
                    link(nc.vector.reciprocal(t1[:], t1[:]))
                    link(nc.vector.tensor_tensor(choice, probs[:, :, E:E + K],
                                                 t1[:].unsqueeze(2).to_broadcast([P, TILES, K]), ALU.mult))
                elif mode == "softmax_top":
                    link(nc.vector.tensor_tensor(probs[:, :, 0:K], best[:, :, 0:K],
                                                 best[:, :, 0:1].to_broadcast([P, TILES, K]), ALU.subtract))
                    nc.vector.memset(t2[:], 0.0).then_inc(s["exp_asked"], 1)
                    dve.wait_ge(s["exp_done"], 1)
                    link(nc.vector.tensor_reduce(t1[:], probs[:, :, 0:K], AX_X, ALU.add))
                    link(nc.vector.reciprocal(t1[:], t1[:]))
                    link(nc.vector.tensor_tensor(choice, probs[:, :, 0:K],
                                                 t1[:].unsqueeze(2).to_broadcast([P, TILES, K]), ALU.mult))
                nc.vector.memset(t2[:], 0.0).then_inc(s["keyed"], 1)
            sort_positions(nc, k, block, m.name + "_sort", key_ready, k.key[:], m.items, E, E, m.tiles,
                           k.slot_expert[0:1, 0:m.tiles], finish)
        with nc.Block() as block:
            @block.gpsimd
            def _(pool):
                for j in range(m.items):
                    nc.gpsimd.indirect_dma_start(slots, bass.IndirectOffsetOnAxis(ap=k.slot_i[:, j:j + 1], axis=0),
                                                 k.y[:, j // K, :], None).then_inc(s["laid"], 16)
                pool.wait_ge(s["laid"], 16 * m.items)


def run_experts(nc, k, m, func, w1, b1, w2, b2, relu_out, slots, results, meanwhile):
    sem, F, FP, FB, E, n = k.sem, m.F, m.FP, m.FB, m.E, m.tiles
    s = {n: sem(f"{m.name}_x_{n}") for n in ("turned", "turned_sb", "up", "hidden", "down", "out", "b1_in",
                                             "b1_turned", "b1", "sum")}
    loaded = [sem(f"{m.name}_x_loaded{u}") for u in range(DEEP)]
    rows_in = [sem(f"{m.name}_x_rows_in{u}") for u in range(DEEP)]
    stored = [sem(f"{m.name}_x_stored{u}") for u in range(DEEP)]
    b2_in = sem(f"{m.name}_x_b2_in")
    rows_b1 = E * FB
    LAG = 2

    def experts_from(engine, c):
        count = min(DEEP, n - c) if isinstance(c, int) else DEEP
        return nc.values_load_multi_w_load_instructions(
            k.slot_expert[0:1, bass.ds(c, count)], engines=[engine], min_val=0, max_val=E - 1)[1]
    with ExitStack() as scope:
        def sb(n, shape, dt=F32):
            return scope.enter_context(nc.sbuf_tensor(f"{m.name}_x_{n}", shape, dt))

        def bank(n, shape):
            return scope.enter_context(nc.psum_tensor(f"{m.name}_x_{n}", shape, F32))
        wa, wb, b2b = sb("wa", [P, DEEP, KD, F]), sb("wb", [FP, DEEP, FB, D]), sb("b2b", [P, E, D])
        xin, xt, h, yo = sb("xin", [P, DEEP, D]), sb("xt", [P, 2, D]), sb("h", [FP, 2, FB, P]), sb("yo", [P, DEEP, D])
        b1_given, b1t = sb("b1_given", [rows_b1, FP]), sb("b1t", [FP, rows_b1])
        turn_psum, h_psum, y_psum = bank("tp", [P, 2, 512]), bank("hp", [FP, 2, 512]), bank("yp", [P, 2, 512])
        b1_psum = bank("b1p", [FP, rows_b1])
        with nc.Block() as block:
            meanwhile(block)

            @block.sync
            def _(sp):
                sp.dma_start(b1_given[:], b1.rearrange("e (b f) -> (e b) f", f=FP)).then_inc(s["b1_in"], 16)
                experts = []

                def step(c, u, i, first):
                    if u == 0:
                        experts[:] = experts_from(mybir.EngineType.SP, c)
                    e = experts[u]
                    if not first:
                        sp.wait_ge(s["turned"], c - DEEP + 1)
                    sp.dma_start(xin[:, u, :], slots[bass.ds(c * P, P), :]).then_inc(rows_in[u], 16)
                    if not first:
                        sp.wait_ge(s["down"], c - DEEP + 1)
                    sp.dma_start(wa[:, u, :, :], w1[bass.ds(e, 1), :, :].rearrange("e (b p) f -> p (e b) f", p=P))\
                        .then_inc(loaded[u], 16)
                    sp.dma_start(wb[:, u, :, :], w2[bass.ds(e, 1), :, :].rearrange("e (b p) f -> p (e b) f", p=FP))\
                        .then_inc(loaded[u], 16)
                    if first and u == 0:
                        sp.dma_start(b2b[:], b2.partition_broadcast(P)).then_inc(b2_in, 16)
                over(sp, n, DEEP, step)

            @block.tensor
            def _(pe):
                pe.wait_ge(s["b1_in"], 16)
                nc.tensor.transpose(b1_psum[:], b1_given[:], k.ident[0:rows_b1, 0:rows_b1]).then_inc(s["b1_turned"], 1)

                def turn(c, u, i, early):
                    pe.wait_ge(rows_in[u], (i + 1) * 16)
                    if not early:
                        pe.wait_ge(s["turned_sb"], c - 1)
                    for b in range(KD):
                        mm = nc.tensor.transpose(turn_psum[:, u % 2, b * P:(b + 1) * P],
                                                 xin[:, u, b * P:(b + 1) * P], k.ident[:])
                    mm.then_inc(s["turned"], 1)

                def down(c, u, early):
                    pe.wait_ge(s["hidden"], c + 1)
                    if not early:
                        pe.wait_ge(s["out"], c - 1)
                    for f in range(FB):
                        mm = nc.tensor.matmul(y_psum[:, u % 2, 0:D], h[:, u % 2, f, :], wb[:, u, f, :],
                                              start=(f == 0), stop=(f == FB - 1))
                    mm.then_inc(s["down"], 1)

                def step(c, u, i, first):
                    if not (isinstance(c, int) and c == n - 1):
                        turn(c + 1, (u + 1) % DEEP, i + (u + 1) // DEEP, first and u == 0)
                    pe.wait_ge(s["turned_sb"], c + 1)
                    pe.wait_ge(loaded[u], (i + 1) * 32)
                    if not first or u >= 2:
                        pe.wait_ge(s["hidden"], c - 1)
                    for f in range(FB):
                        for b in range(KD):
                            mm = nc.tensor.matmul(h_psum[:, u % 2, f * P:(f + 1) * P],
                                                  wa[:, u, b, f * FP:(f + 1) * FP],
                                                  xt[:, u % 2, b * P:(b + 1) * P], start=(b == 0), stop=(b == KD - 1))
                    mm.then_inc(s["up"], 1)
                    if not first or u >= 1:
                        down(c - 1, (u - 1) % DEEP, first and u <= 2)
                turn(0, 0, 0, True)
                over(pe, n, DEEP, step, last_apart=True)
                down(n - 1, (n - 1) % DEEP, False)

            @block.scalar
            def _(act):
                act.wait_ge(s["b1"], 1)
                experts = []

                def store(c, u):
                    act.wait_ge(s["out"], c + 1)
                    act.dma_start(results[bass.ds(c * P, P), :], yo[:, u, :]).then_inc(stored[u], 16)

                def step(c, u, i, first):
                    if u == 0:
                        experts[:] = experts_from(mybir.EngineType.Activation, c)
                    e = experts[u]
                    act.wait_ge(s["up"], c + 1)
                    if not first or u >= 2:
                        act.wait_ge(s["down"], c - 1)
                    for f in range(FB):
                        ins = nc.scalar.activation(h[:, u % 2, f, :], h_psum[:, u % 2, f * P:(f + 1) * P], func,
                                                   bias=b1t[:, bass.ds(e * FB + f, 1)])
                    ins.then_inc(s["hidden"], 1)
                    if not first or u >= LAG:
                        store(c - LAG, (u - LAG) % DEEP)
                over(act, n, DEEP, step)
                for c in range(n - LAG, n):
                    store(c, c % DEEP)
                for u in range(DEEP):
                    act.wait_ge(stored[u], 16 * len(range(u, n, DEEP)))

            @block.vector
            def _(dve):
                dve.wait_ge(s["b1_turned"], 1)
                nc.vector.tensor_copy(b1t[:], b1_psum[:]).then_inc(s["b1"], 1)

                def copy(c, u, early):
                    dve.wait_ge(s["turned"], c + 1)
                    if not early:
                        dve.wait_ge(s["up"], c - 1)
                    nc.vector.tensor_copy(xt[:, u % 2, :], turn_psum[:, u % 2, 0:D]).then_inc(s["turned_sb"], 1)

                def finish(c, u, i, e):
                    dve.wait_ge(s["down"], c + 1)
                    if not isinstance(i, int) or i:
                        dve.wait_ge(stored[u], i * 16)
                    ins = nc.vector.tensor_tensor(yo[:, u, :], y_psum[:, u % 2, 0:D],
                                                  b2b[:, bass.ds(e, 1), :].rearrange("p e f -> p (e f)"), ALU.add)
                    if relu_out:
                        ins.then_inc(s["sum"], 1)
                        dve.wait_ge(s["sum"], c + 1)
                        ins = nc.vector.tensor_scalar(yo[:, u, :], yo[:, u, :], 0.0, None, ALU.max)
                    ins.then_inc(s["out"], 1)

                def step(c, u, i, first):
                    if not (isinstance(c, int) and c == n - 1):
                        copy(c + 1, u + 1, first and u == 0)
                    if u == 0:
                        experts[:] = experts_from(mybir.EngineType.DVE, c if first else c - 1)
                        experts[:0] = [None] * first
                    if not first or u >= 1:
                        finish(c - 1, (u - 1) % DEEP, i if u else i - 1, experts[u])
                experts = []
                copy(0, 0, True)
                dve.wait_ge(b2_in, 16)
                over(dve, n, DEEP, step, last_apart=True, peeled=2)
                finish(n - 1, (n - 1) % DEEP, (n - 1) // DEEP, experts_from(mybir.EngineType.DVE, n - 1)[0])


def combine(nc, k, m, results, into, weighted):
    added = k.sem(m.name + "_c_added")
    gathered = [k.sem(f"{m.name}_c_gathered{u}") for u in range(GROUP)]
    with nc.sbuf_tensor(m.name + "_c_rows", [P, GROUP, D], F32) as rows, nc.Block() as block:
        @block.gpsimd
        def _(pool):
            for j in range(m.items):
                if j >= GROUP:
                    pool.wait_ge(added, j - GROUP + 1)
                nc.gpsimd.indirect_dma_start(rows[:, j % GROUP, :], None, results[0:m.tiles * P, :],
                                             bass.IndirectOffsetOnAxis(ap=k.slot_i[:, j:j + 1], axis=0))\
                    .then_inc(gathered[j % GROUP], 16)

        @block.vector
        def _(dve):
            for j in range(m.items):
                dve.wait_ge(gathered[j % GROUP], (j // GROUP + 1) * 16)
                if j:
                    dve.wait_ge(added, j)
                to = into[:, j // m.K, :]
                if weighted:
                    ins = nc.vector.scalar_tensor_tensor(to, rows[:, j % GROUP, :], k.choice[:, j:j + 1], to,
                                                         ALU.mult, ALU.add)
                else:
                    ins = nc.vector.tensor_tensor(to, to, rows[:, j % GROUP, :], ALU.add)
                ins.then_inc(added, 1)


def add_y(nc, k, block):
    done = k.sem("added_y")

    @block.gpsimd
    def _(pool):
        nc.gpsimd.tensor_tensor(k.x[:], k.x[:], k.y[:], ALU.add).then_inc(done, 1)
        pool.wait_ge(done, 1)



def pooled_ffn(nc, k, meanwhile, router, router_bias, w1, b1, w2, b2):
    E, _, F = w1.shape
    FB, K = F // P, 2
    capacity = float(-(-N * 5 // (4 * E)))
    sem = k.sem
    s = {n: sem("pool_" + n) for n in ("in", "stats", "link", "prepared", "kept", "turned", "turned_sb", "mean",
                                       "scored", "chosen", "exp_asked", "exp_done", "wide", "experts_in", "scaled",
                                       "b1_turned", "up", "hidden", "down", "out", "sum")}
    with ExitStack() as scope:
        def sb(n, shape, dt=F32):
            return scope.enter_context(nc.sbuf_tensor("pool_" + n, shape, dt))

        def bank(n, shape):
            return scope.enter_context(nc.psum_tensor("pool_" + n, shape, F32))
        ybuf, rt, rb = sb("ybuf", [P, 2, D]), sb("rt", [P, KD, E]), sb("rb", [1, E])
        yt = k.acc[:, :, :].rearrange("p t f -> p (t f)")[:, 0:KD * TILES * P].rearrange("p (b n) -> p b n", b=KD)
        mean, lg, t = sb("mean", [P, KD]), sb("lg", [1, 8]), sb("t", [1, 8])
        best, which, cw = sb("best", [1, 8]), sb("which", [1, 8], U32), sb("cw", [1, K])
        cwb = sb("cwb", [P, K])
        wa, wb, b2b = sb("wa", [P, K, KD, F]), sb("wb", [P, K, FB, D]), sb("b2b", [P, K, D])
        b1_given, b1t, b1s = sb("b1_given", [E * FB, P]), sb("b1t", [P, E * FB]), sb("b1s", [P, K, FB])
        h = sb("h", [P, 2, K * FB, P])
        turn_psum = bank("tp", [P, 2, 512])
        small_psum = bank("sp", [P, 512])
        h_psum, y_psum = bank("hp", [P, K, 512]), bank("yp", [P, 2, 512])
        with nc.Block() as block:
            @block.sync
            def _(sp):
                sp.dma_start(rt[:], rows_of(router, KD)).then_inc(s["in"], 16)
                sp.dma_start(rb[:], router_bias.rearrange("(a e) -> a e", a=1)).then_inc(s["in"], 16)
                sp.dma_start(b1_given[:], b1.rearrange("e (b f) -> (e b) f", f=P)).then_inc(s["in"], 16)
                sp.wait_ge(s["chosen"], 1)
                for j in range(K):
                    e = sp.value_load(which[0:1, j:j + 1], min_val=0, max_val=E - 1)
                    sp.dma_start(wa[:, j, :, :], w1[bass.ds(e, 1), :, :].rearrange("e (b p) f -> p (e b) f", p=P))\
                        .then_inc(s["experts_in"], 16)
                    sp.dma_start(wb[:, j, :, :], w2[bass.ds(e, 1), :, :].rearrange("e (b p) f -> p (e b) f", p=P))\
                        .then_inc(s["experts_in"], 16)
                    sp.dma_start(b2b[:, j, :], b2[bass.ds(e, 1), :].rearrange("e f -> (e f)").partition_broadcast(P))\
                        .then_inc(s["experts_in"], 16)

            @block.scalar
            def _(act):
                serve_root(nc, k, act)
                act.wait_ge(s["stats"], 1)

                def step(c, u, i, first):
                    if not first:
                        act.wait_ge(s["turned"], c - 1)
                        act.wait_ge(s["kept"], c - 1)
                    nc.scalar.activation(ybuf[:, u, :], k.x[:, bass.ds(c, 1), :].rearrange("p a f -> p (a f)"),
                                         ACT.Identity, bias=one(k.ln_shift, c), scale=one(k.ln_scale, c))\
                        .then_inc(s["prepared"], 1)
                over(act, TILES, 2, step)
                for n in range(3):
                    act.wait_ge(s["exp_asked"], n + 1)
                    nc.scalar.activation(t[:], t[:], ACT.Exp).then_inc(s["exp_done"], 1)

                def gelu(c, u, i, first):
                    if not first:
                        act.wait_ge(s["down"], c - 1)
                    for j in range(K):
                        act.wait_ge(s["up"], c * K + j + 1)
                        for f in range(FB):
                            ins = nc.scalar.activation(h[:, u, j * FB + f, :], h_psum[:, j, f * P:(f + 1) * P],
                                                       ACT.Gelu, bias=b1s[:, j, f:f + 1])
                        ins.then_inc(s["hidden"], 1)
                act.wait_ge(s["scaled"], 1)
                over(act, TILES, 2, gelu)

            @block.gpsimd
            def _(pool):
                def step(c, u, i, first):
                    pool.wait_ge(s["prepared"], c + 1)
                    nc.gpsimd.tensor_copy(k.y[:, bass.ds(c, 1), :].rearrange("p a f -> p (a f)"), ybuf[:, u, :])\
                        .then_inc(s["kept"], 1)
                over(pool, TILES, 2, step)

            meanwhile(block)

            @block.tensor
            def _(pe):
                pe.wait_ge(s["in"], 48)
                nc.tensor.transpose(small_psum[:, 0:E * FB], b1_given[:], k.ident[0:E * FB, 0:E * FB])\
                    .then_inc(s["b1_turned"], 1)

                def step(c, u, i, first):
                    pe.wait_ge(s["prepared"], c + 1)
                    if not first:
                        pe.wait_ge(s["turned_sb"], c - 1)
                    for b in range(KD):
                        mm = nc.tensor.transpose(turn_psum[:, u, b * P:(b + 1) * P], ybuf[:, u, b * P:(b + 1) * P],
                                                 k.ident[:])
                    mm.then_inc(s["turned"], 1)
                over(pe, TILES, 2, step)
                pe.wait_ge(s["mean"], 1)
                for b in range(KD):
                    mm = nc.tensor.matmul(y_psum[0:1, 0, 0:E], mean[:, b:b + 1], rt[:, b, :],
                                          start=(b == 0), stop=(b == KD - 1))
                mm.then_inc(s["scored"], 1)
                pe.wait_ge(s["chosen"], 2)
                nc.tensor.matmul(y_psum[:, 1, 0:K], k.ones[0:1, :], cw[:], start=True, stop=True)\
                    .then_inc(s["wide"], 1)
                pe.wait_ge(s["scaled"], 1)

                def down(c, u, early):
                    pe.wait_ge(s["hidden"], c * K + K)
                    if not early:
                        pe.wait_ge(s["out"], c)
                    for j in range(K * FB):
                        mm = nc.tensor.matmul(y_psum[:, u, 0:D], h[:, u, j, :], wb[:, j // FB, j % FB, :],
                                              start=(j == 0), stop=(j == K * FB - 1))
                    mm.then_inc(s["down"], 1)

                def work(c, u, i, first):
                    for j in range(K):
                        if not (first and u == 0):
                            pe.wait_ge(s["hidden"], c * K + j - 1)
                        for f in range(FB):
                            for b in range(KD):
                                mm = nc.tensor.matmul(h_psum[:, j, f * P:(f + 1) * P], wa[:, j, b, f * P:(f + 1) * P],
                                                      yt[:, b, bass.ds(c * P, P)], start=(b == 0), stop=(b == KD - 1))
                        mm.then_inc(s["up"], 1)
                    if not first or u:
                        down(c - 1, 1 - u, first)
                over(pe, TILES, 2, work)
                down(TILES - 1, (TILES - 1) % 2, False)

            @block.vector
            def _(dve):
                link = Chain(dve, s["link"])
                dve.wait_ge(s["b1_turned"], 1)
                link(nc.vector.tensor_copy(b1t[:], small_psum[:, 0:E * FB]))
                ln_stats(nc, k, dve, link, k.x, done=s["stats"])

                def step(c, u, i, first):
                    dve.wait_ge(s["turned"], c + 1)
                    nc.vector.tensor_scalar(yt[:, :, bass.ds(c * P, P)],
                                            turn_psum[:, u, 0:D].rearrange("p (b n) -> p b n", b=KD), 1.0, None, ALU.mult)\
                        .then_inc(s["turned_sb"], 1)
                over(dve, TILES, 2, step)
                dve.wait_ge(s["turned_sb"], TILES)
                link(nc.vector.tensor_reduce(mean[:], yt[:, :, 0:N], AX_X, ALU.add))
                nc.vector.tensor_scalar(mean[:], mean[:], 1.0 / N, None, ALU.mult).then_inc(s["mean"], 1)
                dve.wait_ge(s["scored"], 1)
                link(nc.vector.tensor_tensor(lg[:], y_psum[0:1, 0, 0:E], rb[:], ALU.add))

                def softmax(n):
                    link(nc.vector.tensor_reduce(best[:, 0:1], lg[:], AX_X, ALU.max))
                    nc.vector.tensor_scalar(t[:], lg[:], best[:, 0:1], None, ALU.subtract).then_inc(s["exp_asked"], 1)
                    dve.wait_ge(s["exp_done"], n)
                    link(nc.vector.tensor_reduce(best[:, 0:1], t[:], AX_X, ALU.add))
                    link(nc.vector.reciprocal(best[:, 0:1], best[:, 0:1]))
                    link(nc.vector.tensor_scalar(lg[:], t[:], best[:, 0:1], None, ALU.mult))
                softmax(1)
                link(nc.vector.tensor_scalar(t[:], lg[:], float(N), None, ALU.mult))
                link(nc.vector.reciprocal(t[:], t[:]))
                link(nc.vector.tensor_scalar(t[:], t[:], capacity, 1.0, ALU.mult, ALU.min))
                link(nc.vector.tensor_tensor(lg[:], lg[:], t[:], ALU.mult))
                softmax(2)
                link(nc.vector.max(best[:], lg[:]))
                nc.vector.max_index(which[:], best[:], lg[:]).then_inc(s["chosen"], 1)
                nc.vector.tensor_scalar(t[:], best[:], best[:, 0:1], None, ALU.subtract).then_inc(s["exp_asked"], 1)
                dve.wait_ge(s["exp_done"], 3)
                link(nc.vector.tensor_reduce(lg[:, 0:1], t[:, 0:K], AX_X, ALU.add))
                link(nc.vector.reciprocal(lg[:, 0:1], lg[:, 0:1]))
                nc.vector.tensor_scalar(cw[:], t[:, 0:K], lg[:, 0:1], None, ALU.mult).then_inc(s["chosen"], 1)
                dve.wait_ge(s["wide"], 1)
                link(nc.vector.tensor_copy(cwb[:], y_psum[:, 1, 0:K]))
                dve.wait_ge(s["experts_in"], 48 * K)
                for j in range(K):
                    link(nc.vector.tensor_scalar(wb[:, j, :, :], wb[:, j, :, :], cwb[:, j:j + 1], None, ALU.mult))
                    link(nc.vector.tensor_scalar(b2b[:, j, :], b2b[:, j, :], cwb[:, j:j + 1], None, ALU.mult))
                    e = dve.value_load(which[0:1, j:j + 1], min_val=0, max_val=E - 1)
                    link(nc.vector.tensor_copy(b1s[:, j, :], b1t[:, bass.ds(e * FB, FB)]))
                nc.vector.tensor_tensor(b2b[:, 0, :], b2b[:, 0, :], b2b[:, 1, :], ALU.add).then_inc(s["scaled"], 1)

                def out(c, u, i, first):
                    dve.wait_ge(s["down"], c + 1)
                    to = k.y[:, bass.ds(c, 1), :].rearrange("p a f -> p (a f)")
                    nc.vector.tensor_tensor(to, to, y_psum[:, u, 0:D], ALU.add).then_inc(s["out"], 1)
                    dve.wait_ge(s["out"], c + 1)
                    nc.vector.tensor_tensor(to, to, b2b[:, 0, :], ALU.add)
                dve.wait_ge(s["kept"], TILES)
                over(dve, TILES, 2, out)



def rows_of(w, blocks):
    return w.rearrange("(b p) n -> p b n", p=P)


def spread(v):
    return v.partition_broadcast(P)


def build(nc, a, out):
    k = Shared()
    k.made = 0

    def numbered(name):
        k.made += 1
        k.used.append(nc.alloc_semaphore(f"{name}_{k.made}"))
        return k.used[-1]
    k.sem, k.used = numbered, []

    def reuse_semaphores():
        nc.clear_and_free_semaphores(k.used)
        nc.all_engine_barrier()
        k.used = []
    ctx = ExitStack()

    def held(scope, name, shape, dt=F32):
        k.made += 1
        t = scope.enter_context(nc.sbuf_tensor(f"{name}_{k.made}", shape, dt))
        return t

    def bank(scope, name, shape):
        k.made += 1
        t = scope.enter_context(nc.psum_tensor(f"{name}_{k.made}", shape, F32))
        return t

    def dram(name, shape, dt=F32):
        return nc.dram_tensor(name, shape, dt).ap()

    k.by_dst = dram("by_dst", (P * SLOTS, 4))
    k.by_src = dram("by_src", (P * SLOTS, 4))
    table = dram("table", (TILES * P, D))

    with ctx:
        k.ident = held(ctx, "ident", [P, P])
        k.before = held(ctx, "before", [P, P])
        k.ones = held(ctx, "ones", [P, P])
        k.count_i = held(ctx, "count_i", [P, CHUNKS], I32)
        k.count = held(ctx, "count", [P, CHUNKS])
        k.x = held(ctx, "x", [P, TILES, D])
        k.y = held(ctx, "y", [P, TILES, D])
        k.acc = held(ctx, "acc", [P, NB, D + 1])
        k.pos_dst = held(ctx, "pos_dst", [P, L], I32)
        k.pos_src = held(ctx, "pos_src", [P, L], I32)
        k.edge_dst = held(ctx, "edge_dst", [P, L, 4])
        k.edge_src = held(ctx, "edge_src", [P, L, 4])
        k.rec_dst = held(ctx, "rec_dst", [P, SLOTS, 4])
        k.ids_dst = held(ctx, "ids_dst", [1, CHUNKS], I32)
        k.ids_src = held(ctx, "ids_src", [1, CHUNKS], I32)
        k.index = held(ctx, "index", [P, PARTS, GROUP], I32)
        k.one_col = held(ctx, "one_col", [P, 1], BF16)
        k.records = held(ctx, "records", [P, 2, GROUP, 4])
        k.stats = held(ctx, "stats", [P, TILES, 6])
        k.ln_work = held(ctx, "ln_work", [P, 6, TILES])
        k.ln_scale = held(ctx, "ln_scale", [P, TILES])
        k.ln_shift = held(ctx, "ln_shift", [P, TILES])
        k.root_in = held(ctx, "root_in", [P, TILES])
        k.root_out = held(ctx, "root_out", [P, TILES])
        k.choice = held(ctx, "choice", [P, 2 * TILES])
        k.slot_i = held(ctx, "slot_i", [P, 2 * TILES], I32)
        k.slot_expert = held(ctx, "slot_expert", [1, SLOT_TILES], I32)
        k.gru0 = held(ctx, "gru0", [P, KD, D])
        k.gru1 = held(ctx, "gru1", [P, KD, D])
        k.dinv_loop = held(ctx, "dinv_loop", [P, TILES])
        k.dinv = held(ctx, "dinv", [P, TILES])
        k.degree = held(ctx, "degree", [P, TILES])
        k.root_asked, k.root_done = nc.alloc_semaphore("root_asked"), nc.alloc_semaphore("root_done")
        k.roots = k.served = 0

        def gnn_buffers(scope):
            k.ybuf = held(scope, "ybuf", [P, 2, D])
            k.yt = held(scope, "yt", [P, 2, D])
            k.w_a = held(scope, "w_a", [P, KD, D])
            k.turn_psum = bank(scope, "turn_psum", [P, 2, 512])
            k.out_psum = bank(scope, "out_psum", [P, 2, 512])

        def sum_buffers(scope):
            k.rows = held(scope, "rows", [P, RING, D])
            k.hot = held(scope, "hot", [P, RING, P])
            k.away = held(scope, "away", [P, 2, P])
            k.hot1 = held(scope, "hot1", [P, RING, P], BF16)
            k.sum_psum = bank(scope, "sum_psum", [P, BANKS, 512])

        slots = dram("slots", (SLOT_TILES * P, D))
        results = dram("results", (SLOT_TILES * P, D))

        with ExitStack() as scope:
            k.dst = held(scope, "dst", [P, L], I32)
            k.src = held(scope, "src", [P, L], I32)
            k.w = held(scope, "w", [P, L])
            k.key_i = held(scope, "key_i", [P, L], I32)
            k.key = held(scope, "key", [P, L])
            k.pos = held(scope, "pos", [P, L])
            k.member = k.y[:, :, :].rearrange("p t f -> p (t f)").bitcast(BF16)
            k.running = held(scope, "running", [P, max(NB * L, TILES * CHUNKS)])
            k.small = held(scope, "small", [P, 5, 32])
            k.small_i = held(scope, "small_i", [P, 32], I32)
            k.id_f = held(scope, "id_f", [1, CHUNKS])
            k.sort_psum = bank(scope, "sort_psum", [P, 2, 64])
            with nc.Block() as block:
                constants(nc, k, block)
                load_edges(nc, k, block, a)
            with nc.Block() as block:
                sort_edges(nc, k, block, k.dst, k.src, k.w, k.edge_dst, k.pos_dst, k.ids_dst, "dst",
                           lambda dve: dve.wait_ge(k.edges_in, 96))
                load_x(nc, k, block, a["x"], slots)
            with nc.Block() as block:
                scatter_edges(nc, k, block, "dst0", k.pos_dst, k.edge_dst, k.by_dst, 0, FIRST_GROUPS)
                sort_edges(nc, k, block, k.src, k.dst, k.w, k.edge_src, k.pos_src, k.ids_src, "src",
                           lambda dve: dve.wait_ge(k.edges_in, 96))

        def projected(name, weight=None, weight_in=None, meanwhile=lambda block, scope: None, **more):
            with ExitStack() as scope:
                gnn_buffers(scope)
                loads = list(more.pop("loads", ()))
                if weight_in is not None:
                    loads.append((k.w_a[:], rows_of(weight_in, KD)))
                    weight = k.w_a
                with nc.Block() as block:
                    project(nc, k, block, name, weight, table, loads=loads, **more)
                    meanwhile(block, scope)

        src_groups = [0]

        def some_src(name, groups):
            start = src_groups[0]
            src_groups[0] += groups
            return lambda block, scope=None: scatter_edges(nc, k, block, name, k.pos_src, k.edge_src, k.by_src,
                                                           start, groups)

        def summed(name, ids, weighted, degree):
            with ExitStack() as scope:
                sum_buffers(scope)
                with nc.Block() as block:
                    spmm(nc, k, block, name, table, k.rec_dst, ids, weighted, degree)

        def routed(m, func, router, by_expert, bias, mode, w1, b1, w2, b2, relu_out,
                   meanwhile=lambda block: None):
            route(nc, k, m, router, by_expert, bias, mode, slots)
            run_experts(nc, k, m, func, w1, b1, w2, b2, relu_out, slots, results, meanwhile)

        def weights_and_edges(block, scope):
            gru(nc, k, block, scope,
                [(f"gru{n}", *(a[f"L1_gnn_{v}{n}"] for v in ("iw", "wih", "whh", "bih", "bhh")), w[:])
                 for n, w in enumerate((k.gru0, k.gru1))])
            scatter_edges(nc, k, block, "dst1", k.pos_dst, k.edge_dst, k.by_dst, FIRST_GROUPS,
                          L // GROUP - FIRST_GROUPS)
        projected("l0a", weight_in=a["L0_gnn_W1"], norm_src=k.x, unit=True, meanwhile=weights_and_edges)
        with nc.Block() as block:
            load_records(nc, k, block, k.by_dst, k.rec_dst, "dst")
        summed("l0a", k.ids_dst, True, True)
        degrees(nc, k)
        relu_bias(nc, k, "l0r", a["L0_gnn_b1"])
        projected("l0b", weight_in=a["L0_gnn_W2"], plain_src=k.y, meanwhile=some_src("src0", 5))
        summed("l0b", k.ids_dst, True, False)
        add_elu(nc, k, "l0e", a["L0_gnn_b2"])
        reuse_semaphores()
        m = Experts("m0", 8, 2, 256)
        rest = some_src("src1", 13)
        routed(m, ACT.Gelu, a["L0_ffn_router_w"], True, None, "softmax_all",
               a["L0_ffn_w1"], a["L0_ffn_b1"], a["L0_ffn_w2"], a["L0_ffn_b2"], False,
               lambda block: (add_y(nc, k, block), rest(block)))
        combine(nc, k, m, results, k.x, True)
        reuse_semaphores()
        projected("l1a", weight=k.gru0, norm_src=k.x, row_scale=k.dinv_loop, self_loop=True)
        summed("l1a", k.ids_dst, False, False)
        add_acc(nc, k, "l1a", k.dinv_loop, False)
        with nc.sbuf_tensor("l1_affine", [P, 2, D], F32) as affine:
            projected("l1b", weight=k.gru1, norm_src=k.y, affine=(affine[:, 0, :], affine[:, 1, :]),
                      row_scale=k.dinv_loop, self_loop=True,
                      loads=[(affine[:, 0, :], spread(a["L1_gnn_ln_g0"])), (affine[:, 1, :], spread(a["L1_gnn_ln_b0"]))])
        summed("l1b", k.ids_dst, False, False)
        add_acc(nc, k, "l1b", k.dinv_loop, True)
        reuse_semaphores()
        m = Experts("m1", 32, 1, 64)
        routed(m, ACT.Relu, a["L1_ffn_router_w"], True, a["L1_ffn_router_b"], "none",
               a["L1_ffn_W1"], a["L1_ffn_b1"], a["L1_ffn_W2"], a["L1_ffn_b2"], True,
               some_src("src2", 7))
        combine(nc, k, m, results, k.x, False)
        reuse_semaphores()
        projected("l2", weight_in=a["L2_gnn_W"], norm_src=k.x, row_scale=k.dinv)
        summed("l2", k.ids_dst, False, False)
        add_acc(nc, k, "l2", k.dinv, True)
        reuse_semaphores()
        pooled_ffn(nc, k, some_src("src3", L // GROUP - src_groups[0]), a["L2_ffn_Wr"], a["L2_ffn_br"], a["L2_ffn_W1"], a["L2_ffn_b1"], a["L2_ffn_W2"], a["L2_ffn_b2"])
        add_norm(nc, k, "l2n", a["L2_ffn_gamma"], a["L2_ffn_beta"])
        reuse_semaphores()
        with nc.Block() as block:
            load_records(nc, k, block, k.by_src, k.rec_dst, "src")
        with nc.sbuf_tensor("l3_wr", [P, KD, D], F32) as wr, nc.sbuf_tensor("l3_b", [P, 2, D], F32) as b, \
                nc.psum_tensor("l3_psum", [P, 2, 512], F32) as k.out2_psum:
            projected("l3", weight_in=a["L3_gnn_weight_l"], norm_src=k.x, second=(wr, b[:, 0, :], b[:, 1, :]),
                      loads=[(wr[:], rows_of(a["L3_gnn_weight_r"], KD)), (b[:, 0, :], spread(a["L3_gnn_bias_l"])),
                             (b[:, 1, :], spread(a["L3_gnn_bias_r"]))])
        summed("l3", k.ids_src, True, False)
        add_acc(nc, k, "l3", None, True)
        reuse_semaphores()
        m = Experts("m3", 16, 2, 512)
        routed(m, ACT.Relu, a["L3_ffn_gate_w"], False, a["L3_ffn_gate_b"], "softmax_top",
               a["L3_ffn_w1"], a["L3_ffn_b1"], a["L3_ffn_w2"], a["L3_ffn_b2"], False)
        combine(nc, k, m, results, k.y, True)
        add_norm(nc, k, "l3n", a["L3_ffn_gamma"], a["L3_ffn_beta"])
        last = k.sem("out_stored")
        with nc.Block() as block:
            @block.sync
            def _(sp):
                sp.dma_start(out[0:(TILES - 1) * P, :].rearrange("(t p) f -> p t f", p=P), k.x[:, 0:TILES - 1, :])\
                    .then_inc(last, 16)
                sp.dma_start(out[(TILES - 1) * P:N, :], k.x[0:LAST, TILES - 1, :]).then_inc(last, 16)
                sp.wait_ge(last, 32)


def kernel(**inputs):
    import numpy as _np
    import concourse.bacc as _bacc
    from concourse import mybir as _mybir
    from concourse.bass_utils import run_bass_kernel_spmd as _run

    nc = _bacc.Bacc("TRN2", target_bir_lowering=False, num_devices=1)
    arrays, given = {}, {}
    for name, value in inputs.items():
        v = _np.ascontiguousarray(value)
        arrays[f"in_{name}_dram"] = v
        given[name] = nc.dram_tensor(f"in_{name}_dram", v.shape, _mybir.dt.from_np(v.dtype), kind="ExternalInput").ap()
    out = nc.dram_tensor("out_0_dram", (N, D), F32, kind="ExternalOutput").ap()
    build(nc, given, out)
    r = _run(nc, [arrays], core_ids=[0])
    return r.results[0]["out_0_dram"]
```

```python
from contextlib import ExitStack

import concourse.bass as bass
from concourse import mybir

F32 = mybir.dt.float32
BF16 = mybir.dt.bfloat16
I32 = mybir.dt.int32
U32 = mybir.dt.uint32
ALU = mybir.AluOpType
ACT = mybir.ActivationFunctionType
AX_X = mybir.AxisListType.X

P = 128
N, D, NE = 3125, 256, 50000
KD = D // P
TILES = -(-N // P)
LAST = N - (TILES - 1) * P
GROUP = 8
PARTS = 4
RING = PARTS * GROUP
BANKS = 4
DEEP = 4
L = -(-NE // (P * GROUP)) * GROUP
LAST_L = NE - (P - 1) * L
NB = TILES + 1
REAL_CHUNKS = (NE + TILES * (P - 1)) // P
CHUNKS = -(-REAL_CHUNKS // RING) * RING
SLOTS = REAL_CHUNKS + -(-(P * L - NE) // P)
SLOT_TILES = 66
FIRST_GROUPS = 3
SECOND_GROUPS = 8
LN_EPS = 1e-5
NO_NODE = 200.0


def over(eng, n, ways, body, last_apart=False, peeled=1):
    rounds = (n - last_apart) // ways
    for c in range(peeled * ways):
        body(c, c % ways, c // ways, c < ways)
    with eng.Fori(peeled, rounds) as i:
        for u in range(ways):
            body(i * ways + u, u, i, False)
    for u in range(n - rounds * ways):
        body(rounds * ways + u, u, rounds, False)


class Shared:
    pass


class Chain:

    def __init__(self, eng, sem):
        self.eng, self.sem, self.n = eng, sem, 0

    def __call__(self, ins):
        self.n += 1
        ins.then_inc(self.sem, 1)
        self.eng.wait_ge(self.sem, self.n)


def one(ap, i, n=1):
    return ap[:, bass.ds(i, n)]



def constants(nc, k, block):
    sem = k.sem
    filled, cut, row = sem("const_filled"), sem("const_cut"), sem("const_row")

    @block.gpsimd
    def _(pool):
        nc.gpsimd.memset(k.ident[:], 1.0).then_inc(filled, 1)
        nc.gpsimd.memset(k.before[:], 1.0).then_inc(filled, 1)
        nc.gpsimd.memset(k.ones[:], 1.0).then_inc(filled, 1)
        nc.gpsimd.memset(k.one_col[:], 1.0).then_inc(filled, 1)
        pool.wait_ge(filled, 4)
        nc.gpsimd.affine_select(out=k.ident[:], in_=k.ident[:], compare_op=ALU.is_equal, fill=0.0,
                                base=0, pattern=[[-1, P]], channel_multiplier=1).then_inc(cut, 1)
        nc.gpsimd.affine_select(out=k.before[:], in_=k.before[:], compare_op=ALU.is_gt, fill=0.0,
                                base=0, pattern=[[1, P]], channel_multiplier=-1).then_inc(cut, 1)
        nc.gpsimd.iota(k.count_i[:], pattern=[[1, CHUNKS]], base=0, channel_multiplier=0).then_inc(row, 1)
        pool.wait_ge(cut, 2)

    @block.vector
    def _(dve):
        dve.wait_ge(row, 1)
        nc.vector.tensor_copy(k.count[:], k.count_i[:]).then_inc(row, 1)
        dve.wait_ge(row, 2)



def sort_positions(nc, k, block, name, key_ready, key, items, buckets, real, chunks, ids, finish):
    sem = k.sem
    link_sem, counted, offset = sem(name + "_link"), sem(name + "_counted"), sem(name + "_offset")
    member, running, pos, small, psum = k.member, k.running, k.pos, k.small, k.sort_psum
    m = member[:, 0:buckets * items].rearrange("p (b l) -> p b l", b=buckets)
    s = running[:, 0:buckets * items].rearrange("p (b l) -> p b l", b=buckets)
    prev, cnt, chunk_f, end, off = (small[:, j, 0:buckets] for j in range(5))
    chunk_i = k.small_i[:, 0:buckets]
    long = items > P
    masked = sem(name + "_masked") if long else None

    @block.vector
    def _(dve):
        link = Chain(dve, link_sem)
        key_ready(dve)
        if long:
            for b in range(buckets):
                ins = nc.vector.tensor_scalar(m[:, b, :], key, float(b), None, ALU.is_equal)
            link(ins)
        else:
            link(nc.vector.tensor_tensor(m, key.unsqueeze(1).to_broadcast([P, buckets, items]),
                                         k.count[:, 0:buckets].unsqueeze(2).to_broadcast([P, buckets, items]),
                                         ALU.is_equal))
        flat = member[:, 0:buckets * items]
        link(nc.vector.tensor_tensor_scan(running[:, 0:buckets * items], flat, flat, 0.0, ALU.add, ALU.max))
        nc.vector.memset(prev[:, 0:1], 0.0).then_inc(link_sem, 1)
        link.n += 1
        link(nc.vector.tensor_copy(prev[:, 1:buckets], s[:, 0:buckets - 1, items - 1]))
        nc.vector.tensor_tensor(cnt, s[:, :, items - 1], prev, ALU.subtract).then_inc(counted, 1)
        dve.wait_ge(offset, 1)
        link(nc.vector.tensor_scalar(chunk_i, psum[:, 1, 0:buckets], float(P - 1), None, ALU.add))
        link(nc.vector.tensor_scalar(chunk_i, chunk_i, 7, None, ALU.arith_shift_right))
        link(nc.vector.tensor_copy(chunk_f, chunk_i))
        link(nc.vector.tensor_tensor_scan(end, chunk_f, chunk_f, 0.0, ALU.add, ALU.max))
        link(nc.vector.tensor_tensor(off, end, chunk_f, ALU.subtract))
        link(nc.vector.scalar_tensor_tensor(off, off, float(P), psum[:, 0, 0:buckets], ALU.mult, ALU.add))
        link(nc.vector.scalar_tensor_tensor(off, off, -1.0, prev, ALU.add, ALU.subtract))
        for b in range(buckets):
            ins = nc.vector.scalar_tensor_tensor(s[:, b, :], s[:, b, :], off[:, b:b + 1], m[:, b, :],
                                                 ALU.add, ALU.mult)
            if long:
                ins.then_inc(masked, 1)
        if long:
            dve.wait_ge(offset, 2)
            link(nc.vector.tensor_copy(pos[:, 0:items], k.pos_psum[:, 0:items]))
        else:
            link(ins)
            link(nc.vector.tensor_reduce(pos[:, 0:items], s.rearrange("p b l -> p l b"), AX_X, ALU.add))
        finish(link, pos[:, 0:items])
        ends = running[0:1, 0:chunks * real].rearrange("p (c b) -> p c b", b=real)
        link(nc.vector.tensor_tensor(ends, k.count[0:1, 0:chunks].unsqueeze(2).to_broadcast([1, chunks, real]),
                                     end[0:1, 0:real].unsqueeze(1).to_broadcast([1, chunks, real]), ALU.is_ge))
        link(nc.vector.tensor_reduce(k.id_f[0:1, 0:chunks], ends, AX_X, ALU.add))
        link(nc.vector.tensor_scalar(ids, k.id_f[0:1, 0:chunks], float(buckets - 1), None, ALU.min))

    @block.tensor
    def _(pe):
        pe.wait_ge(counted, 1)
        nc.tensor.matmul(psum[:, 0, 0:buckets], k.before[:], cnt, start=True, stop=True)
        nc.tensor.matmul(psum[:, 1, 0:buckets], k.ones[:], cnt, start=True, stop=True).then_inc(offset, 1)
        if long:
            for b in range(buckets):
                pe.wait_ge(masked, b + 1)
                mm = nc.tensor.matmul(k.pos_psum[:, 0:items], k.ident[:], s[:, b, :],
                                      start=(b == 0), stop=(b == buckets - 1))
            mm.then_inc(offset, 1)


def sort_edges(nc, k, block, by, other, w, rec, pos_i, table_ids, name, loaded):
    key_link, placed = k.sem(name + "_key"), k.sem(name + "_placed")

    def key_ready(dve):
        link = Chain(dve, key_link)
        loaded(dve)
        link(nc.vector.tensor_scalar(k.key_i[:], by[:], 7, None, ALU.arith_shift_right))
        link(nc.vector.tensor_copy(k.bucket[:], k.key_i[:]))
        link(nc.vector.tensor_scalar(k.key_i[:], by[:], P - 1, None, ALU.bitwise_and))
        link(nc.vector.tensor_copy(rec[:, :, 1], k.key_i[:]))
        link(nc.vector.tensor_copy(rec[:, :, 2], w[:]))
        link(nc.vector.tensor_copy(rec[:, :, 3], w[:]))
        link(nc.vector.tensor_scalar(rec[:, :, 0], other[:], float(N - 1), None, ALU.min))

    def finish(link, pos):
        link(nc.vector.tensor_copy(pos_i[:], pos))
        link(nc.vector.tensor_scalar(k.key_i[:], pos_i[:], P - 1, None, ALU.bitwise_and))
        link(nc.vector.tensor_scalar(pos_i[:], pos_i[:], 7, None, ALU.arith_shift_right))
        link(nc.vector.tensor_copy(k.key[:], k.key_i[:]))
        link(nc.vector.tensor_copy(pos, pos_i[:]))
        nc.vector.scalar_tensor_tensor(pos_i[:], k.key[:], float(SLOTS), pos, ALU.mult, ALU.add).then_inc(placed, 1)

    sort_positions(nc, k, block, name, key_ready, k.bucket[:], L, NB, TILES, CHUNKS, table_ids[:], finish)
    return placed


def scatter_edges(nc, k, block, name, pos_i, rec, table, start, groups, placed=None):
    staged = k.sem(name + "_staged")
    laid = [k.sem(f"{name}_laid{half}") for half in range(2)]

    @block.gpsimd
    def _(pool):
        def turns(i, first, halves=2):
            for half in range(halves):
                at = (start + i * 2 + half) * GROUP
                if not first:
                    pool.wait_ge(laid[half], i * (16 * GROUP))
                    pool.nop(nofuse=True)
                nc.gpsimd.tensor_copy(k.index[:, half, :], pos_i[:, bass.ds(at, GROUP)]).then_inc(staged, 1)
                nc.gpsimd.tensor_copy(k.records[:, half, :, :], rec[:, bass.ds(at, GROUP), :]).then_inc(staged, 1)
                pool.wait_ge(staged, (i * 2 + half + 1) * 2)
                pool.nop(nofuse=True)
                for j in range(GROUP):
                    nc.gpsimd.indirect_dma_start(
                        table, bass.IndirectOffsetOnAxis(ap=k.index[:, half, j:j + 1], axis=0),
                        k.records[:, half, j, :], None).then_inc(laid[half], 16)
        if placed is not None:
            pool.wait_ge(placed, 1)
            pool.wait_ge(k.blank_stored, 32)
        turns(0, True)
        if groups >= 4:
            with pool.Fori(1, groups // 2) as i:
                turns(i, False)
        if groups % 2:
            turns(groups // 2, False, 1)
        for half in range(2):
            pool.wait_ge(laid[half], (groups + 1 - half) // 2 * 16 * GROUP)


def load_edges(nc, k, block, a):
    sem = k.sem
    blank, k.edges_in = sem("edge_blank"), sem("edges_in")
    k.blank_stored = sem("blank_stored")

    @block.vector
    def _(dve):
        nc.vector.memset(k.dst[:], TILES * P).then_inc(blank, 1)
        nc.vector.memset(k.src[:], TILES * P).then_inc(blank, 1)
        nc.vector.memset(k.w[:], 0.0).then_inc(blank, 1)
        nc.vector.memset(k.rec_dst[:], 0.0).then_inc(blank, 1)
        dve.wait_ge(blank, 4)
        nc.vector.memset(k.rec_dst[:, :, 1], NO_NODE).then_inc(blank, 1)

    @block.sync
    def _(sp):
        sp.wait_ge(blank, 3)
        for t, d in ((k.dst, a["dst"]), (k.src, a["src"]), (k.w, a["edge_weight"])):
            sp.dma_start(t[0:P - 1, :], d[0:(P - 1) * L].rearrange("(p l) -> p l", l=L)).then_inc(k.edges_in, 16)
            sp.dma_start(t[P - 1:P, 0:LAST_L], d[(P - 1) * L:NE].rearrange("(p l) -> p l", p=1))\
                .then_inc(k.edges_in, 16)
        sp.wait_ge(blank, 5)
        for r in (k.by_dst, k.by_src):
            sp.dma_start(r.rearrange("(p c) f -> p (c f)", p=P), k.rec_dst[:, :, :].rearrange("p c f -> p (c f)"))\
                .then_inc(k.blank_stored, 16)


def load_x(nc, k, block, x, slots):
    blank, x_in, slots_blank = k.sem("x_blank"), k.sem("x_in"), k.sem("slots_blank")

    @block.gpsimd
    def _(pool):
        nc.gpsimd.memset(k.x[:, TILES - 1, :], 0.0).then_inc(blank, 1)
        nc.gpsimd.memset(k.acc[:], 0.0).then_inc(blank, 1)

    @block.sync
    def _(sp):
        sp.wait_ge(blank, 1)
        sp.dma_start(k.x[:, 0:TILES - 1, :], x[0:(TILES - 1) * P, :].rearrange("(t p) f -> p t f", p=P))\
            .then_inc(x_in, 16)
        sp.dma_start(k.x[0:LAST, TILES - 1, :], x[(TILES - 1) * P:N, :]).then_inc(x_in, 16)
        sp.wait_ge(blank, 2)
        parts = range(0, SLOT_TILES, TILES)
        for t in parts:
            n = min(TILES, SLOT_TILES - t)
            sp.dma_start(slots[t * P:(t + n) * P, :].rearrange("(t p) f -> p t f", p=P), k.acc[:, 0:n, 0:D])\
                .then_inc(slots_blank, 16)
        sp.wait_ge(x_in, 32)
        sp.wait_ge(slots_blank, 16 * len(parts))


def load_records(nc, k, block, records, rec, name):
    got = k.sem(name + "_records_in")

    @block.sync
    def _(sp):
        sp.dma_start(rec[:, :, :].rearrange("p c f -> p (c f)"), records.rearrange("(p c) f -> p (c f)", p=P))\
            .then_inc(got, 16)
        sp.wait_ge(got, 16)



def spmm(nc, k, block, name, table, rec, ids, weighted, degree):
    sem = k.sem
    gathered = [sem(f"{name}_gathered{u}") for u in range(RING)]
    hot_ready, summed, added = sem(name + "_hot"), sem(name + "_summed"), sem(name + "_added")
    away, hot1_ready = sem(name + "_away"), sem(name + "_hot1")
    index_at = sem(name + "_index")
    width = D + 1 if degree else D

    @block.scalar
    def _(act):
        def indices(i, part, first):
            at = i * RING + part * GROUP
            if not first:
                act.wait_ge(summed, at + GROUP - RING)
            nc.scalar.activation(k.index[:, part, :], rec[:, bass.ds(at, GROUP), 0], ACT.Copy).then_inc(index_at, 1)

        def one_hots(i, part):
            for j in range(GROUP):
                c = i * RING + part * GROUP + j
                if j >= 2:
                    act.wait_ge(hot1_ready, c - 1)
                nc.scalar.activation(k.away[:, j % 2, :], k.count[:, 0:P], ACT.Abs,
                                     bias=rec[:, bass.ds(c, 1), 1], scale=-1.0).then_inc(away, 1)
                act.wait_ge(away, c + 1)
                nc.scalar.activation(k.hot1[:, part * GROUP + j, :], k.away[:, j % 2, :], ACT.Relu,
                                     bias=1.0, scale=-1.0).then_inc(hot1_ready, 1)

        def round_of(i, first):
            for part in range(PARTS):
                indices(i, part, first)
                if degree:
                    one_hots(i, part)
        round_of(0, True)
        with act.Fori(1, CHUNKS // RING) as i:
            round_of(i, False)

    @block.gpsimd
    def _(pool):
        def round_of(i):
            for part in range(PARTS):
                pool.wait_ge(index_at, i * PARTS + part + 1)
                pool.nop(nofuse=True)
                for j in range(GROUP):
                    u = part * GROUP + j
                    nc.gpsimd.indirect_dma_start(
                        k.rows[:, u, :], None, table,
                        bass.IndirectOffsetOnAxis(ap=k.index[:, part, j:j + 1], axis=0)).then_inc(gathered[u], 16)
        round_of(0)
        with pool.Fori(1, CHUNKS // RING) as i:
            round_of(i)

    @block.vector
    def _(dve):
        def one_hot(c, u):
            local = rec[:, bass.ds(c, 1), 1]
            if weighted:
                hot = nc.vector.scalar_tensor_tensor(k.hot[:, u, :], k.count[:, 0:P], local,
                                                     rec[:, bass.ds(c, 1), 2].to_broadcast([P, P]),
                                                     ALU.is_equal, ALU.mult)
            else:
                hot = nc.vector.tensor_tensor(k.hot[:, u, :], k.count[:, 0:P], local.to_broadcast([P, P]),
                                              ALU.is_equal)
            hot.then_inc(hot_ready, 1)

        def add(c, u, tile, first):
            dve.wait_ge(summed, c + 1)
            if not first:
                dve.wait_ge(added, c)
            into = k.acc[:, bass.ds(tile, 1), 0:width].rearrange("p a f -> p (a f)")
            nc.vector.tensor_tensor(into, into, k.sum_psum[:, u % BANKS, 0:width], ALU.add).then_inc(added, 1)

        def part_of(at, part, first=False, last=False):
            tiles = nc.values_load_multi_w_load_instructions(
                ids[0:1, bass.ds(at, GROUP)], engines=[mybir.EngineType.DVE], min_val=0, max_val=TILES)[1]
            for j in range(GROUP):
                u = part * GROUP + j
                if not last:
                    one_hot(at + GROUP + j, (u + GROUP) % RING)
                add(at + j, u, tiles[j], first and j == 0)

        for j in range(GROUP):
            one_hot(j, j)
        part_of(0, 0, first=True)
        with dve.Fori(0, CHUNKS // RING - 1) as i:
            for part in range(1, PARTS + 1):
                part_of(i * RING + part * GROUP, part % PARTS)
        for part in range(1, PARTS):
            part_of(CHUNKS + (part - PARTS) * GROUP, part, last=part == PARTS - 1)

    @block.tensor
    def _(pe):
        def step(c, u, i, first):
            pe.wait_ge(gathered[u], (i + 1) * 16)
            pe.wait_ge(hot_ready, c + 1)
            if not first or u >= BANKS:
                pe.wait_ge(added, c - BANKS + 1)
            mm = nc.tensor.matmul(k.sum_psum[:, u % BANKS, 0:D], k.hot[:, u, :], k.rows[:, u, :],
                                  start=True, stop=True)
            if degree:
                pe.wait_ge(hot1_ready, c + 1)
                mm = nc.tensor.matmul(k.sum_psum[:, u % BANKS, D:D + 1], k.hot1[:, u, :], k.one_col[:],
                                      start=True, stop=True)
            mm.then_inc(summed, 1)
        over(pe, CHUNKS, RING, step)



def ln_stats(nc, k, dve, link, src, done=None, unit=False, counted=False):
    st, w = k.stats, k.ln_work
    mean, var, t, r, a = (w[:, j, :] for j in range(5))
    if not counted:
        with dve.Fori(0, TILES // 5) as i:
            for u in range(5):
                tile = src[:, bass.ds(i * 5 + u, 1), 0:D].rearrange("p a f -> p (a f)")
                nc.vector.bn_stats(st[:, bass.ds(i * 5 + u, 1), :].rearrange("p a f -> p (a f)"), tile)
    nc.vector.memset(a, 0.0).then_inc(link.sem, 1)
    link.n += 1
    dve.wait_ge(link.sem, link.n)
    link(nc.vector.tensor_tensor(mean, st[:, :, 1], st[:, :, 4], ALU.add))
    link(nc.vector.tensor_tensor(a, st[:, :, 1], st[:, :, 4], ALU.subtract))
    link(nc.vector.tensor_tensor(var, st[:, :, 2], st[:, :, 5], ALU.add))
    link(nc.vector.tensor_scalar(mean, mean, 0.5, None, ALU.mult))
    link(nc.vector.tensor_tensor(a, a, a, ALU.mult))
    link(nc.vector.tensor_scalar(a, a, 0.25, None, ALU.mult))
    link(nc.vector.scalar_tensor_tensor(var, var, 1.0 / D, a, ALU.mult, ALU.add))
    link(nc.vector.tensor_scalar(t, var, LN_EPS, None, ALU.add))
    inverse_root(nc, k, dve, link, t, k.ln_scale[:, :])
    if unit:
        link(nc.vector.tensor_scalar(t, var, float(D), None, ALU.mult))
        link(nc.vector.tensor_tensor(t, t, k.ln_scale[:, :], ALU.mult))
        link(nc.vector.tensor_tensor(t, t, k.ln_scale[:, :], ALU.mult))
        link(nc.vector.tensor_scalar(t, t, 1e-24, None, ALU.max))
        inverse_root(nc, k, dve, link, t, r)
        link(nc.vector.tensor_tensor(k.ln_scale[:, :], k.ln_scale[:, :], r, ALU.mult))
    ins = nc.vector.scalar_tensor_tensor(k.ln_shift[:, :], mean, -1.0, k.ln_scale[:, :], ALU.mult, ALU.mult)
    if done is not None:
        ins.then_inc(done, 1)
    else:
        link(ins)


def inverse_root(nc, k, dve, link, t, out):
    a = k.ln_work[:, 5, :]
    link(nc.vector.tensor_copy(k.root_in[:, :], t))
    k.roots += 1
    nc.vector.tensor_copy(a, k.root_in[:, :]).then_inc(k.root_asked, 1)
    dve.wait_ge(k.root_done, k.roots)
    link(nc.vector.reciprocal(out, k.root_out[:, :]))
    link(nc.vector.tensor_tensor(a, out, out, ALU.mult))
    link(nc.vector.tensor_tensor(a, a, k.root_in[:, :], ALU.mult))
    link(nc.vector.tensor_scalar(a, a, -0.5, 1.5, ALU.mult, ALU.add))
    link(nc.vector.tensor_tensor(out, out, a, ALU.mult))


def serve_root(nc, k, act, count=1):
    for _ in range(count):
        k.served += 1
        act.wait_ge(k.root_asked, k.served)
        nc.scalar.activation(k.root_out[:, :], k.root_in[:, :], ACT.Sqrt).then_inc(k.root_done, 1)



def project(nc, k, block, name, weight, table, *, norm_src=None, unit=False, plain_src=None,
            affine=None, row_scale=None, second=None, self_loop=False, counted=False, loads=()):
    sem = k.sem
    stat_done, link_sem = sem(name + "_stats"), sem(name + "_link")
    prepared, turned, turned_sb = sem(name + "_prepared"), sem(name + "_turned"), sem(name + "_turned_sb")
    projected, evacuated = sem(name + "_projected"), sem(name + "_evacuated")
    w_in, stored = sem(name + "_w_in"), sem(name + "_stored")
    src = norm_src if norm_src is not None else plain_src
    n_loads = len(loads)
    x_part = sem(name + "_x_part")

    @block.sync
    def _(sp):
        for held, given in loads:
            sp.dma_start(held, given).then_inc(w_in, 16)

        def store(c, u, i, first):
            sp.wait_ge(evacuated, c + 1)
            sp.dma_start(table[bass.ds(c * P, P), :], k.y[:, bass.ds(c, 1), :].rearrange("p a f -> p (a f)"))\
                .then_inc(stored, 16)
        over(sp, TILES, 2, store)
        sp.wait_ge(stored, 16 * TILES)

    @block.scalar
    def _(act):
        if norm_src is not None:
            serve_root(nc, k, act, 2 if unit else 1)
            act.wait_ge(stat_done, 1)

        def step(c, u, i, first):
            if not first:
                act.wait_ge(turned, c - 1)
            tile = src[:, bass.ds(c, 1), 0:D].rearrange("p a f -> p (a f)")
            if norm_src is not None:
                ins = nc.scalar.activation(k.ybuf[:, u, :], tile, ACT.Identity, bias=one(k.ln_shift, c),
                                           scale=one(k.ln_scale, c))
            else:
                ins = nc.scalar.activation(k.ybuf[:, u, :], tile, ACT.Copy)
            ins.then_inc(prepared, 1)
            if affine and not (first and u == 0):
                refine(c - 1, 1 - u)

        def refine(c, u):
            act.wait_ge(turned, c + 1)
            if not isinstance(c, int) or c >= 2:
                act.wait_ge(projected, c - 1)
            for b in range(KD):
                ins = nc.scalar.activation(k.yt[:, u, b * P:(b + 1) * P], k.turn_psum[:, u, b * P:(b + 1) * P],
                                           ACT.Relu, bias=affine[1][:, b:b + 1], scale=affine[0][:, b:b + 1])
            ins.then_inc(turned_sb, 1)
        if affine:
            act.wait_ge(w_in, 16 * n_loads)
        over(act, TILES, 2, step, peeled=2 if affine else 1)
        if affine:
            refine(TILES - 1, (TILES - 1) % 2)

    @block.tensor
    def _(pe):
        if n_loads:
            pe.wait_ge(w_in, 16 * n_loads)

        def turn(c, u, first):
            pe.wait_ge(prepared, c + 1)
            if not first:
                pe.wait_ge(turned_sb, c - 1)
            for b in range(KD):
                mm = nc.tensor.transpose(k.turn_psum[:, u, b * P:(b + 1) * P], k.ybuf[:, u, b * P:(b + 1) * P],
                                         k.ident[:])
            mm.then_inc(turned, 1)

        def step(c, u, i, first):
            if not (isinstance(c, int) and c == TILES - 1):
                turn(c + 1, 1 - u, first and u == 0)
            pe.wait_ge(turned_sb, c + 1)
            if not first:
                pe.wait_ge(evacuated, c - 1)
            for b in range(KD):
                mm = nc.tensor.matmul(k.out_psum[:, u, 0:D], k.yt[:, u, b * P:(b + 1) * P], weight[:, b, :],
                                      start=(b == 0), stop=(b == KD - 1))
            if second:
                for b in range(KD):
                    mm = nc.tensor.matmul(k.out2_psum[:, u, 0:D], k.yt[:, u, b * P:(b + 1) * P], second[0][:, b, :],
                                          start=(b == 0), stop=(b == KD - 1))
            mm.then_inc(projected, 1)
        turn(0, 0, True)
        over(pe, TILES, 2, step, last_apart=True)

    @block.vector
    def _(dve):
        link = Chain(dve, link_sem)
        if norm_src is not None:
            ln_stats(nc, k, dve, link, norm_src, done=stat_done, unit=unit, counted=counted)
        if second:
            dve.wait_ge(w_in, 16 * n_loads)
        if second:
            link(nc.vector.tensor_tensor(second[1], second[1], second[2], ALU.add))

        def ahead(c, u):
            dve.wait_ge(turned, c + 1)
            if not isinstance(c, int) or c >= 2:
                dve.wait_ge(projected, c - 1)
            nc.vector.tensor_copy(k.yt[:, u, :], k.turn_psum[:, u, 0:D]).then_inc(turned_sb, 1)

        def step(c, u, i, first):
            if not affine and not (isinstance(c, int) and c == TILES - 1):
                ahead(c + 1, 1 - u)
            dve.wait_ge(projected, c + 1)
            if second:
                xt = k.x[:, bass.ds(c, 1), :].rearrange("p a f -> p (a f)")
                nc.vector.tensor_tensor(xt, xt, k.out2_psum[:, u, 0:D], ALU.add).then_inc(x_part, 1)
                dve.wait_ge(x_part, c + 1)
                nc.vector.tensor_tensor(xt, xt, second[1], ALU.add)
            out = k.y[:, bass.ds(c, 1), :].rearrange("p a f -> p (a f)")
            nc.vector.tensor_scalar(out, k.out_psum[:, u, 0:D],
                                    one(row_scale, c) if row_scale is not None else 1.0, None, ALU.mult)\
                .then_inc(evacuated, 1)
        if not affine:
            ahead(0, 0)
        over(dve, TILES, 2, step, last_apart=True)

    @block.gpsimd
    def _(pool):
        if self_loop:
            own_rows = sem(name + "_own")
            nc.gpsimd.memset(k.acc[:, TILES, :], 0.0).then_inc(own_rows, 1)

            def copy(c, u, i, first):
                pool.wait_ge(evacuated, c + 1)
                pool.nop(nofuse=True)
                nc.gpsimd.tensor_copy(k.acc[:, bass.ds(c, 1), 0:D].rearrange("p a f -> p (a f)"),
                                      k.y[:, bass.ds(c, 1), :].rearrange("p a f -> p (a f)")).then_inc(own_rows, 1)
            over(pool, TILES, 2, copy)
            pool.wait_ge(own_rows, TILES + 1)
        else:
            cleared = sem(name + "_cleared")
            nc.gpsimd.memset(k.acc[:], 0.0).then_inc(cleared, 1)
            pool.wait_ge(cleared, 1)



def wide(row):
    return row.unsqueeze(1).to_broadcast([P, TILES, D])


def narrow(col):
    return col.unsqueeze(2).to_broadcast([P, TILES, D])


def degrees(nc, k):
    done = k.sem("degree_link")
    with nc.Block() as block:
        @block.vector
        def _(dve):
            link = Chain(dve, done)
            t, has = k.ln_work[:, 0, :], k.ln_work[:, 1, :]
            link(nc.vector.tensor_copy(k.degree[:], k.acc[:, 0:TILES, D]))
            link(nc.vector.tensor_scalar(t, k.degree[:], 1.0, None, ALU.add))
            inverse_root(nc, k, dve, link, t, k.dinv_loop[:])
            link(nc.vector.tensor_scalar(t, k.degree[:], 1.0, None, ALU.max))
            inverse_root(nc, k, dve, link, t, k.dinv[:])
            link(nc.vector.tensor_scalar(has, k.degree[:], 0.0, None, ALU.is_gt))
            link(nc.vector.tensor_tensor(k.dinv[:], k.dinv[:], has, ALU.mult))

        @block.scalar
        def _(act):
            serve_root(nc, k, act, 2)


def relu_bias(nc, k, name, vec):
    got, linked = k.sem(name + "_in"), k.sem(name + "_link")
    with nc.sbuf_tensor(name + "_row", [P, D], F32) as row, nc.Block() as block:
        @block.sync
        def _(sp):
            sp.dma_start(row[:], spread(vec)).then_inc(got, 16)

        @block.vector
        def _(dve):
            link = Chain(dve, linked)
            dve.wait_ge(got, 16)
            link(nc.vector.tensor_tensor(k.y[:], k.acc[:, 0:TILES, 0:D], wide(row[:]), ALU.add))
            link(nc.vector.tensor_scalar(k.y[:], k.y[:], 0.0, None, ALU.max))


def add_elu(nc, k, name, vec):
    got, linked, shifted, raised = (k.sem(name + s) for s in ("_in", "_link", "_shifted", "_exp"))
    spans = [slice(t, min(t + 9, TILES)) for t in range(0, TILES, 9)]
    acc = k.acc[:, :, 0:D]
    with nc.sbuf_tensor(name + "_row", [P, D], F32) as row, nc.Block() as block:
        @block.sync
        def _(sp):
            sp.dma_start(row[:], spread(vec)).then_inc(got, 16)

        @block.vector
        def _(dve):
            dve.wait_ge(got, 16)
            for part in spans:
                n = part.stop - part.start
                nc.vector.tensor_tensor(acc[:, part, :], acc[:, part, :],
                                        row[:].unsqueeze(1).to_broadcast([P, n, D]), ALU.add).then_inc(shifted, 1)
            for j, part in enumerate(spans):
                dve.wait_ge(shifted, j + 1)
                nc.vector.scalar_tensor_tensor(k.x[:, part, :], acc[:, part, :], 0.0, k.x[:, part, :],
                                               ALU.max, ALU.add).then_inc(linked, 1)
            for j, part in enumerate(spans):
                dve.wait_ge(linked, j + 1)
                dve.wait_ge(raised, 2 * (j + 1))
                nc.vector.scalar_tensor_tensor(k.x[:, part, :], k.y[:, part, :], 0.0, k.x[:, part, :],
                                               ALU.min, ALU.add).then_inc(linked, 1)

        @block.scalar
        def _(act):
            for j, part in enumerate(spans):
                act.wait_ge(shifted, j + 1)
                nc.scalar.activation(k.y[:, part, :], acc[:, part, :], ACT.Exp).then_inc(raised, 1)
                act.wait_ge(raised, 2 * j + 1)
                nc.scalar.activation(k.y[:, part, :], k.y[:, part, :], ACT.Copy, bias=-1.0).then_inc(raised, 1)


def add_acc(nc, k, name, scale, to_x):
    linked = k.sem(name + "_link")
    acc = k.acc[:, 0:TILES, 0:D]
    with nc.Block() as block:
        @block.vector
        def _(dve):
            link = Chain(dve, linked)
            if not to_x:
                link(nc.vector.tensor_tensor(k.y[:], acc, narrow(scale[:]), ALU.mult))
            elif scale is None:
                link(nc.vector.tensor_tensor(k.x[:], k.x[:], acc, ALU.add))
            else:
                def step(c, u, i, first):
                    to = k.x[:, bass.ds(c, 1), :].rearrange("p a f -> p (a f)")
                    nc.vector.scalar_tensor_tensor(to, k.acc[:, bass.ds(c, 1), 0:D].rearrange("p a f -> p (a f)"),
                                                   one(scale, c), to, ALU.mult, ALU.add)
                over(dve, TILES, 5, step)


def add_norm(nc, k, name, gamma, beta, counted=False, out=None):
    got, linked, scaled = k.sem(name + "_in"), k.sem(name + "_link"), k.sem(name + "_scaled")
    stat_done, prepared, shifted = k.sem(name + "_stats"), k.sem(name + "_prepared"), k.sem(name + "_shifted")
    finished, stored = k.sem(name + "_finished"), k.sem(name + "_stored")
    BUFFERS, SPAN = 4, 5
    with nc.sbuf_tensor(name + "_rows", [P, 2, D], F32) as row, \
            nc.sbuf_tensor(name + "_normed", [P, BUFFERS, D], F32) as normed, nc.Block() as block:
        @block.sync
        def _(sp):
            sp.dma_start(row[:, 0, :], spread(gamma)).then_inc(got, 16)
            sp.dma_start(row[:, 1, :], spread(beta)).then_inc(got, 16)
            if out is not None:
                for t in range(0, TILES, SPAN):
                    n = min(SPAN, TILES - 1 - t)
                    sp.wait_ge(finished, t + n)
                    sp.dma_start(out[t * P:(t + n) * P, :].rearrange("(t p) f -> p t f", p=P), k.x[:, t:t + n, :])\
                        .then_inc(stored, 16)
                sp.wait_ge(finished, TILES)
                sp.dma_start(out[(TILES - 1) * P:N, :], k.x[0:LAST, TILES - 1, :]).then_inc(stored, 16)
                sp.wait_ge(stored, 16 * (len(range(0, TILES, SPAN)) + 1))

        @block.scalar
        def _(act):
            serve_root(nc, k, act)
            act.wait_ge(stat_done, 1)

            def step(c, u, i, first):
                if not first:
                    act.wait_ge(finished, c - BUFFERS + 1)
                nc.scalar.activation(normed[:, u, :], k.y[:, bass.ds(c, 1), :].rearrange("p a f -> p (a f)"),
                                     ACT.Identity, bias=one(k.ln_shift, c), scale=one(k.ln_scale, c))\
                    .then_inc(prepared, 1)
            over(act, TILES, BUFFERS, step)

        @block.gpsimd
        def _(pool):
            pool.wait_ge(got, 32)
            nc.gpsimd.tensor_tensor(k.x[:], k.x[:], wide(row[:, 1, :]), ALU.add).then_inc(shifted, 1)

        @block.vector
        def _(dve):
            link = Chain(dve, linked)
            ln_stats(nc, k, dve, link, k.y, done=stat_done, counted=counted)
            dve.wait_ge(got, 32)

            def scale(c, u):
                dve.wait_ge(prepared, c + 1)
                nc.vector.tensor_tensor(normed[:, u, :], normed[:, u, :], row[:, 0, :], ALU.mult).then_inc(scaled, 1)

            def step(c, u, i, first):
                if not (isinstance(c, int) and c == TILES - 1):
                    scale(c + 1, (u + 1) % BUFFERS)
                dve.wait_ge(scaled, c + 1)
                to = k.x[:, bass.ds(c, 1), :].rearrange("p a f -> p (a f)")
                nc.vector.tensor_tensor(to, to, normed[:, u, :], ALU.add).then_inc(finished, 1)
            scale(0, 0)
            dve.wait_ge(shifted, 1)
            over(dve, TILES, BUFFERS, step, last_apart=True)



def gru(nc, k, block, scope, layers):
    def sb(n, shape):
        return scope.enter_context(nc.sbuf_tensor("gru" + n, shape, F32))
    GB = 3 * D // P
    k.gru_h = sb("_h", [P, KD, D])
    k.gru_w = [sb("_wi", [P, GB, D]), sb("_wh", [P, GB, D])]
    k.gru_b = sb("_b", [P, 2, 3 * D])
    k.gru_ht = sb("_ht", [P, KD, D])
    k.gru_wt = [sb("_wit", [P, KD, 3 * D]), sb("_wht", [P, KD, 3 * D])]
    k.gru_rznt = [sb(f"_{x}", [P, KD, D]) for x in "rznt"]
    k.gru_turned = scope.enter_context(nc.psum_tensor("gru_tp", [P, 2, 512], F32))
    k.gru_gates = scope.enter_context(nc.psum_tensor("gru_gates", [P, 2, 512], F32))
    before = None
    for layer in layers:
        before = gru_layer(nc, k, block, before, *layer)


def gru_layer(nc, k, block, before, name, iw, wih, whh, bih, bhh, weight):
    G = 3 * D
    GB = G // P
    sem = k.sem
    got, turned, copied, linked = (sem(name + s) for s in ("_in", "_turned", "_copied", "_link"))
    mul, read, act_done, finished = sem(name + "_mul"), sem(name + "_read"), sem(name + "_act"), sem(name + "_done")
    h, ws, b, ht, wt, tp, gates = k.gru_h, k.gru_w, k.gru_b, k.gru_ht, k.gru_wt, k.gru_turned, k.gru_gates
    r, z, n, t = k.gru_rznt
    turns = [(h[:, rb, cb * P:(cb + 1) * P], ht[:, cb, rb * P:(rb + 1) * P]) for cb in range(KD) for rb in range(KD)]
    for w, o in zip(ws, wt):
        turns += [(w[:, rb, cb * P:(cb + 1) * P], o[:, cb, rb * P:(rb + 1) * P])
                  for cb in range(KD) for rb in range(GB)]
    @block.sync
    def _(sp):
        if before is not None:
            sp.wait_ge(before, 1)
        sp.dma_start(h[:], rows_of(iw, KD)).then_inc(got, 16)
        sp.dma_start(ws[0][:], rows_of(wih, GB)).then_inc(got, 16)
        sp.dma_start(ws[1][:], rows_of(whh, GB)).then_inc(got, 16)
        sp.dma_start(b[:, 0, :], spread(bih)).then_inc(got, 16)
        sp.dma_start(b[:, 1, :], spread(bhh)).then_inc(got, 16)

    @block.tensor
    def _(pe):
        pe.wait_ge(got, 80)
        for j, (s, _) in enumerate(turns):
            if j >= 2:
                pe.wait_ge(copied, j - 1)
            nc.tensor.transpose(tp[:, j % 2, 0:P], s, k.ident[:]).then_inc(turned, 1)
        pe.wait_ge(copied, len(turns))
        for rb in range(KD):
            if rb:
                pe.wait_ge(read, rb)
            own = [ht[:, cb, rb * P:(rb + 1) * P] for cb in range(KD)]
            for j in range(2 * KD):
                nc.tensor.matmul(gates[:, 0, :], own[j % KD], wt[j // KD][:, j % KD, 0:2 * D],
                                 start=(j == 0), stop=(j == 2 * KD - 1))
            for part in range(2):
                for cb in range(KD):
                    mm = nc.tensor.matmul(gates[:, 1, part * D:(part + 1) * D], own[cb],
                                          wt[part][:, cb, 2 * D:G], start=(cb == 0), stop=(cb == KD - 1))
            mm.then_inc(mul, 1)

    @block.vector
    def _(dve):
        link = Chain(dve, linked)
        for j, (_, o) in enumerate(turns):
            dve.wait_ge(turned, j + 1)
            nc.vector.tensor_copy(o, tp[:, j % 2, 0:P]).then_inc(copied, 1)
        link(nc.vector.tensor_tensor(b[:, 0, 0:2 * D], b[:, 0, 0:2 * D], b[:, 1, 0:2 * D], ALU.add))
        for rb in range(KD):
            dve.wait_ge(mul, rb + 1)
            link(nc.vector.tensor_tensor(r[:, rb, :], gates[:, 0, 0:D], b[:, 0, 0:D], ALU.add))
            link(nc.vector.tensor_tensor(z[:, rb, :], gates[:, 0, D:2 * D], b[:, 0, D:2 * D], ALU.add))
            link(nc.vector.tensor_tensor(n[:, rb, :], gates[:, 1, 0:D], b[:, 0, 2 * D:G], ALU.add))
            nc.vector.tensor_tensor(t[:, rb, :], gates[:, 1, D:2 * D], b[:, 1, 2 * D:G], ALU.add)\
                .then_inc(read, 1)
            dve.wait_ge(read, rb + 1)
        nc.vector.tensor_copy(weight, t[:]).then_inc(act_done, 1)
        dve.wait_ge(act_done, 3)
        link(nc.vector.tensor_tensor(t[:], r[:], t[:], ALU.mult))
        link(nc.vector.tensor_tensor(n[:], n[:], t[:], ALU.add))
        nc.vector.tensor_copy(weight, n[:]).then_inc(act_done, 1)
        dve.wait_ge(act_done, 5)
        link(nc.vector.tensor_scalar(t[:], z[:], -1.0, 1.0, ALU.mult, ALU.add))
        link(nc.vector.tensor_tensor(n[:], n[:], t[:], ALU.mult))
        link(nc.vector.tensor_tensor(z[:], z[:], h[:], ALU.mult))
        nc.vector.tensor_tensor(weight, n[:], z[:], ALU.add).then_inc(finished, 1)
        dve.wait_ge(finished, 1)

    @block.scalar
    def _(act):
        act.wait_ge(act_done, 1)
        nc.scalar.activation(r[:], r[:], ACT.Sigmoid).then_inc(act_done, 1)
        nc.scalar.activation(z[:], z[:], ACT.Sigmoid).then_inc(act_done, 1)
        act.wait_ge(act_done, 4)
        nc.scalar.activation(n[:], n[:], ACT.Tanh).then_inc(act_done, 1)
    return finished



class Experts:

    def __init__(self, name, experts, top, hidden):
        self.name, self.E, self.K, self.F = name, experts, top, hidden
        self.items = TILES * top
        self.FP = min(P, hidden)
        self.FB = hidden // self.FP
        self.tiles = (TILES * P * top + experts * (P - 1)) // P


def keep_even(nc, k, pool, ybuf, prepared, kept):
    def step(j, u, i, first):
        pool.wait_ge(prepared, 2 * j + 1)
        nc.gpsimd.tensor_copy(k.y[:, bass.ds(2 * j, 1), :].rearrange("p a f -> p (a f)"), ybuf[:, 0, :])\
            .then_inc(kept, 1)
    over(pool, TILES - TILES // 2, 1, step)


def keep_odd(nc, k, dve, c, ybuf, prepared, kept):
    dve.wait_ge(prepared, c + 1)
    nc.vector.tensor_scalar(k.y[:, bass.ds(c, 1), :].rearrange("p a f -> p (a f)"), ybuf[:, 1, :], 1.0, None,
                            ALU.mult).then_inc(kept, 1)


def route(nc, k, m, router, router_by_expert, bias, mode, slots):
    sem, E, K = k.sem, m.E, m.K
    s = {n: sem(f"{m.name}_{n}") for n in ("in", "stats", "link", "prepared", "turned", "turned_sb",
                                           "scored", "biased", "rt_turned", "rt", "exp_asked", "exp_done",
                                           "keyed", "slots", "laid")}
    kept = [sem(f"{m.name}_kept{u}") for u in range(2)]
    with ExitStack() as scope:
        def sb(n, shape, dt=F32):
            return scope.enter_context(nc.sbuf_tensor(f"{m.name}_{n}", shape, dt))

        def bank(n, shape):
            return scope.enter_context(nc.psum_tensor(f"{m.name}_{n}", shape, F32))
        ybuf, yt = sb("ybuf", [P, 2, D]), sb("yt", [P, 2, D])
        rt = sb("rt", [P, KD, E])
        given = sb("router", [E, D]) if router_by_expert else None
        bias_row = sb("bias", [P, E]) if bias is not None else None
        logits, best, which = sb("logits", [P, TILES, E]), sb("best", [P, TILES, 8]), sb("which", [P, TILES, 8], U32)
        probs, t1, t2 = sb("probs", [P, TILES, E + 8]), sb("t1", [P, TILES]), sb("t2", [P, TILES])
        k.member, k.running = sb("member", [P, E * m.items], BF16), sb("running", [P, max(E * m.items, m.tiles * E)])
        k.pos, k.key = sb("pos", [P, m.items]), sb("key", [P, m.items])
        k.small, k.small_i, k.id_f = sb("small", [P, 5, 32]), sb("small_i", [P, 32], I32), sb("id_f", [1, m.tiles])
        turn_psum, out_psum = bank("turn_psum", [P, 2, 512]), bank("out_psum", [P, 2, 512])
        k.sort_psum, rt_psum = bank("sort_psum", [P, 2, 64]), bank("rt_psum", [P, KD, 64])
        n_in = 1 + (bias is not None)
        choice = k.choice[:, 0:m.items].rearrange("p (t c) -> p t c", c=K)

        def finish(link, pos):
            nc.vector.tensor_copy(k.slot_i[:, 0:m.items], pos).then_inc(s["slots"], 1)

        def key_ready(dve):
            dve.wait_ge(s["keyed"], 1)

        with nc.Block() as block:
            @block.sync
            def _(sp):
                if router_by_expert:
                    sp.dma_start(given[:], router).then_inc(s["in"], 16)
                else:
                    sp.dma_start(rt[:], rows_of(router, KD)).then_inc(s["in"], 16)
                if bias is not None:
                    sp.dma_start(bias_row[:], spread(bias)).then_inc(s["in"], 16)

            @block.scalar
            def _(act):
                serve_root(nc, k, act)
                act.wait_ge(s["stats"], 1)

                def step(c, u, i, first):
                    if not first:
                        act.wait_ge(s["turned"], c - 1)
                        act.wait_ge(kept[u], i)
                    nc.scalar.activation(ybuf[:, u, :], k.x[:, bass.ds(c, 1), :].rearrange("p a f -> p (a f)"),
                                         ACT.Identity, bias=one(k.ln_shift, c), scale=one(k.ln_scale, c))\
                        .then_inc(s["prepared"], 1)
                over(act, TILES, 2, step)
                if mode != "none":
                    act.wait_ge(s["exp_asked"], 1)
                    used = probs[:, :, 0:E + K if mode == "softmax_all" else K]
                    nc.scalar.activation(used, used, ACT.Exp).then_inc(s["exp_done"], 1)

            @block.gpsimd
            def _(pool):
                keep_even(nc, k, pool, ybuf, s["prepared"], kept[0])

            @block.tensor
            def _(pe):
                pe.wait_ge(s["in"], 16 * n_in)
                if router_by_expert:
                    for b in range(KD):
                        mm = nc.tensor.transpose(rt_psum[:, b, 0:E], given[:, b * P:(b + 1) * P], k.ident[0:E, 0:E])
                    mm.then_inc(s["rt_turned"], 1)
                    pe.wait_ge(s["rt"], 1)

                def turn(c, u, first):
                    pe.wait_ge(s["prepared"], c + 1)
                    if not first:
                        pe.wait_ge(s["turned_sb"], c - 1)
                    for b in range(KD):
                        mm = nc.tensor.transpose(turn_psum[:, u, b * P:(b + 1) * P], ybuf[:, u, b * P:(b + 1) * P],
                                                 k.ident[:])
                    mm.then_inc(s["turned"], 1)

                def step(c, u, i, first):
                    if not (isinstance(c, int) and c == TILES - 1):
                        turn(c + 1, 1 - u, first and u == 0)
                    pe.wait_ge(s["turned_sb"], c + 1)
                    if not first:
                        pe.wait_ge(s["biased"], c - 1)
                    for b in range(KD):
                        mm = nc.tensor.matmul(out_psum[:, u, 0:E], yt[:, u, b * P:(b + 1) * P], rt[:, b, :],
                                              start=(b == 0), stop=(b == KD - 1))
                    mm.then_inc(s["scored"], 1)
                turn(0, 0, True)
                over(pe, TILES, 2, step, last_apart=True)

            @block.vector
            def _(dve):
                link = Chain(dve, s["link"])
                if router_by_expert:
                    dve.wait_ge(s["rt_turned"], 1)
                    nc.vector.tensor_copy(rt[:], rt_psum[:, :, 0:E]).then_inc(s["rt"], 1)
                ln_stats(nc, k, dve, link, k.x, done=s["stats"])
                if bias is not None:
                    dve.wait_ge(s["in"], 16 * n_in)

                def ahead(c, u):
                    dve.wait_ge(s["turned"], c + 1)
                    if not isinstance(c, int) or c >= 2:
                        dve.wait_ge(s["scored"], c - 1)
                    nc.vector.tensor_copy(yt[:, u, :], turn_psum[:, u, 0:D]).then_inc(s["turned_sb"], 1)
                    if u:
                        keep_odd(nc, k, dve, c, ybuf, s["prepared"], kept[1])

                def step(c, u, i, first):
                    if not (isinstance(c, int) and c == TILES - 1):
                        ahead(c + 1, 1 - u)
                    dve.wait_ge(s["scored"], c + 1)
                    lg = logits[:, bass.ds(c, 1), :].rearrange("p a e -> p (a e)")
                    if bias is None:
                        nc.vector.tensor_scalar(lg, out_psum[:, u, 0:E], 0.0, None, ALU.add).then_inc(s["biased"], 1)
                    else:
                        nc.vector.tensor_tensor(lg, out_psum[:, u, 0:E], bias_row[:], ALU.add).then_inc(s["biased"], 1)
                ahead(0, 0)
                over(dve, TILES, 2, step, last_apart=True)
                dve.wait_ge(s["biased"], TILES)
                for c in range(TILES):
                    ins = nc.vector.max(best[:, c, :], logits[:, c, :])
                link(ins)
                for c in range(TILES):
                    ins = nc.vector.max_index(which[:, c, :], best[:, c, :], logits[:, c, :])
                link(ins)
                link(nc.vector.tensor_copy(k.key[:, :].rearrange("p (t c) -> p t c", c=K), which[:, :, 0:K]))
                if mode == "softmax_all":
                    link(nc.vector.tensor_tensor(probs[:, :, 0:E], logits[:],
                                                 best[:, :, 0:1].to_broadcast([P, TILES, E]),
                                                 ALU.subtract))
                    nc.vector.tensor_tensor(probs[:, :, E:E + K], best[:, :, 0:K],
                                            best[:, :, 0:1].to_broadcast([P, TILES, K]), ALU.subtract)\
                        .then_inc(s["exp_asked"], 1)
                    dve.wait_ge(s["exp_done"], 1)
                    link(nc.vector.tensor_reduce(t1[:], probs[:, :, 0:E], AX_X, ALU.add))
                    link(nc.vector.reciprocal(t1[:], t1[:]))
                    link(nc.vector.tensor_tensor(probs[:, :, E:E + K], probs[:, :, E:E + K],
                                                 t1[:].unsqueeze(2).to_broadcast([P, TILES, K]), ALU.mult))
                    link(nc.vector.tensor_tensor(t1[:], probs[:, :, E], probs[:, :, E + 1], ALU.add))
                    link(nc.vector.tensor_scalar(t1[:], t1[:], 1e-12, None, ALU.max))
                    link(nc.vector.reciprocal(t1[:], t1[:]))
                    link(nc.vector.tensor_tensor(choice, probs[:, :, E:E + K],
                                                 t1[:].unsqueeze(2).to_broadcast([P, TILES, K]), ALU.mult))
                elif mode == "softmax_top":
                    link(nc.vector.tensor_tensor(probs[:, :, 0:K], best[:, :, 0:K],
                                                 best[:, :, 0:1].to_broadcast([P, TILES, K]), ALU.subtract))
                    nc.vector.memset(t2[:], 0.0).then_inc(s["exp_asked"], 1)
                    dve.wait_ge(s["exp_done"], 1)
                    link(nc.vector.tensor_reduce(t1[:], probs[:, :, 0:K], AX_X, ALU.add))
                    link(nc.vector.reciprocal(t1[:], t1[:]))
                    link(nc.vector.tensor_tensor(choice, probs[:, :, 0:K],
                                                 t1[:].unsqueeze(2).to_broadcast([P, TILES, K]), ALU.mult))
                nc.vector.memset(t2[:], 0.0).then_inc(s["keyed"], 1)
            sort_positions(nc, k, block, m.name + "_sort", key_ready, k.key[:], m.items, E, E, m.tiles,
                           k.slot_expert[0:1, 0:m.tiles], finish)

            @block.gpsimd
            def _(pool):
                pool.wait_ge(s["slots"], 1)
                pool.wait_ge(kept[0], TILES - TILES // 2)
                pool.wait_ge(kept[1], TILES // 2)
                for j in range(m.items):
                    nc.gpsimd.indirect_dma_start(slots, bass.IndirectOffsetOnAxis(ap=k.slot_i[:, j:j + 1], axis=0),
                                                 k.y[:, j // K, :], None).then_inc(s["laid"], 16)
                pool.wait_ge(s["laid"], 16 * m.items)


def run_experts(nc, k, m, func, w1, b1, w2, b2, relu_out, slots, results, meanwhile):
    sem, F, FP, FB, E, n = k.sem, m.F, m.FP, m.FB, m.E, m.tiles
    s = {n: sem(f"{m.name}_x_{n}") for n in ("turned", "turned_sb", "up", "hidden", "down", "out", "b1_in",
                                             "b1_turned", "b1", "sum")}
    W = 2 * DEEP if F <= 256 else DEEP
    all_w2 = FP == P and E * FB <= 16
    per_tile = 16 if all_w2 else 32
    w2_in = sem(f"{m.name}_x_w2_in")
    loaded = [sem(f"{m.name}_x_loaded{u}") for u in range(W)]
    rows_in = [sem(f"{m.name}_x_rows_in{u}") for u in range(2)]
    stored = [sem(f"{m.name}_x_stored{u}") for u in range(2)]
    b2_in = sem(f"{m.name}_x_b2_in")
    rows_b1 = E * FB
    ROUND = 2 * DEEP

    def experts_from(engine, c):
        count = min(DEEP, n - c) if isinstance(c, int) else DEEP
        return nc.values_load_multi_w_load_instructions(
            k.slot_expert[0:1, bass.ds(c, count)], engines=[engine], min_val=0, max_val=E - 1)[1]
    with ExitStack() as scope:
        def sb(n, shape, dt=F32):
            return scope.enter_context(nc.sbuf_tensor(f"{m.name}_x_{n}", shape, dt))

        def bank(n, shape):
            return scope.enter_context(nc.psum_tensor(f"{m.name}_x_{n}", shape, F32))

        def b2_room(scope):
            if E <= TILES:
                return k.acc[:, :, :].rearrange("p t f -> p (t f)")[:, 0:E * D].rearrange("p (e f) -> p e f", e=E)
            return sb("b2b", [P, E, D])
        wa, wb, b2b = sb("wa", [P, W, KD, F]), sb("wb", [FP, E if all_w2 else W, FB, D]), b2_room(scope)
        xin, xt, h, yo = sb("xin", [P, ROUND, D]), sb("xt", [P, 2, D]), sb("h", [FP, 2, FB, P]), sb("yo", [P, DEEP, D])
        b1_given, b1t = sb("b1_given", [rows_b1, FP]), sb("b1t", [FP, rows_b1])
        turn_psum, h_psum, y_psum = bank("tp", [P, 2, 512]), bank("hp", [FP, 2, 512]), bank("yp", [P, 2, 512])
        b1_psum = bank("b1p", [FP, rows_b1])
        with nc.Block() as block:
            meanwhile(block)

            @block.sync
            def _(sp):
                sp.dma_start(b1_given[:], b1.rearrange("e (b f) -> (e b) f", f=FP)).then_inc(s["b1_in"], 16)
                experts = []

                def step(c, u, i, first):
                    if u % DEEP == 0:
                        count = min(DEEP, n - c) if isinstance(c, int) else DEEP
                        if not first:
                            sp.wait_ge(s["turned"], c - DEEP)
                        sp.dma_start(xin[:, u:u + count, :],
                                     slots[bass.ds(c * P, count * P), :].rearrange("(t p) f -> p t f", p=P))\
                            .then_inc(rows_in[u // DEEP], 16)
                        experts[:] = experts_from(mybir.EngineType.SP, c)
                    e, v = experts[u % DEEP], u % W
                    if not first or u >= W:
                        sp.wait_ge(s["down"], c - W + 1)
                    sp.dma_start(wa[:, v, :, :], w1[bass.ds(e, 1), :, :].rearrange("e (b p) f -> p (e b) f", p=P))\
                        .then_inc(loaded[v], 16)
                    if not all_w2:
                        sp.dma_start(wb[:, v, :, :],
                                     w2[bass.ds(e, 1), :, :].rearrange("e (b p) f -> p (e b) f", p=FP))\
                            .then_inc(loaded[v], 16)
                    if first and u == 0:
                        if all_w2:
                            sp.dma_start(wb[:, :, :, :].rearrange("p e b f -> p (e b) f"),
                                         w2.rearrange("e (b p) f -> p (e b) f", p=FP)).then_inc(w2_in, 16)
                        sp.dma_start(b2b[:], b2.partition_broadcast(P)).then_inc(b2_in, 16)
                over(sp, n, ROUND, step)

            @block.tensor
            def _(pe):
                pe.wait_ge(s["b1_in"], 16)
                nc.tensor.transpose(b1_psum[:], b1_given[:], k.ident[0:rows_b1, 0:rows_b1]).then_inc(s["b1_turned"], 1)

                def turn(c, u, i, early):
                    if u % DEEP == 0:
                        pe.wait_ge(rows_in[u // DEEP], (i + 1) * 16)
                    if not early:
                        pe.wait_ge(s["turned_sb"], c - 1)
                    for b in range(KD):
                        mm = nc.tensor.transpose(turn_psum[:, u % 2, b * P:(b + 1) * P],
                                                 xin[:, u, b * P:(b + 1) * P], k.ident[:])
                    mm.then_inc(s["turned"], 1)

                def down(c, u, early, e):
                    pe.wait_ge(s["hidden"], c + 1)
                    if not early:
                        pe.wait_ge(s["out"], c - 1)
                    for f in range(FB):
                        w = wb[:, bass.ds(e, 1), f, :].rearrange("p e f -> p (e f)") if all_w2 else wb[:, u % W, f, :]
                        mm = nc.tensor.matmul(y_psum[:, u % 2, 0:D], h[:, u % 2, f, :], w,
                                              start=(f == 0), stop=(f == FB - 1))
                    mm.then_inc(s["down"], 1)

                def step(c, u, i, first):
                    if not (isinstance(c, int) and c == n - 1):
                        turn(c + 1, (u + 1) % ROUND, i + (u + 1) // ROUND, first and u == 0)
                    pe.wait_ge(s["turned_sb"], c + 1)
                    pe.wait_ge(loaded[u % W], (i * (ROUND // W) + u // W + 1) * per_tile)
                    if not first or u >= 2:
                        pe.wait_ge(s["hidden"], c - 1)
                    for f in range(FB):
                        for b in range(KD):
                            mm = nc.tensor.matmul(h_psum[:, u % 2, f * P:(f + 1) * P],
                                                  wa[:, u % W, b, f * FP:(f + 1) * FP],
                                                  xt[:, u % 2, b * P:(b + 1) * P], start=(b == 0), stop=(b == KD - 1))
                    mm.then_inc(s["up"], 1)
                    if all_w2 and u % DEEP == 0:
                        start = first and u == 0
                        experts[:] = [None] * start + list(experts_from(mybir.EngineType.PE, c if start else c - 1))
                    if all_w2 and first and u == 1:
                        pe.wait_ge(w2_in, 16)
                    if not first or u >= 1:
                        down(c - 1, (u - 1) % ROUND, first and u <= 2, experts[u % DEEP] if all_w2 else None)
                experts = []
                turn(0, 0, 0, True)
                over(pe, n, ROUND, step, last_apart=True)
                down(n - 1, (n - 1) % ROUND, False, experts_from(mybir.EngineType.PE, n - 1)[0] if all_w2 else None)

            @block.scalar
            def _(act):
                act.wait_ge(s["b1"], 1)
                experts = []

                def store(c, u, count):
                    act.wait_ge(s["out"], c + count)
                    act.dma_start(results[bass.ds(c * P, count * P), :].rearrange("(t p) f -> p t f", p=P),
                                  yo[:, u:u + count, :]).then_inc(stored[u // 2], 16)

                def step(c, u, i, first):
                    if u % DEEP == 0:
                        experts[:] = experts_from(mybir.EngineType.Activation, c)
                    e = experts[u % DEEP]
                    act.wait_ge(s["up"], c + 1)
                    if not first or u >= 2:
                        act.wait_ge(s["down"], c - 1)
                    for f in range(FB):
                        ins = nc.scalar.activation(h[:, u % 2, f, :], h_psum[:, u % 2, f * P:(f + 1) * P], func,
                                                   bias=b1t[:, bass.ds(e * FB + f, 1)])
                    ins.then_inc(s["hidden"], 1)
                    if u % 2 and (not first or u > 2):
                        store(c - 3, (u - 3) % DEEP, 2)
                over(act, n, ROUND, step)
                for c in range(n - 2 - n % 2, n, 2):
                    store(c, c % DEEP, min(2, n - c))
                for u in range(2):
                    act.wait_ge(stored[u], 16 * len(range(2 * u, n, DEEP)))

            @block.vector
            def _(dve):
                dve.wait_ge(s["b1_turned"], 1)
                nc.vector.tensor_copy(b1t[:], b1_psum[:]).then_inc(s["b1"], 1)

                def copy(c, u, early):
                    dve.wait_ge(s["turned"], c + 1)
                    if not early:
                        dve.wait_ge(s["up"], c - 1)
                    nc.vector.tensor_copy(xt[:, u % 2, :], turn_psum[:, u % 2, 0:D]).then_inc(s["turned_sb"], 1)

                def finish(c, u, i, e):
                    dve.wait_ge(s["down"], c + 1)
                    if not isinstance(c, int) or c >= DEEP:
                        dve.wait_ge(stored[u % DEEP // 2], (2 * i + u // DEEP) * 16)
                    to = yo[:, u % DEEP, :]
                    ins = nc.vector.tensor_tensor(to, y_psum[:, u % 2, 0:D],
                                                  b2b[:, bass.ds(e, 1), :].rearrange("p e f -> p (e f)"), ALU.add)
                    if relu_out:
                        ins.then_inc(s["sum"], 1)
                        dve.wait_ge(s["sum"], c + 1)
                        ins = nc.vector.tensor_scalar(to, to, 0.0, None, ALU.max)
                    ins.then_inc(s["out"], 1)

                def step(c, u, i, first):
                    if not (isinstance(c, int) and c == n - 1):
                        copy(c + 1, u + 1, first and u == 0)
                    if u % DEEP == 0:
                        start = first and u == 0
                        experts[:] = [None] * start + list(experts_from(mybir.EngineType.DVE, c if start else c - 1))
                    if not first or u >= 1:
                        finish(c - 1, (u - 1) % ROUND, i if u else i - 1, experts[u % DEEP])
                experts = []
                copy(0, 0, True)
                dve.wait_ge(b2_in, 16)
                over(dve, n, ROUND, step, last_apart=True)
                finish(n - 1, (n - 1) % ROUND, (n - 1) // ROUND, experts_from(mybir.EngineType.DVE, n - 1)[0])


def combine(nc, k, m, results, into, weighted):
    added = k.sem(m.name + "_c_added")
    gathered = [k.sem(f"{m.name}_c_gathered{u}") for u in range(GROUP)]
    with nc.sbuf_tensor(m.name + "_c_rows", [P, GROUP, D], F32) as rows, nc.Block() as block:
        @block.gpsimd
        def _(pool):
            for j in range(m.items):
                if j >= GROUP:
                    pool.wait_ge(added, j - GROUP + 1)
                nc.gpsimd.indirect_dma_start(rows[:, j % GROUP, :], None, results[0:m.tiles * P, :],
                                             bass.IndirectOffsetOnAxis(ap=k.slot_i[:, j:j + 1], axis=0))\
                    .then_inc(gathered[j % GROUP], 16)

        @block.vector
        def _(dve):
            for j in range(m.items):
                dve.wait_ge(gathered[j % GROUP], (j // GROUP + 1) * 16)
                if j:
                    dve.wait_ge(added, j)
                to = into[:, j // m.K, :]
                if weighted:
                    ins = nc.vector.scalar_tensor_tensor(to, rows[:, j % GROUP, :], k.choice[:, j:j + 1], to,
                                                         ALU.mult, ALU.add)
                else:
                    ins = nc.vector.tensor_tensor(to, to, rows[:, j % GROUP, :], ALU.add)
                ins.then_inc(added, 1)
                if j % m.K == m.K - 1:
                    dve.wait_ge(added, j + 1)
                    nc.vector.bn_stats(k.stats[:, j // m.K, :], to)


def add_y(nc, k, block):
    done = k.sem("added_y")

    @block.gpsimd
    def _(pool):
        nc.gpsimd.tensor_tensor(k.x[:], k.x[:], k.y[:], ALU.add).then_inc(done, 1)
        pool.wait_ge(done, 1)



def pooled_ffn(nc, k, meanwhile, router, router_bias, w1, b1, w2, b2):
    E, _, F = w1.shape
    FB, K = F // P, 2
    capacity = float(-(-N * 5 // (4 * E)))
    sem = k.sem
    s = {n: sem("pool_" + n) for n in ("in", "stats", "link", "prepared", "turned", "turned_sb", "mean",
                                       "scored", "chosen", "exp_asked", "exp_done", "wide", "w1_in", "w2_in", "b1_chosen", "scaled",
                                       "b1_turned", "up", "hidden", "down", "out", "sum")}
    kept = [sem(f"pool_kept{u}") for u in range(2)]
    with ExitStack() as scope:
        def sb(n, shape, dt=F32):
            return scope.enter_context(nc.sbuf_tensor("pool_" + n, shape, dt))

        def bank(n, shape):
            return scope.enter_context(nc.psum_tensor("pool_" + n, shape, F32))
        ybuf, rt, rb = sb("ybuf", [P, 2, D]), sb("rt", [P, KD, E]), sb("rb", [1, E])
        yt = k.acc[:, :, :].rearrange("p t f -> p (t f)")[:, 0:KD * TILES * P].rearrange("p (b n) -> p b n", b=KD)
        mean, lg, t = sb("mean", [P, KD]), sb("lg", [1, 8]), sb("t", [1, 8])
        best, which, cw = sb("best", [1, 8]), sb("which", [1, 8], U32), sb("cw", [1, K])
        cwb = sb("cwb", [P, K])
        wa, wb, b2b = sb("wa", [P, K, KD, F]), sb("wb", [P, K, FB, D]), sb("b2b", [P, K, D])
        b1_given, b1t, b1s = sb("b1_given", [E * FB, P]), sb("b1t", [P, E * FB]), sb("b1s", [P, K, FB])
        h = sb("h", [P, 2, K * FB, P])
        turn_psum = bank("tp", [P, 2, 512])
        small_psum = bank("sp", [P, 512])
        h_psum, y_psum = bank("hp", [P, K, 512]), bank("yp", [P, 2, 512])
        with nc.Block() as block:
            @block.sync
            def _(sp):
                sp.dma_start(rt[:], rows_of(router, KD)).then_inc(s["in"], 16)
                sp.dma_start(rb[:], router_bias.rearrange("(a e) -> a e", a=1)).then_inc(s["in"], 16)
                sp.dma_start(b1_given[:], b1.rearrange("e (b f) -> (e b) f", f=P)).then_inc(s["in"], 16)
                sp.wait_ge(s["chosen"], 1)
                experts = [sp.value_load(which[0:1, j:j + 1], min_val=0, max_val=E - 1) for j in range(K)]
                for j, e in enumerate(experts):
                    sp.dma_start(wa[:, j, :, :], w1[bass.ds(e, 1), :, :].rearrange("e (b p) f -> p (e b) f", p=P))\
                        .then_inc(s["w1_in"], 16)
                for j, e in enumerate(experts):
                    sp.dma_start(wb[:, j, :, :], w2[bass.ds(e, 1), :, :].rearrange("e (b p) f -> p (e b) f", p=P))\
                        .then_inc(s["w2_in"], 16)
                    sp.dma_start(b2b[:, j, :], b2[bass.ds(e, 1), :].rearrange("e f -> (e f)").partition_broadcast(P))\
                        .then_inc(s["w2_in"], 16)

            @block.scalar
            def _(act):
                serve_root(nc, k, act)
                act.wait_ge(s["stats"], 1)

                def step(c, u, i, first):
                    if not first:
                        act.wait_ge(s["turned"], c - 1)
                        act.wait_ge(kept[u], i)
                    nc.scalar.activation(ybuf[:, u, :], k.x[:, bass.ds(c, 1), :].rearrange("p a f -> p (a f)"),
                                         ACT.Identity, bias=one(k.ln_shift, c), scale=one(k.ln_scale, c))\
                        .then_inc(s["prepared"], 1)
                over(act, TILES, 2, step)
                for n in range(3):
                    act.wait_ge(s["exp_asked"], n + 1)
                    nc.scalar.activation(t[:], t[:], ACT.Exp).then_inc(s["exp_done"], 1)

                def gelu(c, u, i, first):
                    if not first:
                        act.wait_ge(s["down"], c - 1)
                    for j in range(K):
                        act.wait_ge(s["up"], c * K + j + 1)
                        for f in range(FB):
                            ins = nc.scalar.activation(h[:, u, j * FB + f, :], h_psum[:, j, f * P:(f + 1) * P],
                                                       ACT.Gelu, bias=b1s[:, j, f:f + 1])
                        ins.then_inc(s["hidden"], 1)
                act.wait_ge(s["b1_chosen"], 1)
                over(act, TILES, 2, gelu)

            @block.gpsimd
            def _(pool):
                keep_even(nc, k, pool, ybuf, s["prepared"], kept[0])

            meanwhile(block)

            @block.tensor
            def _(pe):
                pe.wait_ge(s["in"], 48)
                nc.tensor.transpose(small_psum[:, 0:E * FB], b1_given[:], k.ident[0:E * FB, 0:E * FB])\
                    .then_inc(s["b1_turned"], 1)

                def step(c, u, i, first):
                    pe.wait_ge(s["prepared"], c + 1)
                    if not first:
                        pe.wait_ge(s["turned_sb"], c - 1)
                    for b in range(KD):
                        mm = nc.tensor.transpose(turn_psum[:, u, b * P:(b + 1) * P], ybuf[:, u, b * P:(b + 1) * P],
                                                 k.ident[:])
                    mm.then_inc(s["turned"], 1)
                over(pe, TILES, 2, step)
                pe.wait_ge(s["mean"], 1)
                for b in range(KD):
                    mm = nc.tensor.matmul(y_psum[0:1, 0, 0:E], mean[:, b:b + 1], rt[:, b, :],
                                          start=(b == 0), stop=(b == KD - 1))
                mm.then_inc(s["scored"], 1)
                pe.wait_ge(s["chosen"], 2)
                nc.tensor.matmul(y_psum[:, 1, 0:K], k.ones[0:1, :], cw[:], start=True, stop=True)\
                    .then_inc(s["wide"], 1)
                pe.wait_ge(s["w1_in"], 16 * K)

                def down(c, u, early):
                    if early:
                        pe.wait_ge(s["scaled"], 1)
                    pe.wait_ge(s["hidden"], c * K + K)
                    if not early:
                        pe.wait_ge(s["out"], c)
                    for j in range(K * FB):
                        mm = nc.tensor.matmul(y_psum[:, u, 0:D], h[:, u, j, :], wb[:, j // FB, j % FB, :],
                                              start=(j == 0), stop=(j == K * FB - 1))
                    mm.then_inc(s["down"], 1)

                def work(c, u, i, first):
                    for j in range(K):
                        if not (first and u == 0):
                            pe.wait_ge(s["hidden"], c * K + j - 1)
                        for f in range(FB):
                            for b in range(KD):
                                mm = nc.tensor.matmul(h_psum[:, j, f * P:(f + 1) * P], wa[:, j, b, f * P:(f + 1) * P],
                                                      yt[:, b, bass.ds(c * P, P)], start=(b == 0), stop=(b == KD - 1))
                        mm.then_inc(s["up"], 1)
                    if not first or u:
                        down(c - 1, 1 - u, first)
                over(pe, TILES, 2, work)
                down(TILES - 1, (TILES - 1) % 2, False)

            @block.vector
            def _(dve):
                link = Chain(dve, s["link"])
                dve.wait_ge(s["b1_turned"], 1)
                link(nc.vector.tensor_copy(b1t[:], small_psum[:, 0:E * FB]))
                ln_stats(nc, k, dve, link, k.x, done=s["stats"])

                def step(c, u, i, first):
                    dve.wait_ge(s["turned"], c + 1)
                    nc.vector.tensor_scalar(yt[:, :, bass.ds(c * P, P)],
                                            turn_psum[:, u, 0:D].rearrange("p (b n) -> p b n", b=KD), 1.0, None, ALU.mult)\
                        .then_inc(s["turned_sb"], 1)
                    if u:
                        keep_odd(nc, k, dve, c, ybuf, s["prepared"], kept[1])
                over(dve, TILES, 2, step)
                dve.wait_ge(s["turned_sb"], TILES)
                link(nc.vector.tensor_reduce(mean[:], yt[:, :, 0:N], AX_X, ALU.add))
                nc.vector.tensor_scalar(mean[:], mean[:], 1.0 / N, None, ALU.mult).then_inc(s["mean"], 1)
                dve.wait_ge(s["scored"], 1)
                link(nc.vector.tensor_tensor(lg[:], y_psum[0:1, 0, 0:E], rb[:], ALU.add))

                def softmax(n):
                    link(nc.vector.tensor_reduce(best[:, 0:1], lg[:], AX_X, ALU.max))
                    nc.vector.tensor_scalar(t[:], lg[:], best[:, 0:1], None, ALU.subtract).then_inc(s["exp_asked"], 1)
                    dve.wait_ge(s["exp_done"], n)
                    link(nc.vector.tensor_reduce(best[:, 0:1], t[:], AX_X, ALU.add))
                    link(nc.vector.reciprocal(best[:, 0:1], best[:, 0:1]))
                    link(nc.vector.tensor_scalar(lg[:], t[:], best[:, 0:1], None, ALU.mult))
                softmax(1)
                link(nc.vector.tensor_scalar(t[:], lg[:], float(N), None, ALU.mult))
                link(nc.vector.reciprocal(t[:], t[:]))
                link(nc.vector.tensor_scalar(t[:], t[:], capacity, 1.0, ALU.mult, ALU.min))
                link(nc.vector.tensor_tensor(lg[:], lg[:], t[:], ALU.mult))
                softmax(2)
                link(nc.vector.max(best[:], lg[:]))
                nc.vector.max_index(which[:], best[:], lg[:]).then_inc(s["chosen"], 1)
                nc.vector.tensor_scalar(t[:], best[:], best[:, 0:1], None, ALU.subtract).then_inc(s["exp_asked"], 1)
                dve.wait_ge(s["exp_done"], 3)
                link(nc.vector.tensor_reduce(lg[:, 0:1], t[:, 0:K], AX_X, ALU.add))
                link(nc.vector.reciprocal(lg[:, 0:1], lg[:, 0:1]))
                nc.vector.tensor_scalar(cw[:], t[:, 0:K], lg[:, 0:1], None, ALU.mult).then_inc(s["chosen"], 1)
                dve.wait_ge(s["wide"], 1)
                link(nc.vector.tensor_copy(cwb[:], y_psum[:, 1, 0:K]))
                for j in range(K):
                    e = dve.value_load(which[0:1, j:j + 1], min_val=0, max_val=E - 1)
                    ins = nc.vector.tensor_copy(b1s[:, j, :], b1t[:, bass.ds(e * FB, FB)])
                ins.then_inc(s["b1_chosen"], 1)
                dve.wait_ge(s["w2_in"], 32 * K)
                for j in range(K):
                    link(nc.vector.tensor_scalar(wb[:, j, :, :], wb[:, j, :, :], cwb[:, j:j + 1], None, ALU.mult))
                    link(nc.vector.tensor_scalar(b2b[:, j, :], b2b[:, j, :], cwb[:, j:j + 1], None, ALU.mult))
                nc.vector.tensor_tensor(b2b[:, 0, :], b2b[:, 0, :], b2b[:, 1, :], ALU.add).then_inc(s["scaled"], 1)

                def out(c, u, i, first):
                    dve.wait_ge(s["down"], c + 1)
                    to = k.y[:, bass.ds(c, 1), :].rearrange("p a f -> p (a f)")
                    nc.vector.tensor_tensor(to, to, y_psum[:, u, 0:D], ALU.add).then_inc(s["out"], 1)
                    dve.wait_ge(s["out"], c + 1)
                    nc.vector.tensor_tensor(to, to, b2b[:, 0, :], ALU.add)
                dve.wait_ge(kept[0], TILES - TILES // 2)
                dve.wait_ge(kept[1], TILES // 2)
                over(dve, TILES, 2, out)



def rows_of(w, blocks):
    return w.rearrange("(b p) n -> p b n", p=P)


def spread(v):
    return v.partition_broadcast(P)


def build(nc, a, out):
    k = Shared()
    k.made = 0

    def numbered(name):
        k.made += 1
        k.used.append(nc.alloc_semaphore(f"{name}_{k.made}"))
        return k.used[-1]
    k.sem, k.used = numbered, []

    def reuse_semaphores():
        nc.clear_and_free_semaphores(k.used)
        nc.all_engine_barrier()
        k.used = []
    ctx = ExitStack()

    def held(scope, name, shape, dt=F32):
        k.made += 1
        t = scope.enter_context(nc.sbuf_tensor(f"{name}_{k.made}", shape, dt))
        return t

    def bank(scope, name, shape):
        k.made += 1
        t = scope.enter_context(nc.psum_tensor(f"{name}_{k.made}", shape, F32))
        return t

    def dram(name, shape, dt=F32):
        return nc.dram_tensor(name, shape, dt).ap()

    k.by_dst = dram("by_dst", (P * SLOTS, 4))
    k.by_src = dram("by_src", (P * SLOTS, 4))
    table = dram("table", (TILES * P, D))

    with ctx:
        k.ident = held(ctx, "ident", [P, P])
        k.before = held(ctx, "before", [P, P])
        k.ones = held(ctx, "ones", [P, P])
        k.count_i = held(ctx, "count_i", [P, CHUNKS], I32)
        k.count = held(ctx, "count", [P, CHUNKS])
        k.x = held(ctx, "x", [P, TILES, D])
        k.y = held(ctx, "y", [P, TILES, D])
        k.acc = held(ctx, "acc", [P, NB, D + 1])
        k.pos_dst = held(ctx, "pos_dst", [P, L], I32)
        k.pos_src = held(ctx, "pos_src", [P, L], I32)
        k.edge_dst = held(ctx, "edge_dst", [P, L, 4])
        k.edge_src = held(ctx, "edge_src", [P, L, 4])
        k.rec_dst = held(ctx, "rec_dst", [P, SLOTS, 4])
        k.ids_dst = held(ctx, "ids_dst", [1, CHUNKS], I32)
        k.ids_src = held(ctx, "ids_src", [1, CHUNKS], I32)
        k.index = held(ctx, "index", [P, PARTS, GROUP], I32)
        k.one_col = held(ctx, "one_col", [P, 1], BF16)
        k.records = held(ctx, "records", [P, 2, GROUP, 4])
        k.stats = held(ctx, "stats", [P, TILES, 6])
        k.ln_work = held(ctx, "ln_work", [P, 6, TILES])
        k.ln_scale = held(ctx, "ln_scale", [P, TILES])
        k.ln_shift = held(ctx, "ln_shift", [P, TILES])
        k.root_in = held(ctx, "root_in", [P, TILES])
        k.root_out = held(ctx, "root_out", [P, TILES])
        k.choice = held(ctx, "choice", [P, 2 * TILES])
        k.slot_i = held(ctx, "slot_i", [P, 2 * TILES], I32)
        k.slot_expert = held(ctx, "slot_expert", [1, SLOT_TILES], I32)
        k.gru0 = held(ctx, "gru0", [P, KD, D])
        k.gru1 = held(ctx, "gru1", [P, KD, D])
        k.dinv_loop = held(ctx, "dinv_loop", [P, TILES])
        k.dinv = held(ctx, "dinv", [P, TILES])
        k.degree = held(ctx, "degree", [P, TILES])
        k.root_asked, k.root_done = nc.alloc_semaphore("root_asked"), nc.alloc_semaphore("root_done")
        k.roots = k.served = 0

        def gnn_buffers(scope):
            k.ybuf = held(scope, "ybuf", [P, 2, D])
            k.yt = held(scope, "yt", [P, 2, D])
            k.w_a = held(scope, "w_a", [P, KD, D])
            k.turn_psum = bank(scope, "turn_psum", [P, 2, 512])
            k.out_psum = bank(scope, "out_psum", [P, 2, 512])

        def sum_buffers(scope):
            k.rows = held(scope, "rows", [P, RING, D])
            k.hot = held(scope, "hot", [P, RING, P])
            k.away = held(scope, "away", [P, 2, P])
            k.hot1 = held(scope, "hot1", [P, RING, P], BF16)
            k.sum_psum = bank(scope, "sum_psum", [P, BANKS, 512])

        slots = dram("slots", (SLOT_TILES * P, D))
        results = dram("results", (SLOT_TILES * P, D))

        with ExitStack() as scope:
            k.dst = held(scope, "dst", [P, L], I32)
            k.src = held(scope, "src", [P, L], I32)
            k.w = held(scope, "w", [P, L])
            k.key_i = held(scope, "key_i", [P, L], I32)
            k.key = held(scope, "key", [P, L])
            k.bucket = held(scope, "bucket", [P, L], BF16)
            k.pos = held(scope, "pos", [P, L])
            k.member = k.y[:, :, :].rearrange("p t f -> p (t f)").bitcast(BF16)
            k.running = held(scope, "running", [P, max(NB * L, TILES * CHUNKS)])
            k.small = held(scope, "small", [P, 5, 32])
            k.small_i = held(scope, "small_i", [P, 32], I32)
            k.id_f = held(scope, "id_f", [1, CHUNKS])
            k.sort_psum = bank(scope, "sort_psum", [P, 2, 64])
            k.pos_psum = bank(scope, "pos_psum", [P, 512])
            with nc.Block() as block:
                constants(nc, k, block)
                load_edges(nc, k, block, a)
            with nc.Block() as block:
                placed = sort_edges(nc, k, block, k.dst, k.src, k.w, k.edge_dst, k.pos_dst, k.ids_dst, "dst",
                                    lambda dve: dve.wait_ge(k.edges_in, 96))
                load_x(nc, k, block, a["x"], slots)
                scatter_edges(nc, k, block, "dst0", k.pos_dst, k.edge_dst, k.by_dst, 0, FIRST_GROUPS, placed)
            with nc.Block() as block:
                scatter_edges(nc, k, block, "dst1", k.pos_dst, k.edge_dst, k.by_dst, FIRST_GROUPS, SECOND_GROUPS)
                sort_edges(nc, k, block, k.src, k.dst, k.w, k.edge_src, k.pos_src, k.ids_src, "src",
                           lambda dve: dve.wait_ge(k.edges_in, 96))

        def projected(name, weight=None, weight_in=None, meanwhile=lambda block, scope: None,
                      before=lambda block: None, **more):
            with ExitStack() as scope:
                gnn_buffers(scope)
                loads = list(more.pop("loads", ()))
                if weight_in is not None:
                    loads.append((k.w_a[:], rows_of(weight_in, KD)))
                    weight = k.w_a
                with nc.Block() as block:
                    before(block)
                    project(nc, k, block, name, weight, table, loads=loads, **more)
                    meanwhile(block, scope)

        src_groups = [0]

        def some_src(name, groups):
            start = src_groups[0]
            src_groups[0] += groups
            return lambda block, scope=None: scatter_edges(nc, k, block, name, k.pos_src, k.edge_src, k.by_src,
                                                           start, groups)

        def summed(name, ids, weighted, degree):
            with ExitStack() as scope:
                sum_buffers(scope)
                with nc.Block() as block:
                    spmm(nc, k, block, name, table, k.rec_dst, ids, weighted, degree)

        def routed(m, func, router, by_expert, bias, mode, w1, b1, w2, b2, relu_out,
                   meanwhile=lambda block: None):
            route(nc, k, m, router, by_expert, bias, mode, slots)
            run_experts(nc, k, m, func, w1, b1, w2, b2, relu_out, slots, results, meanwhile)

        def weights_and_edges(block, scope):
            gru(nc, k, block, scope,
                [(f"gru{n}", *(a[f"L1_gnn_{v}{n}"] for v in ("iw", "wih", "whh", "bih", "bhh")), w[:])
                 for n, w in enumerate((k.gru0, k.gru1))])
            scatter_edges(nc, k, block, "dst2", k.pos_dst, k.edge_dst, k.by_dst, FIRST_GROUPS + SECOND_GROUPS,
                          L // GROUP - FIRST_GROUPS - SECOND_GROUPS)
        projected("l0a", weight_in=a["L0_gnn_W1"], norm_src=k.x, unit=True, meanwhile=weights_and_edges)
        with nc.Block() as block:
            load_records(nc, k, block, k.by_dst, k.rec_dst, "dst")
        summed("l0a", k.ids_dst, True, True)
        degrees(nc, k)
        relu_bias(nc, k, "l0r", a["L0_gnn_b1"])
        projected("l0b", weight_in=a["L0_gnn_W2"], plain_src=k.y, meanwhile=some_src("src0", 3))
        summed("l0b", k.ids_dst, True, False)
        add_elu(nc, k, "l0e", a["L0_gnn_b2"])
        reuse_semaphores()
        m = Experts("m0", 8, 2, 256)
        rest = some_src("src1", 9)
        routed(m, ACT.Gelu, a["L0_ffn_router_w"], True, None, "softmax_all",
               a["L0_ffn_w1"], a["L0_ffn_b1"], a["L0_ffn_w2"], a["L0_ffn_b2"], False,
               lambda block: (add_y(nc, k, block), rest(block)))
        combine(nc, k, m, results, k.x, True)
        reuse_semaphores()
        projected("l1a", weight=k.gru0, norm_src=k.x, row_scale=k.dinv_loop, self_loop=True, counted=True,
                  before=some_src("src2", 2))
        summed("l1a", k.ids_dst, False, False)
        add_acc(nc, k, "l1a", k.dinv_loop, False)
        with nc.sbuf_tensor("l1_affine", [P, 2, KD], F32) as affine:
            projected("l1b", weight=k.gru1, norm_src=k.y, affine=(affine[:, 0, :], affine[:, 1, :]),
                      row_scale=k.dinv_loop, self_loop=True, before=some_src("src3", 2),
                      loads=[(affine[:, j, b:b + 1], a[v][b * P:(b + 1) * P].rearrange("(p a) -> p a", a=1))
                             for j, v in enumerate(("L1_gnn_ln_g0", "L1_gnn_ln_b0")) for b in range(KD)])
        summed("l1b", k.ids_dst, False, False)
        add_acc(nc, k, "l1b", k.dinv_loop, True)
        reuse_semaphores()
        m = Experts("m1", 32, 1, 64)
        rest = some_src("src4", 8)
        routed(m, ACT.Relu, a["L1_ffn_router_w"], True, a["L1_ffn_router_b"], "none",
               a["L1_ffn_W1"], a["L1_ffn_b1"], a["L1_ffn_W2"], a["L1_ffn_b2"], True,
               rest)
        combine(nc, k, m, results, k.x, False)
        reuse_semaphores()
        projected("l2", weight_in=a["L2_gnn_W"], norm_src=k.x, row_scale=k.dinv, counted=True,
                  before=some_src("src5", 3))
        summed("l2", k.ids_dst, False, False)
        add_acc(nc, k, "l2", k.dinv, True)
        reuse_semaphores()
        pooled_ffn(nc, k, some_src("src6", L // GROUP - src_groups[0]), a["L2_ffn_Wr"], a["L2_ffn_br"],
                   a["L2_ffn_W1"], a["L2_ffn_b1"], a["L2_ffn_W2"], a["L2_ffn_b2"])
        add_norm(nc, k, "l2n", a["L2_ffn_gamma"], a["L2_ffn_beta"])
        reuse_semaphores()
        with nc.sbuf_tensor("l3_wr", [P, KD, D], F32) as wr, nc.sbuf_tensor("l3_b", [P, 2, D], F32) as b, \
                nc.psum_tensor("l3_psum", [P, 2, 512], F32) as k.out2_psum:
            projected("l3", weight_in=a["L3_gnn_weight_l"], norm_src=k.x, second=(wr, b[:, 0, :], b[:, 1, :]),
                      meanwhile=lambda block, scope: load_records(nc, k, block, k.by_src, k.rec_dst, "src"),
                      loads=[(wr[:], rows_of(a["L3_gnn_weight_r"], KD)), (b[:, 0, :], spread(a["L3_gnn_bias_l"])),
                             (b[:, 1, :], spread(a["L3_gnn_bias_r"]))])
        summed("l3", k.ids_src, True, False)
        add_acc(nc, k, "l3", None, True)
        reuse_semaphores()
        m = Experts("m3", 16, 2, 512)
        routed(m, ACT.Relu, a["L3_ffn_gate_w"], False, a["L3_ffn_gate_b"], "softmax_top",
               a["L3_ffn_w1"], a["L3_ffn_b1"], a["L3_ffn_w2"], a["L3_ffn_b2"], False)
        combine(nc, k, m, results, k.y, True)
        add_norm(nc, k, "l3n", a["L3_ffn_gamma"], a["L3_ffn_beta"], counted=True, out=out)


def kernel(**inputs):
    import numpy as _np
    import concourse.bacc as _bacc
    from concourse import mybir as _mybir
    from concourse.bass_utils import run_bass_kernel_spmd as _run

    nc = _bacc.Bacc("TRN2", target_bir_lowering=False, num_devices=1)
    arrays, given = {}, {}
    for name, value in inputs.items():
        v = _np.ascontiguousarray(value)
        arrays[f"in_{name}_dram"] = v
        given[name] = nc.dram_tensor(f"in_{name}_dram", v.shape, _mybir.dt.from_np(v.dtype), kind="ExternalInput").ap()
    out = nc.dram_tensor("out_0_dram", (N, D), F32, kind="ExternalOutput").ap()
    build(nc, given, out)
    r = _run(nc, [arrays], core_ids=[0])
    return r.results[0]["out_0_dram"]
```
